# Optimizing a Trainium2 kernel written in Bass

```python
import numpy as np
import jax
import jax.numpy as jnp

def _softmax(x, axis=-1):
    return jax.nn.softmax(x, axis=axis)

def _gelu(x):
    return jax.nn.gelu(x, approximate=True)

def _silu(x):
    return jax.nn.silu(x)

def _sigmoid(x):
    return jax.nn.sigmoid(x)

def _layernorm(x, axis=-1, eps=1e-05):
    m = jnp.mean(x, axis=axis, keepdims=True)
    v = jnp.var(x, axis=axis, keepdims=True)
    return (x - m) / jnp.sqrt(v + eps)

def _scatter_add(tgt, idx, src, axis=0):
    return tgt.at[idx].add(src)

def _segment_sum(src, seg, n):
    return jax.ops.segment_sum(src, seg, n)
kernel_name = 'mk_decoder_postln_d2_seqx_r8_0abbe2'

def setup_inputs(seed: int=0):
    np.random.seed(seed)
    _w = jnp.asarray

    def _rec_inputs():
        import jax
        import jax.numpy as jnp
        _rk = jax.random.key(seed)
        x = -0.0002928 + 1 * jax.random.normal(jax.random.fold_in(_rk, 1), (64, 64, 128), jnp.float32)
        _lenS = 64 - jax.random.randint(jax.random.fold_in(_rk, 7), (64,), 0, max(1, 64 // 4) + 1, jnp.int32)
        _lenS2 = 64 - jax.random.randint(jax.random.fold_in(_rk, 8), (64,), 0, max(1, 64 // 4) + 1, jnp.int32)
        _ctx_1024P = jax.random.normal(jax.random.fold_in(_rk, 11), (64, 16, 128), jnp.float32)
        _ctx_1024c = jax.random.dirichlet(jax.random.fold_in(_rk, 511), 0.3 * jnp.ones((16,), jnp.float32), (64, 64))
        _ctx_1024t = jnp.einsum('bsk,bkd->bsd', _ctx_1024c, _ctx_1024P)
        _ctx_1024t = _ctx_1024t * jax.lax.rsqrt(jnp.mean(jnp.square(_ctx_1024t)) + 1e-12) * 0.953939
        ctx_1024 = -1.39393e-06 + 0.999914 * (_ctx_1024t + 0.3 * jax.random.normal(jax.random.fold_in(_rk, 611), (64, 64, 128), jnp.float32))
        _validS = jnp.arange(64)[None, :] < _lenS[:, None]
        _validS2 = jnp.arange(64)[None, :] < _lenS2[:, None]
        _causal = jnp.tril(jnp.ones((64, 64), dtype=bool))
        mask_BxS2_bk0 = jnp.logical_not(jnp.broadcast_to(_validS2[:, :], (64, 64)))
        return (x, ctx_1024, mask_BxS2_bk0)
    x, ctx_1024, mask_BxS2_bk0 = _rec_inputs()

    def _L0_attn_setup():
        import jax, jax.numpy as jnp
        import numpy as np
        import math
        DIM = 128
        K = 3
        NUM_LAYERS = 1
        RES_SCALE = 1.0 / math.sqrt(NUM_LAYERS)

        def rmsnorm(x, gamma):
            n = jnp.sqrt(jnp.sum(x * x, axis=-1, keepdims=True))
            return x / jnp.maximum(n, 1e-12) * x.shape[-1] ** 0.5 * (gamma + 1.0)

        def causal_dwconv(x, w_dw, b_dw, w_pw, b_pw):
            xt = jnp.transpose(x, (0, 2, 1))
            xt = jnp.pad(xt, ((0, 0), (0, 0), (K - 1, 0)))
            y = jax.lax.conv_general_dilated(xt, w_dw, window_strides=(1,), padding='VALID', feature_group_count=xt.shape[1], dimension_numbers=('NCH', 'OIH', 'NCH'))
            y = y + b_dw[None, :, None]
            y = jnp.transpose(y, (0, 2, 1))
            return jnp.einsum('bld,ed->ble', y, w_pw) + b_pw

        def log_g(x):
            return jnp.where(x >= 0, jnp.log(jax.nn.relu(x) + 0.5), -jax.nn.softplus(-x))

        def heinsen_scan_log(log_coeffs, log_values):
            a_star = jnp.cumsum(log_coeffs, axis=1)
            log_h = a_star + jax.lax.cumlogsumexp(log_values - a_star, axis=1)
            return jnp.exp(log_h)

        def min_gru(x, w_hg):
            hg = jnp.einsum('bld,ed->ble', x, w_hg)
            hidden, gate = jnp.split(hg, 2, axis=-1)
            log_coeffs = -jax.nn.softplus(gate)
            log_values = -jax.nn.softplus(-gate) + log_g(hidden)
            out = heinsen_scan_log(log_coeffs, log_values)
            next_hidden = out[:, -1:]
            return (out, next_hidden)

        def _reference_tuple_inner(x, conv_dw_w, conv_dw_b, conv_pw_w, conv_pw_b, conv_norm_g, gru_norm_g, gru_w, ff_norm_g, ff_w1, ff_b1, ff_w2, ff_b2):
            x = causal_dwconv(rmsnorm(x, conv_norm_g), conv_dw_w, conv_dw_b, conv_pw_w, conv_pw_b) * RES_SCALE + x
            gru_out, next_hidden = min_gru(rmsnorm(x, gru_norm_g), gru_w)
            x = gru_out * RES_SCALE + x
            h = rmsnorm(x, ff_norm_g)
            h = jax.nn.gelu(jnp.einsum('bld,ed->ble', h, ff_w1) + ff_b1, approximate=False)
            h = jnp.einsum('ble,de->bld', h, ff_w2) + ff_b2
            x = h * RES_SCALE + x
            return (x, next_hidden)
        key = jax.random.key(seed)
        ks = jax.random.split(key, 12)
        D = DIM
        s = 0.02
        return {'x': jax.random.normal(ks[0], (4, 512, D), jnp.float32), 'conv_dw_w': jax.random.normal(ks[1], (D, 1, K), jnp.float32) * s, 'conv_dw_b': jax.random.normal(ks[2], (D,), jnp.float32) * s, 'conv_pw_w': jax.random.normal(ks[3], (D, D), jnp.float32) * s, 'conv_pw_b': jax.random.normal(ks[4], (D,), jnp.float32) * s, 'conv_norm_g': jax.random.normal(ks[5], (D,), jnp.float32) * s, 'gru_norm_g': jax.random.normal(ks[6], (D,), jnp.float32) * s, 'gru_w': jax.random.normal(ks[7], (2 * D, D), jnp.float32) * s, 'ff_norm_g': jax.random.normal(ks[8], (D,), jnp.float32) * s, 'ff_w1': jax.random.normal(ks[9], (4 * D, D), jnp.float32) * s, 'ff_b1': jax.random.normal(ks[10], (4 * D,), jnp.float32) * s, 'ff_w2': jax.random.normal(ks[11], (D, 4 * D), jnp.float32) * s, 'ff_b2': jnp.zeros((D,), jnp.float32)}
    _L0_attn_all = _L0_attn_setup()
    _L0_attn_in = {k: v for k, v in _L0_attn_all.items() if k in ('conv_dw_w', 'conv_dw_b', 'conv_pw_w', 'conv_pw_b', 'conv_norm_g', 'gru_norm_g', 'gru_w', 'ff_norm_g', 'ff_w1', 'ff_b1', 'ff_w2', 'ff_b2')}
    del _L0_attn_all

    def _L0_xattn_setup():
        import jax, jax.numpy as jnp
        import numpy as np
        B, S, E, H = (2, 256, 128, 16)
        D = E // H
        key = jax.random.key(seed)
        ks = jax.random.split(key, 7)
        sc = 0.02
        return {'q': jax.random.normal(ks[0], (B, S, E), dtype=jnp.float32), 'k': jax.random.normal(ks[1], (B, S, E), dtype=jnp.float32), 'v': jax.random.normal(ks[2], (B, S, E), dtype=jnp.float32), 'Wq': jax.random.normal(ks[3], (E, E), dtype=jnp.float32) * sc, 'Wk': jax.random.normal(ks[4], (E, E), dtype=jnp.float32) * sc, 'Wv': jax.random.normal(ks[5], (E, E), dtype=jnp.float32) * sc, 'Wo': jax.random.normal(ks[6], (E, E), dtype=jnp.float32) * sc}
    _L0_xattn_all = _L0_xattn_setup()
    _L0_xattn_in = {k: v for k, v in _L0_xattn_all.items() if k in ('Wq', 'Wk', 'Wv', 'Wo')}
    del _L0_xattn_all

    def _L0_ffn_setup():
        import jax, jax.numpy as jnp
        import numpy as np
        EPS = 1e-12

        def rms_norm(t, gamma):
            n = jnp.maximum(jnp.linalg.norm(t, axis=-1, keepdims=True), EPS)
            scale = jnp.sqrt(jnp.asarray(t.shape[-1], t.dtype))
            return t / n * scale * gamma
        key = jax.random.key(seed)
        ks = jax.random.split(key, 4)
        b, s, d = (4, 512, 128)
        e, t = (8, 64)
        hidden = 4 * d
        return {'x': jax.random.normal(ks[0], (b, s, d), dtype=jnp.float32), 'gamma_x': jnp.ones((d,), dtype=jnp.float32), 'gamma_slot': jnp.ones((d,), dtype=jnp.float32), 'slot_embeds': jax.random.normal(ks[1], (e, t, d), dtype=jnp.float32), 'w1': jax.random.normal(ks[2], (d, hidden), dtype=jnp.float32) * (1.0 / np.sqrt(d)), 'w2': jax.random.normal(ks[3], (hidden, d), dtype=jnp.float32) * (1.0 / np.sqrt(hidden))}
    _L0_ffn_all = _L0_ffn_setup()
    _L0_ffn_in = {k: v for k, v in _L0_ffn_all.items() if k in ('gamma_x', 'gamma_slot', 'slot_embeds', 'w1', 'w2')}
    del _L0_ffn_all

    def _L1_attn_setup():
        import math
        import jax, jax.numpy as jnp
        import numpy as np
        B, T, H = (2, 256, 128)
        NH, WINDOW = (16, 32)
        HD = H // NH
        key = jax.random.key(seed)
        ks = jax.random.split(key, 4)
        x = jax.random.normal(ks[0], (B, T, H), dtype=jnp.float32)
        W_qkv = jax.random.normal(ks[1], (H, 3 * H), dtype=jnp.float32) * (1.0 / math.sqrt(H))
        b_qkv = jnp.zeros((3 * H,), dtype=jnp.float32)
        W_out = jax.random.normal(ks[2], (H, H), dtype=jnp.float32) * (1.0 / math.sqrt(H))
        b_out = jnp.zeros((H,), dtype=jnp.float32)
        return {'x': x, 'W_qkv': W_qkv, 'b_qkv': b_qkv, 'W_out': W_out, 'b_out': b_out}
    _L1_attn_all = _L1_attn_setup()
    _L1_attn_in = {k: v for k, v in _L1_attn_all.items() if k in ('W_qkv', 'b_qkv', 'W_out', 'b_out')}
    del _L1_attn_all

    def _L1_xattn_setup():
        import jax, jax.numpy as jnp
        import numpy as np
        DIM = 128
        DIM_LATENT = 128
        DIM_HEAD = 64
        INNER = max(DIM, DIM_LATENT)
        HEADS = INNER // DIM_HEAD
        SCALE = DIM_HEAD ** (-0.5)
        LN_EPS = 1e-05
        RMS_EPS = 1e-08

        def layernorm(x, g, b):
            mu = jnp.mean(x, axis=-1, keepdims=True)
            var = jnp.mean(jnp.square(x - mu), axis=-1, keepdims=True)
            return (x - mu) * jax.lax.rsqrt(var + LN_EPS) * g + b

        def rmsnorm(x, gamma):
            n = jnp.linalg.norm(x, axis=-1, keepdims=True) * x.shape[-1] ** (-0.5)
            return x / jnp.maximum(n, RMS_EPS) * gamma
        key = jax.random.key(seed)
        ks = jax.random.split(key, 8)
        b, n, nl = (8, 256, 64)
        x = jax.random.normal(ks[0], (b, n, DIM), dtype=jnp.float32)
        latents = jax.random.normal(ks[1], (b, nl, DIM_LATENT), dtype=jnp.float32)
        mask = jax.random.randint(ks[2], (b, n), 0, 2).astype(bool)
        init = lambda k, shape, fan_in: jax.random.normal(k, shape, jnp.float32) * fan_in ** (-0.5)
        return {'x': x, 'latents': latents, 'mask': mask, 'ln_x_g': jnp.ones((DIM,), jnp.float32), 'ln_x_b': jnp.zeros((DIM,), jnp.float32), 'ln_l_g': jnp.ones((DIM_LATENT,), jnp.float32), 'ln_l_b': jnp.zeros((DIM_LATENT,), jnp.float32), 'q_gamma': jnp.ones((DIM_HEAD,), jnp.float32), 'k_gamma': jnp.ones((DIM_HEAD,), jnp.float32), 'W_q': init(ks[3], (DIM_LATENT, INNER), DIM_LATENT), 'W_kv': init(ks[4], (DIM, 2 * INNER), DIM), 'W_out': init(ks[5], (INNER, DIM_LATENT), INNER), 'b_out': jnp.zeros((DIM_LATENT,), jnp.float32)}
    _L1_xattn_all = _L1_xattn_setup()
    _L1_xattn_in = {k: v for k, v in _L1_xattn_all.items() if k in ('ln_x_g', 'ln_x_b', 'ln_l_g', 'ln_l_b', 'q_gamma', 'k_gamma', 'W_q', 'W_kv', 'W_out', 'b_out')}
    del _L1_xattn_all

    def _L1_ffn_setup():
        import jax, jax.numpy as jnp
        import numpy as np
        D_MODEL = 128
        HIDDEN = 256
        E_ROUTED = 14
        E_SHARED = 2
        TOP_K = 2
        EPS = 1e-09
        RMS_EPS = 1.1920929e-07

        def _ffn(xn, rw, W1, W2):
            ms = jnp.mean(xn * xn, axis=-1, keepdims=True)
            h = xn * jax.lax.rsqrt(ms + RMS_EPS) * rw
            return jax.nn.silu(h @ W1) @ W2
        key = jax.random.key(seed)
        ks = jax.random.split(key, 9)
        B, T = (2, 128)
        x = jax.random.normal(ks[0], (B, T, D_MODEL), dtype=jnp.float32)
        router_w = jax.random.normal(ks[1], (D_MODEL, E_ROUTED), dtype=jnp.float32) * 0.006
        rms_w = jnp.ones((E_ROUTED, D_MODEL), dtype=jnp.float32)
        w1 = jax.random.normal(ks[2], (E_ROUTED, D_MODEL, HIDDEN), dtype=jnp.float32) * 0.02
        w2 = jax.random.normal(ks[3], (E_ROUTED, HIDDEN, D_MODEL), dtype=jnp.float32) * 0.02
        rms_w_s = jnp.ones((E_SHARED, D_MODEL), dtype=jnp.float32)
        w1_s = jax.random.normal(ks[4], (E_SHARED, D_MODEL, HIDDEN), dtype=jnp.float32) * 0.02
        w2_s = jax.random.normal(ks[5], (E_SHARED, HIDDEN, D_MODEL), dtype=jnp.float32) * 0.02
        return {'x': x, 'router_w': router_w, 'rms_w': rms_w, 'w1': w1, 'w2': w2, 'rms_w_s': rms_w_s, 'w1_s': w1_s, 'w2_s': w2_s}
    _L1_ffn_all = _L1_ffn_setup()
    _L1_ffn_in = {k: v for k, v in _L1_ffn_all.items() if k in ('router_w', 'rms_w', 'w1', 'w2', 'rms_w_s', 'w1_s', 'w2_s')}
    del _L1_ffn_all
    return {'x': x, 'ctx_1024': ctx_1024, 'mask_BxS2_bk0': mask_BxS2_bk0, 'L0_attn_conv_dw_w': _L0_attn_in['conv_dw_w'], 'L0_attn_conv_dw_b': _L0_attn_in['conv_dw_b'], 'L0_attn_conv_pw_w': _L0_attn_in['conv_pw_w'], 'L0_attn_conv_pw_b': _L0_attn_in['conv_pw_b'], 'L0_attn_conv_norm_g': _L0_attn_in['conv_norm_g'], 'L0_attn_gru_norm_g': _L0_attn_in['gru_norm_g'], 'L0_attn_gru_w': _L0_attn_in['gru_w'], 'L0_attn_ff_norm_g': _L0_attn_in['ff_norm_g'], 'L0_attn_ff_w1': _L0_attn_in['ff_w1'], 'L0_attn_ff_b1': _L0_attn_in['ff_b1'], 'L0_attn_ff_w2': _L0_attn_in['ff_w2'], 'L0_attn_ff_b2': _L0_attn_in['ff_b2'], 'L0_xattn_Wq': _L0_xattn_in['Wq'], 'L0_xattn_Wk': _L0_xattn_in['Wk'], 'L0_xattn_Wv': _L0_xattn_in['Wv'], 'L0_xattn_Wo': _L0_xattn_in['Wo'], 'L0_ffn_gamma_x': _L0_ffn_in['gamma_x'], 'L0_ffn_gamma_slot': _L0_ffn_in['gamma_slot'], 'L0_ffn_slot_embeds': _L0_ffn_in['slot_embeds'], 'L0_ffn_w1': _L0_ffn_in['w1'], 'L0_ffn_w2': _L0_ffn_in['w2'], 'L1_attn_W_qkv': _L1_attn_in['W_qkv'], 'L1_attn_b_qkv': _L1_attn_in['b_qkv'], 'L1_attn_W_out': _L1_attn_in['W_out'], 'L1_attn_b_out': _L1_attn_in['b_out'], 'L1_xattn_ln_x_g': _L1_xattn_in['ln_x_g'], 'L1_xattn_ln_x_b': _L1_xattn_in['ln_x_b'], 'L1_xattn_ln_l_g': _L1_xattn_in['ln_l_g'], 'L1_xattn_ln_l_b': _L1_xattn_in['ln_l_b'], 'L1_xattn_q_gamma': _L1_xattn_in['q_gamma'], 'L1_xattn_k_gamma': _L1_xattn_in['k_gamma'], 'L1_xattn_W_q': _L1_xattn_in['W_q'], 'L1_xattn_W_kv': _L1_xattn_in['W_kv'], 'L1_xattn_W_out': _L1_xattn_in['W_out'], 'L1_xattn_b_out': _L1_xattn_in['b_out'], 'L1_ffn_router_w': _L1_ffn_in['router_w'], 'L1_ffn_rms_w': _L1_ffn_in['rms_w'], 'L1_ffn_w1': _L1_ffn_in['w1'], 'L1_ffn_w2': _L1_ffn_in['w2'], 'L1_ffn_rms_w_s': _L1_ffn_in['rms_w_s'], 'L1_ffn_w1_s': _L1_ffn_in['w1_s'], 'L1_ffn_w2_s': _L1_ffn_in['w2_s']}

def reference(x, ctx_1024, mask_BxS2_bk0, L0_attn_conv_dw_w, L0_attn_conv_dw_b, L0_attn_conv_pw_w, L0_attn_conv_pw_b, L0_attn_conv_norm_g, L0_attn_gru_norm_g, L0_attn_gru_w, L0_attn_ff_norm_g, L0_attn_ff_w1, L0_attn_ff_b1, L0_attn_ff_w2, L0_attn_ff_b2, L0_xattn_Wq, L0_xattn_Wk, L0_xattn_Wv, L0_xattn_Wo, L0_ffn_gamma_x, L0_ffn_gamma_slot, L0_ffn_slot_embeds, L0_ffn_w1, L0_ffn_w2, L1_attn_W_qkv, L1_attn_b_qkv, L1_attn_W_out, L1_attn_b_out, L1_xattn_ln_x_g, L1_xattn_ln_x_b, L1_xattn_ln_l_g, L1_xattn_ln_l_b, L1_xattn_q_gamma, L1_xattn_k_gamma, L1_xattn_W_q, L1_xattn_W_kv, L1_xattn_W_out, L1_xattn_b_out, L1_ffn_router_w, L1_ffn_rms_w, L1_ffn_w1, L1_ffn_w2, L1_ffn_rms_w_s, L1_ffn_w1_s, L1_ffn_w2_s):
    import jax
    import jax.numpy as jnp

    def _L0_attn_ref(x, conv_dw_w, conv_dw_b, conv_pw_w, conv_pw_b, conv_norm_g, gru_norm_g, gru_w, ff_norm_g, ff_w1, ff_b1, ff_w2, ff_b2):
        import jax, jax.numpy as jnp
        import numpy as np
        import math
        DIM = 128
        K = 3
        NUM_LAYERS = 1
        RES_SCALE = 1.0 / math.sqrt(NUM_LAYERS)

        def rmsnorm(x, gamma):
            n = jnp.sqrt(jnp.sum(x * x, axis=-1, keepdims=True))
            return x / jnp.maximum(n, 1e-12) * x.shape[-1] ** 0.5 * (gamma + 1.0)

        def causal_dwconv(x, w_dw, b_dw, w_pw, b_pw):
            xt = jnp.transpose(x, (0, 2, 1))
            xt = jnp.pad(xt, ((0, 0), (0, 0), (K - 1, 0)))
            y = jax.lax.conv_general_dilated(xt, w_dw, window_strides=(1,), padding='VALID', feature_group_count=xt.shape[1], dimension_numbers=('NCH', 'OIH', 'NCH'))
            y = y + b_dw[None, :, None]
            y = jnp.transpose(y, (0, 2, 1))
            return jnp.einsum('bld,ed->ble', y, w_pw) + b_pw

        def log_g(x):
            return jnp.where(x >= 0, jnp.log(jax.nn.relu(x) + 0.5), -jax.nn.softplus(-x))

        def heinsen_scan_log(log_coeffs, log_values):
            a_star = jnp.cumsum(log_coeffs, axis=1)
            log_h = a_star + jax.lax.cumlogsumexp(log_values - a_star, axis=1)
            return jnp.exp(log_h)

        def min_gru(x, w_hg):
            hg = jnp.einsum('bld,ed->ble', x, w_hg)
            hidden, gate = jnp.split(hg, 2, axis=-1)
            log_coeffs = -jax.nn.softplus(gate)
            log_values = -jax.nn.softplus(-gate) + log_g(hidden)
            out = heinsen_scan_log(log_coeffs, log_values)
            next_hidden = out[:, -1:]
            return (out, next_hidden)

        def _reference_tuple_inner(x, conv_dw_w, conv_dw_b, conv_pw_w, conv_pw_b, conv_norm_g, gru_norm_g, gru_w, ff_norm_g, ff_w1, ff_b1, ff_w2, ff_b2):
            x = causal_dwconv(rmsnorm(x, conv_norm_g), conv_dw_w, conv_dw_b, conv_pw_w, conv_pw_b) * RES_SCALE + x
            gru_out, next_hidden = min_gru(rmsnorm(x, gru_norm_g), gru_w)
            x = gru_out * RES_SCALE + x
            h = rmsnorm(x, ff_norm_g)
            h = jax.nn.gelu(jnp.einsum('bld,ed->ble', h, ff_w1) + ff_b1, approximate=False)
            h = jnp.einsum('ble,de->bld', h, ff_w2) + ff_b2
            x = h * RES_SCALE + x
            return (x, next_hidden)
        return _reference_tuple_inner(x, conv_dw_w, conv_dw_b, conv_pw_w, conv_pw_b, conv_norm_g, gru_norm_g, gru_w, ff_norm_g, ff_w1, ff_b1, ff_w2, ff_b2)[0]

    def _L0_xattn_ref(q, k, v, Wq, Wk, Wv, Wo):
        import jax, jax.numpy as jnp
        import numpy as np
        B, S, E, H = (2, 256, 128, 16)
        D = E // H
        bs, seq_len, n_emb = q.shape
        qp = (q @ Wq.T).reshape(bs, seq_len, H, D).transpose(0, 2, 1, 3)
        kp = (k @ Wk.T).reshape(bs, seq_len, H, D).transpose(0, 2, 1, 3)
        vp = (v @ Wv.T).reshape(bs, seq_len, H, D).transpose(0, 2, 1, 3)
        scale = 1.0 / jnp.sqrt(jnp.float32(D))
        scores = scale * jnp.einsum('bhqd,bhkd->bhqk', qp, kp)
        probs = jax.nn.softmax(scores, axis=-1)
        atten = jnp.einsum('bhqk,bhkd->bhqd', probs, vp)
        atten = atten.transpose(0, 2, 1, 3).reshape(bs, seq_len, n_emb)
        return atten @ Wo.T

    def _L0_ffn_ref(x, gamma_x, gamma_slot, slot_embeds, w1, w2):
        import jax, jax.numpy as jnp
        import numpy as np
        EPS = 1e-12

        def rms_norm(t, gamma):
            n = jnp.maximum(jnp.linalg.norm(t, axis=-1, keepdims=True), EPS)
            scale = jnp.sqrt(jnp.asarray(t.shape[-1], t.dtype))
            return t / n * scale * gamma
        b, s, d = x.shape
        e, t, _ = slot_embeds.shape
        xn = rms_norm(x, gamma_x)
        se = rms_norm(slot_embeds, gamma_slot)
        logits = jnp.einsum('bsd,etd->bset', xn, se)
        dispatch = jax.nn.softmax(logits, axis=1)
        slots = jnp.einsum('bsd,bset->betd', xn, dispatch)
        h = jax.nn.gelu(slots @ w1, approximate=False)
        processed = h @ w2
        combine = jax.nn.softmax(logits.reshape(b, s, e * t), axis=-1)
        out = jnp.einsum('bnd,bsn->bsd', processed.reshape(b, e * t, d), combine)
        return out

    def _L1_attn_ref(x, W_qkv, b_qkv, W_out, b_out):
        import math
        import jax, jax.numpy as jnp
        import numpy as np
        B, T, H = (2, 256, 128)
        NH, WINDOW = (16, 32)
        HD = H // NH
        b, t, h = x.shape
        qkv = x @ W_qkv + b_qkv
        qkv = qkv.reshape(b, t, 3, NH, HD)
        qkv = jnp.transpose(qkv, (2, 0, 3, 1, 4))
        q, k, v = (qkv[0], qkv[1], qkv[2])
        scores = jnp.einsum('bnid,bnjd->bnij', q, k) / math.sqrt(HD)
        idx = jnp.arange(t)
        diff = idx[:, None] - idx[None, :]
        mask = (diff < 0) | (diff >= WINDOW)
        scores = jnp.where(mask[None, None], -jnp.inf, scores)
        attn = jax.nn.softmax(scores, axis=-1)
        out = jnp.einsum('bnij,bnjd->bnid', attn, v)
        out = jnp.transpose(out, (0, 2, 1, 3)).reshape(b, t, h)
        return out @ W_out + b_out

    def _L1_xattn_ref(x, latents, mask, ln_x_g, ln_x_b, ln_l_g, ln_l_b, q_gamma, k_gamma, W_q, W_kv, W_out, b_out):
        import jax, jax.numpy as jnp
        import numpy as np
        DIM = 128
        DIM_LATENT = 128
        DIM_HEAD = 64
        INNER = max(DIM, DIM_LATENT)
        HEADS = INNER // DIM_HEAD
        SCALE = DIM_HEAD ** (-0.5)
        LN_EPS = 1e-05
        RMS_EPS = 1e-08

        def layernorm(x, g, b):
            mu = jnp.mean(x, axis=-1, keepdims=True)
            var = jnp.mean(jnp.square(x - mu), axis=-1, keepdims=True)
            return (x - mu) * jax.lax.rsqrt(var + LN_EPS) * g + b

        def rmsnorm(x, gamma):
            n = jnp.linalg.norm(x, axis=-1, keepdims=True) * x.shape[-1] ** (-0.5)
            return x / jnp.maximum(n, RMS_EPS) * gamma
        b, n, _ = x.shape
        nl = latents.shape[1]
        xn = layernorm(x, ln_x_g, ln_x_b)
        ln = layernorm(latents, ln_l_g, ln_l_b)
        q = ln @ W_q
        kv = jnp.concatenate([xn @ W_kv, ln @ W_kv], axis=1)
        k, v = (kv[..., :INNER], kv[..., INNER:])
        to_heads = lambda t: t.reshape(t.shape[0], t.shape[1], HEADS, DIM_HEAD).transpose(0, 2, 1, 3)
        q, k, v = (to_heads(q), to_heads(k), to_heads(v))
        qn = rmsnorm(q, q_gamma) * SCALE
        kn = rmsnorm(k, k_gamma)
        sim = jnp.einsum('bhid,bhjd->bhij', qn, kn)
        full_mask = jnp.pad(mask, ((0, 0), (0, nl)), constant_values=True)
        neg = -jnp.finfo(sim.dtype).max
        sim = jnp.where(full_mask[:, None, None, :], sim, neg)
        attn = jax.nn.softmax(sim.astype(jnp.float32), axis=-1).astype(sim.dtype)
        out = jnp.einsum('bhij,bhjd->bhid', attn, v)
        out = out.transpose(0, 2, 1, 3).reshape(b, nl, INNER)
        return out @ W_out + b_out

    def _L1_ffn_ref(x, router_w, rms_w, w1, w2, rms_w_s, w1_s, w2_s):
        import jax, jax.numpy as jnp
        import numpy as np
        D_MODEL = 128
        HIDDEN = 256
        E_ROUTED = 14
        E_SHARED = 2
        TOP_K = 2
        EPS = 1e-09
        RMS_EPS = 1.1920929e-07

        def _ffn(xn, rw, W1, W2):
            ms = jnp.mean(xn * xn, axis=-1, keepdims=True)
            h = xn * jax.lax.rsqrt(ms + RMS_EPS) * rw
            return jax.nn.silu(h @ W1) @ W2
        B, T, D = x.shape
        N = B * T
        xf = x.reshape(N, D)
        gates = jax.nn.softmax(xf @ router_w, axis=-1)
        top_v, top_i = jax.lax.top_k(gates, TOP_K)
        masked = jnp.zeros_like(gates).at[jnp.arange(N)[:, None], top_i].set(top_v)
        masked = masked / (masked.sum(axis=-1, keepdims=True) + EPS)
        routed = jax.vmap(lambda rw_, W1_, W2_: _ffn(xf, rw_, W1_, W2_))(rms_w, w1, w2)
        routed_out = jnp.einsum('end,ne->nd', routed, masked)
        shared = jax.vmap(lambda rw_, W1_, W2_: _ffn(xf, rw_, W1_, W2_))(rms_w_s, w1_s, w2_s).sum(0)
        return (routed_out + shared).reshape(B, T, D)
    x = _layernorm(x + _L0_attn_ref(x, L0_attn_conv_dw_w, L0_attn_conv_dw_b, L0_attn_conv_pw_w, L0_attn_conv_pw_b, L0_attn_conv_norm_g, L0_attn_gru_norm_g, L0_attn_gru_w, L0_attn_ff_norm_g, L0_attn_ff_w1, L0_attn_ff_b1, L0_attn_ff_w2, L0_attn_ff_b2), axis=-1)
    x = _layernorm(x + _L0_xattn_ref(x, ctx_1024, ctx_1024, L0_xattn_Wq, L0_xattn_Wk, L0_xattn_Wv, L0_xattn_Wo), axis=-1)
    x = _layernorm(x + _L0_ffn_ref(x, L0_ffn_gamma_x, L0_ffn_gamma_slot, L0_ffn_slot_embeds, L0_ffn_w1, L0_ffn_w2), axis=-1)
    x = _layernorm(x + _L1_attn_ref(x, L1_attn_W_qkv, L1_attn_b_qkv, L1_attn_W_out, L1_attn_b_out), axis=-1)
    x = _layernorm(x + _L1_xattn_ref(ctx_1024, x, mask_BxS2_bk0, L1_xattn_ln_x_g, L1_xattn_ln_x_b, L1_xattn_ln_l_g, L1_xattn_ln_l_b, L1_xattn_q_gamma, L1_xattn_k_gamma, L1_xattn_W_q, L1_xattn_W_kv, L1_xattn_W_out, L1_xattn_b_out), axis=-1)
    x = _layernorm(x + _L1_ffn_ref(x, L1_ffn_router_w, L1_ffn_rms_w, L1_ffn_w1, L1_ffn_w2, L1_ffn_rms_w_s, L1_ffn_w1_s, L1_ffn_w2_s), axis=-1)
    return x

_drawn_inputs = setup_inputs


def setup_inputs(seed=0):
    import zlib

    import numpy as np

    out = dict(_drawn_inputs(seed))
    spreads = {'L0_attn_ff_b2': (0.0, 0.1),
     'L0_ffn_gamma_x': (1.0, 0.2),
     'L0_ffn_gamma_slot': (1.0, 0.2),
     'L1_attn_b_qkv': (0.0, 0.1),
     'L1_attn_b_out': (0.0, 0.1),
     'L1_xattn_ln_x_g': (1.0, 0.2),
     'L1_xattn_ln_x_b': (0.0, 0.352),
     'L1_xattn_ln_l_g': (1.0, 0.2),
     'L1_xattn_ln_l_b': (0.0, 0.1),
     'L1_xattn_q_gamma': (1.0, 0.2),
     'L1_xattn_k_gamma': (1.0, 0.2),
     'L1_xattn_b_out': (0.0, 0.1),
     'L1_ffn_rms_w': (1.0, 0.6),
     'L1_ffn_rms_w_s': (1.0, 0.6)}
    factors = {'L0_attn_conv_dw_w': 8.0,
     'L0_attn_conv_dw_b': 8.0,
     'L0_attn_conv_pw_w': 7.691,
     'L0_attn_conv_pw_b': 3.184,
     'L0_attn_conv_norm_g': 8.0,
     'L0_attn_gru_norm_g': 36.427,
     'L0_attn_ff_norm_g': 60.241,
     'L0_attn_ff_b1': 8.0,
     'L0_xattn_Wq': 8.0,
     'L0_xattn_Wk': 8.0}
    for name, (base, spread) in spreads.items():
        noise = np.random.default_rng([zlib.crc32(name.encode()), seed]).standard_normal(out[name].shape)
        drawn = base * np.exp(spread * noise) if base else spread * noise
        out[name] = jnp.asarray(drawn.astype(out[name].dtype))
    for name, factor in factors.items():
        out[name] = (out[name] * factor).astype(out[name].dtype)
    return out
```

```python
from contextlib import ExitStack

import numpy as np

import concourse.bass as bass
from concourse import mybir

ALU = mybir.AluOpType
ACT = mybir.ActivationFunctionType
F32 = mybir.dt.float32
BF16 = mybir.dt.bfloat16
U8 = mybir.dt.uint8
AX_X = mybir.AxisListType.X

P = 128
D = 128
BATCH, SEQ = 64, 64
SPT = P // SEQ
TILES = BATCH // SPT
HIDDEN = 4 * D
SLOTS = 512
HEADS, HD = 16, 8
ROUTED, SHARED, EH = 14, 2, 256
EXPERTS = ROUTED + SHARED
WINDOW = 32
LN_EPS = 1e-5
NORM_FLOOR = 1e-24


class Signal:

    def __init__(self, ctx, nc, name, per):
        self.sem, self.per = nc.alloc_semaphore(name), per

    def now(self, turn, n):
        return (turn + 1) * self.per + n

    def before(self, turn, n):
        return turn * self.per + n


def credit(engine, *signals):
    for s in signals:
        engine.nop().then_inc(s.sem, s.per)
class NormTail:

    def __init__(self, ctx, nc, name, n):
        def sb(part, shape):
            return ctx.enter_context(nc.sbuf_tensor(f"{name}_{part}", shape, F32))

        def sig(part):
            return Signal(ctx, nc, f"{name}_{part}", 1)

        self.nc, self.n = nc, n
        self.total = sb("total", [P, n, D])
        self.stats = sb("stats", [P, n, 6])
        self.moments = sb("moments", [P, n, 2])
        self.var_eps = sb("var_eps", [P, n])
        self.rstd = sb("rstd", [P, n])
        self.scrap = sb("scrap", [P, 1])
        self.added, self.counted, self.aggregated, self.floored = sig("added"), sig("counted"), sig("aggregated"), sig("floored")
        self.rooted, self.done = sig("rooted"), sig("done")

    def credit_vector(self, dve):
        credit(dve, self.added, self.counted, self.aggregated, self.floored, self.done)

    def credit_pool(self, pool):
        credit(pool, self.rooted)

    def moments_vector(self, dve, t, branch, residual):
        nc = self.nc
        nc.vector.tensor_tensor(self.total[:, :, :], branch, residual, ALU.add).then_inc(self.added.sem, 1)
        dve.wait_ge(self.added.sem, self.added.now(t, 1))
        for j in range(self.n):
            last = nc.vector.bn_stats(self.stats[:, j, :], self.total[:, j, :])
        last.then_inc(self.counted.sem, 1)
        dve.wait_ge(self.counted.sem, self.counted.now(t, 1))
        nc.vector.memset(self.scrap[:, :], 0.0)
        for j in range(self.n):
            last = nc.vector.bn_aggr(self.moments[:, j, :], self.stats[:, j, :])
        last.then_inc(self.aggregated.sem, 1)
        dve.wait_ge(self.aggregated.sem, self.aggregated.now(t, 1))
        dve.wait_ge(self.rooted.sem, self.rooted.before(t, 1))
        nc.vector.tensor_scalar(self.var_eps[:, :], self.moments[:, :, 1], LN_EPS, None, ALU.add)\
            .then_inc(self.floored.sem, 1)

    def root_pool(self, pool, t, minus_half):
        pool.wait_ge(self.done.sem, self.done.before(t, 1))
        pool.wait_ge(self.floored.sem, self.floored.now(t, 1))
        self.nc.gpsimd.tensor_tensor(self.rstd[:, :], self.var_eps[:, :], minus_half[:, 0:self.n], ALU.pow)\
            .then_inc(self.rooted.sem, 1)

    def write_vector(self, dve, t, out_tile):
        dve.wait_ge(self.rooted.sem, self.rooted.now(t, 1))
        for j in range(self.n):
            last = self.nc.vector.tensor_scalar(out_tile(j), self.total[:, j, :].unsqueeze(1), self.moments[:, j, 0:1],
                                                self.rstd[:, j:j + 1], ALU.subtract, ALU.mult)
        last.then_inc(self.done.sem, 1)
def stage_conv_gru(nc, X, W):
    GT = 4
    GN = GT * P
    U = 2
    TURNS = TILES // (GT * U)
    NSEQ = GN // SEQ
    with ExitStack() as ctx:
        def sb(name, shape, dt=F32):
            return ctx.enter_context(nc.sbuf_tensor("cg_" + name, shape, dt))

        def sig(name, per=U):
            return Signal(ctx, nc, "cg_" + name, per)

        squares = sb("squares", [P, U, GT, D])
        ssq = sb("ssq", [P, U, 3, GT])
        floored = sb("floored", [P, U, 3, GT])
        rnorm = sb("rnorm", [P, U, 3, GT])
        x_bias = sb("x_bias", [P, U, GT, D])
        x_conv = sb("x_conv", [P, U, GT, D])
        x_gru = sb("x_gru", [P, U, GT, D])
        x_twice = sb("x_twice", [P, U, GT, D])
        x_scaled = sb("x_scaled", [P, U, GT, D])
        padded = sb("padded", [P, U, NSEQ, SEQ + 2])
        conv = sb("conv", [P, U, GN])
        xn = sb("xn", [P, U, GN])
        sig_hidden = sb("sig_hidden", [P, U, GN])
        update = sb("update", [P, U, GN])
        keep = sb("keep", [P, U, GN])
        hgru = sb("hgru", [P, U, GN])
        hff = sb("hff", [P, U, 4, GN])
        total = sb("total", [P, U, GT, D])
        stats = sb("stats", [P, U, GT, 6])
        moments = sb("moments", [P, U, GT, 2])
        var_eps = sb("var_eps", [P, U, GT])
        rstd = sb("rstd", [P, U, GT])
        scrap = sb("scrap", [P, 1])
        ps = ctx.enter_context(nc.psum_tensor("cg_ps", [P, U, 4, GN], F32))
        gain1, gain2, gain3 = (W["gains"][:, k:k + 1] for k in range(3))

        zeroed = nc.alloc_semaphore("cg_zeroed")
        s_sq = [sig(f"sq{k}") for k in range(3)]
        s_fl = [sig(f"fl{k}") for k in range(3)]
        s_rn = [sig(f"rn{k}") for k in range(3)]
        s_xs = [sig(f"xs{k}") for k in range(3)]
        s_xt = [sig(f"xt{k}") for k in range(3)]
        s_xn = [sig(f"xn{k}") for k in range(3)]
        s_xb = sig("xb")
        s_cv = sig("cv", 3 * U)
        s_pw = sig("pw")
        s_x1 = sig("x1")
        s_hg = sig("hg")
        s_sg = sig("sg", 2 * U)
        s_gr = sig("gr", 2 * U)
        s_sc = sig("sc")
        s_ht = sig("ht")
        s_x2 = sig("x2")
        s_x2b = sig("x2b", 2 * U)
        s_f1 = sig("f1", 4 * U)
        s_ge = sig("ge", 4 * U)
        s_f2 = sig("f2")
        s_tt = sig("tt")
        s_bs = sig("bs")
        s_mv = sig("mv")
        s_ve = sig("ve")
        s_rs = sig("rs")
        s_out = sig("out")

        block = ctx.enter_context(nc.Block())

        def group(t, u):
            return X[:, bass.ds((t * U + u) * GT, GT), :]

        def tile_of(t, u, j):
            return X[:, bass.ds((t * U + u) * GT + j, 1), :]

        @block.scalar
        def _(act):
            credit(act, *s_sq, *s_xn, s_sg, s_ge)
            act.wait_ge(zeroed, 2)
            with act.Fori(0, TURNS) as t:
                def sum_squares(k, source):
                    for u in range(U):
                        if k == 1:
                            act.wait_ge(s_x1.sem, s_x1.now(t, u + 1))
                        if k == 2:
                            act.wait_ge(s_x2.sem, s_x2.now(t, u + 1))
                        act.wait_ge(s_fl[k].sem, s_fl[k].before(t, u + 1))
                        for j in range(GT):
                            last = nc.scalar.activation(squares[:, u, j, :].unsqueeze(1), source(u, j), ACT.Square,
                                                        accum_out=ssq[:, u, k, j:j + 1])
                        last.then_inc(s_sq[k].sem, 1)

                def to_features(k):
                    for u in range(U):
                        act.wait_ge(s_xt[k].sem, s_xt[k].now(t, u + 1))
                        if k == 0:
                            act.wait_ge(s_cv.sem, s_cv.before(t, 3 * u + 3))
                            out = padded[:, u, :, 2:]
                            src = ps[:, u, 0, :].rearrange("p (b s) -> p b s", s=SEQ)
                        else:
                            if k == 1:
                                act.wait_ge(s_f1.sem, s_f1.before(t, 4 * u + 4))
                            else:
                                act.wait_ge(s_hg.sem, s_hg.now(t, u + 1))
                            out, src = xn[:, u, :], ps[:, u, 0, :]
                        nc.scalar.activation(out, src, ACT.Copy, scale=(gain1, gain2, gain3)[k])\
                            .then_inc(s_xn[k].sem, 1)

                sum_squares(0, lambda u, j: tile_of(t, u, j))
                to_features(0)
                sum_squares(1, lambda u, j: x_conv[:, u, j, :].unsqueeze(1))
                to_features(1)
                for u in range(U):
                    act.wait_ge(s_hg.sem, s_hg.now(t, u + 1))
                    act.wait_ge(s_gr.sem, s_gr.before(t, 2 * u + 2))
                    nc.scalar.activation(sig_hidden[:, u, :], ps[:, u, 1, :], ACT.Sigmoid).then_inc(s_sg.sem, 1)
                    nc.scalar.activation(update[:, u, :], ps[:, u, 2, :], ACT.Sigmoid)
                    act.wait_ge(s_sc.sem, s_sc.before(t, u + 1))
                    nc.scalar.activation(keep[:, u, :].rearrange("p (b s) -> p b s", s=SEQ)[:, :, 1:],
                                         ps[:, u, 2, :].rearrange("p (b s) -> p b s", s=SEQ)[:, :, 1:],
                                         ACT.Sigmoid, scale=-1.0).then_inc(s_sg.sem, 1)
                sum_squares(2, lambda u, j: x_gru[:, u, j, :].unsqueeze(1))
                to_features(2)
                for u in range(U):
                    act.wait_ge(s_f2.sem, s_f2.before(t, u + 1))
                    for c in range(4):
                        act.wait_ge(s_f1.sem, s_f1.now(t, 4 * u + c + 1))
                        nc.scalar.activation(hff[:, u, c, :], ps[:, u, 1 + c % 3, :], ACT.Gelu,
                                             bias=W["ff_b1"][:, c:c + 1]).then_inc(s_ge.sem, 1)

        @block.gpsimd
        def _(pool):
            nc.gpsimd.memset(padded[:, :, :, 0:2], 0.0).then_inc(zeroed, 1)
            nc.gpsimd.memset(keep[:, :, :].rearrange("p u (b s) -> p u b s", s=SEQ)[:, :, :, 0:1], 0.0)\
                .then_inc(zeroed, 1)
            credit(pool, *s_rn, s_xb, s_x2b, s_rs)
            with pool.Fori(0, TURNS) as t:
                def reciprocal_norm(k):
                    for u in range(U):
                        pool.wait_ge(s_xs[k].sem, s_xs[k].before(t, u + 1))
                        if k == 0:
                            pool.wait_ge(s_out.sem, s_out.before(t, u + 1))
                        pool.wait_ge(s_fl[k].sem, s_fl[k].now(t, u + 1))
                        nc.gpsimd.tensor_tensor(rnorm[:, u, k, :], floored[:, u, k, :], W["minus_half"][:, 0:GT],
                                                ALU.pow).then_inc(s_rn[k].sem, 1)

                reciprocal_norm(0)
                for u in range(U):
                    nc.gpsimd.tensor_tensor(x_bias[:, u, :, :], group(t, u),
                                            W["pw_b"].unsqueeze(1).broadcast_to((P, GT, D)), ALU.add).then_inc(s_xb.sem, 1)
                    nc.gpsimd.tensor_tensor(x_twice[:, u, :, :], group(t, u),
                                            W["ff_b2"].unsqueeze(1).broadcast_to((P, GT, D)), ALU.add)\
                        .then_inc(s_x2b.sem, 1)
                reciprocal_norm(1)
                reciprocal_norm(2)
                for u in range(U):
                    pool.wait_ge(s_x2b.sem, s_x2b.now(t, U + u))
                    pool.wait_ge(s_x2.sem, s_x2.now(t, u + 1))
                    nc.gpsimd.tensor_tensor(x_twice[:, u, :, :], x_twice[:, u, :, :], x_gru[:, u, :, :], ALU.add)\
                        .then_inc(s_x2b.sem, 1)
                for u in range(U):
                    pool.wait_ge(s_ve.sem, s_ve.now(t, u + 1))
                    nc.gpsimd.tensor_tensor(rstd[:, u, :], var_eps[:, u, :], W["minus_half"][:, 0:GT], ALU.pow)\
                        .then_inc(s_rs.sem, 1)

        @block.tensor
        def _(pe):
            credit(pe, *s_xt, s_pw, s_hg, s_ht, s_f1, s_f2)
            with pe.Fori(0, TURNS) as t:
                def transposes(k):
                    for u in range(U):
                        pe.wait_ge(s_xs[k].sem, s_xs[k].now(t, u + 1))
                        if k == 0:
                            pe.wait_ge(s_tt.sem, s_tt.before(t, u + 1))
                        for j in range(GT):
                            last = pe.transpose(ps[:, u, 0, j * P:(j + 1) * P], x_scaled[:, u, j, :], W["ident"])
                        last.then_inc(s_xt[k].sem, 1)

                transposes(0)
                for u in range(U):
                    pe.wait_ge(s_cv.sem, s_cv.now(t, 3 * u + 3))
                    for j in range(GT):
                        last = pe.matmul(ps[:, u, 0, j * P:(j + 1) * P], conv[:, u, j * P:(j + 1) * P], W["pwT"],
                                         start=True, stop=True)
                    last.then_inc(s_pw.sem, 1)
                transposes(1)
                for u in range(U):
                    pe.wait_ge(s_xn[1].sem, s_xn[1].now(t, u + 1))
                    pe.wait_ge(s_ge.sem, s_ge.before(t, 4 * u + 4))
                    pe.matmul(ps[:, u, 1, :], W["gruT"][:, 0:D], xn[:, u, :], start=True, stop=True)
                    pe.matmul(ps[:, u, 2, :], W["gruT"][:, D:2 * D], xn[:, u, :], start=True, stop=True)\
                        .then_inc(s_hg.sem, 1)
                for u in range(U):
                    pe.wait_ge(s_sc.sem, s_sc.now(t, u + 1))
                    for j in range(GT):
                        last = pe.transpose(ps[:, u, 0, j * P:(j + 1) * P], hgru[:, u, j * P:(j + 1) * P], W["ident"])
                    last.then_inc(s_ht.sem, 1)
                transposes(2)
                for u in range(U):
                    pe.wait_ge(s_xn[2].sem, s_xn[2].now(t, u + 1))
                    for c in range(4):
                        if c == 3:
                            pe.wait_ge(s_ge.sem, s_ge.now(t, 4 * u + 1))
                        pe.matmul(ps[:, u, 1 + c % 3, :], W["ff1T"][:, c * P:(c + 1) * P], xn[:, u, :],
                                  start=True, stop=True).then_inc(s_f1.sem, 1)
                for u in range(U):
                    pe.wait_ge(s_ge.sem, s_ge.now(t, 4 * u + 4))
                    for j in range(GT):
                        for c in range(4):
                            last = pe.matmul(ps[:, u, 0, j * P:(j + 1) * P], hff[:, u, c, j * P:(j + 1) * P],
                                             W["ff2T"][:, c, :], start=(c == 0), stop=(c == 3))
                    last.then_inc(s_f2.sem, 1)

        @block.vector
        def _(dve):
            credit(dve, *s_xs, *s_fl, s_ve, s_cv, s_x1, s_gr, s_sc, s_x2, s_tt, s_bs, s_mv, s_out)
            dve.wait_ge(zeroed, 2)
            with dve.Fori(0, TURNS) as t:
                def scale_rows(k, source):
                    for u in range(U):
                        dve.wait_ge(s_sq[k].sem, s_sq[k].now(t, u + 1))
                        nc.vector.tensor_scalar(floored[:, u, k, :], ssq[:, u, k, :], NORM_FLOOR, None, ALU.max)\
                            .then_inc(s_fl[k].sem, 1)
                    for u in range(U):
                        dve.wait_ge(s_rn[k].sem, s_rn[k].now(t, u + 1))
                        if k == 0:
                            dve.wait_ge(s_xt[2].sem, s_xt[2].before(t, u + 1))
                            dve.wait_ge(s_out.sem, s_out.before(t, u + 1))
                        else:
                            dve.wait_ge(s_xt[k - 1].sem, s_xt[k - 1].now(t, u + 1))
                        for j in range(GT):
                            last = nc.vector.tensor_scalar(x_scaled[:, u, j, :].unsqueeze(1), source(u, j),
                                                           rnorm[:, u, k, j:j + 1], None, ALU.mult)
                        last.then_inc(s_xs[k].sem, 1)

                scale_rows(0, lambda u, j: tile_of(t, u, j))
                for u in range(U):
                    y = conv[:, u, :].rearrange("p (b s) -> p b s", s=SEQ)
                    dve.wait_ge(s_xn[0].sem, s_xn[0].now(t, u + 1))
                    dve.wait_ge(s_pw.sem, s_pw.before(t, u + 1))
                    nc.vector.tensor_scalar(y, padded[:, u, :, 0:SEQ], W["dw"][:, 0:1], W["dw_b"], ALU.mult, ALU.add)\
                        .then_inc(s_cv.sem, 1)
                    for k in (1, 2):
                        dve.wait_ge(s_cv.sem, s_cv.now(t, 3 * u + k))
                        nc.vector.scalar_tensor_tensor(out=y, in0=padded[:, u, :, k:k + SEQ], scalar=W["dw"][:, k:k + 1],
                                                       in1=y, op0=ALU.mult, op1=ALU.add).then_inc(s_cv.sem, 1)
                for u in range(U):
                    dve.wait_ge(s_pw.sem, s_pw.now(t, u + 1))
                    dve.wait_ge(s_xb.sem, s_xb.now(t, u + 1))
                    nc.vector.tensor_tensor(x_conv[:, u, :, :], ps[:, u, 0, :].rearrange("p (j d) -> p j d", d=D),
                                            x_bias[:, u, :, :], ALU.add).then_inc(s_x1.sem, 1)
                    dve.wait_ge(s_x1.sem, s_x1.now(t, u + 1))
                scale_rows(1, lambda u, j: x_conv[:, u, j, :].unsqueeze(1))
                for u in range(U):
                    dve.wait_ge(s_sg.sem, s_sg.now(t, 2 * u + 1))
                    nc.vector.scalar_tensor_tensor(out=sig_hidden[:, u, :], in0=ps[:, u, 1, :], scalar=0.5,
                                                   in1=sig_hidden[:, u, :], op0=ALU.add, op1=ALU.max)\
                        .then_inc(s_gr.sem, 1)
                    dve.wait_ge(s_gr.sem, s_gr.now(t, 2 * u + 1))
                    dve.wait_ge(s_sg.sem, s_sg.now(t, 2 * u + 2))
                    nc.vector.tensor_tensor(update[:, u, :], update[:, u, :], sig_hidden[:, u, :], ALU.mult)\
                        .then_inc(s_gr.sem, 1)
                    dve.wait_ge(s_gr.sem, s_gr.now(t, 2 * u + 2))
                    dve.wait_ge(s_ht.sem, s_ht.before(t, u + 1))
                    nc.vector.tensor_tensor_scan(hgru[:, u, :], keep[:, u, :], update[:, u, :], 0.0, ALU.mult, ALU.add)\
                        .then_inc(s_sc.sem, 1)
                for u in range(U):
                    dve.wait_ge(s_ht.sem, s_ht.now(t, u + 1))
                    nc.vector.tensor_tensor(x_gru[:, u, :, :], ps[:, u, 0, :].rearrange("p (j d) -> p j d", d=D),
                                            x_conv[:, u, :, :], ALU.add).then_inc(s_x2.sem, 1)
                    dve.wait_ge(s_x2.sem, s_x2.now(t, u + 1))
                scale_rows(2, lambda u, j: x_gru[:, u, j, :].unsqueeze(1))
                for u in range(U):
                    dve.wait_ge(s_f2.sem, s_f2.now(t, u + 1))
                    dve.wait_ge(s_x2b.sem, s_x2b.now(t, U + u + 1))
                    nc.vector.tensor_tensor(total[:, u, :, :], ps[:, u, 0, :].rearrange("p (j d) -> p j d", d=D),
                                            x_twice[:, u, :, :], ALU.add).then_inc(s_tt.sem, 1)
                    dve.wait_ge(s_tt.sem, s_tt.now(t, u + 1))
                    for j in range(GT):
                        last = nc.vector.bn_stats(stats[:, u, j, :], total[:, u, j, :])
                    last.then_inc(s_bs.sem, 1)
                    dve.wait_ge(s_bs.sem, s_bs.now(t, u + 1))
                    nc.vector.memset(scrap[:, :], 0.0)
                    for j in range(GT):
                        last = nc.vector.bn_aggr(moments[:, u, j, :], stats[:, u, j, :])
                    last.then_inc(s_mv.sem, 1)
                    dve.wait_ge(s_mv.sem, s_mv.now(t, u + 1))
                    nc.vector.tensor_scalar(var_eps[:, u, :], moments[:, u, :, 1], LN_EPS, None, ALU.add)\
                        .then_inc(s_ve.sem, 1)
                for u in range(U):
                    dve.wait_ge(s_rs.sem, s_rs.now(t, u + 1))
                    for j in range(GT):
                        last = nc.vector.tensor_scalar(tile_of(t, u, j), total[:, u, j, :].unsqueeze(1),
                                                       moments[:, u, j, 0:1], rstd[:, u, j:j + 1],
                                                       ALU.subtract, ALU.mult)
                    last.then_inc(s_out.sem, 1)
def stage_attention(nc, X, W, layer, ctx_in):
    NT = 2
    NB = NT * SPT
    TN = NT * P
    TURNS = TILES // NT
    cross = layer == 0
    if cross:
        w_q, w_k, w_v, w_o = W["WqT"], W["WkT"], W["WvT"], W["WoT"]
    else:
        w_q, w_k, w_v, w_o = W["Wqkv"][:, 0:D], W["Wqkv"][:, D:2 * D], W["Wqkv"][:, 2 * D:], W["Wout"]
    name = f"at{layer}_"
    with ExitStack() as ctx:
        def sb(n, shape, dt=F32):
            return ctx.enter_context(nc.sbuf_tensor(name + n, shape, dt))

        def ps(n, shape):
            return ctx.enter_context(nc.psum_tensor(name + n, shape, F32))

        def sig(n, per=1):
            return Signal(ctx, nc, name + n, per)

        x_in = sb("x_in", [P, NT, D])
        c_in = sb("c_in", [P, NT, D]) if cross else None
        feats = sb("feats", [P, 2, TN])
        spread_q = sb("spread_q", [P, NB, 2, 2, SEQ])
        spread_k = sb("spread_k", [P, NB, 4, SEQ])
        spread_v = sb("spread_v", [P, NB, 2, 4, 4, HD])
        neg_max = sb("neg_max", [P, NB, 8])
        shifted = sb("shifted", [P, NB, 8, SEQ])
        probs = sb("probs", [P, NB, 8, SEQ])
        sums = sb("sums", [P, NB, 8])
        rsum = sb("rsum", [P, NB, 8])
        probs_n = sb("probs_n", [P, NB, 8, SEQ])
        probs_t = sb("probs_t", [P, NB, 2, 2 * P])
        mixed = sb("mixed", [P, NB, SEQ])
        residual = sb("residual", [P, NT, D])
        q_bias = sb("q_bias", [P, 1])
        k_bias = sb("k_bias", [P, 4])
        window = sb("window", [P, 8, SEQ], BF16) if not cross else None
        ident_b = sb("ident_b", [P, P], BF16) if not cross else None
        p_t = ps("p_t", [P, 2, TN])
        p_qk = ps("p_qk", [P, 2, TN])
        p_v = ps("p_v", [P, NB, D])
        p_s = ps("p_s", [P, 2, 8, SEQ])
        p_pt = ps("p_pt", [P, 2, 2, 2 * P])
        p_o = ps("p_o", [P, 2, 4, SEQ])
        p_y = p_o[:, 0, :, :].rearrange("p g s -> p (g s)").rearrange("p (j d) -> p j d", j=NT)

        tail = NormTail(ctx, nc, name + "tail", NT)
        constants = nc.alloc_semaphore(name + "constants")
        x_copied = sig("x_copied")
        c_landed = sig("c_landed", 16)
        turned = sig("turned")
        feats_done = sig("feats_done")
        qk_done = sig("qk_done")
        q_spread = sig("q_spread")
        k_spread_a, k_spread_v = sig("k_spread_a"), sig("k_spread_v")
        v_done = sig("v_done")
        v_spread = sig("v_spread")
        scored = sig("scored", NB)
        maxed = sig("maxed", NB)
        shift_done = sig("shift_done", NB)
        exped = sig("exped", NB)
        summed = sig("summed", NB)
        inverted = sig("inverted", NB)
        normed = sig("normed", NB)
        probs_turned = sig("probs_turned", NB)
        probs_copied = sig("probs_copied", NB)
        weighted = sig("weighted", NB)
        mixed_a, mixed_v = sig("mixed_a", 2), sig("mixed_v", 2)
        projected = sig("projected")
        residual_done = sig("residual_done")

        block = ctx.enter_context(nc.Block())
        CONSTANTS = 4 if cross else 8

        def tiles(t):
            return X[:, bass.ds(t * NT, NT), :]

        def all_turns(engine, turn):
            with engine.Fori(0, TURNS - 2) as t:
                turn(t, True, True)
            turn(TURNS - 2, True, False)
            turn(TURNS - 1, False, False)

        @block.sync
        def _(sp):
            if cross:
                def load(t):
                    sp.wait_ge(turned.sem, turned.before(t, 1))
                    sp.dma_start(c_in[:, :, :], ctx_in[bass.ds(t * TN, TN), :].rearrange("(j p) d -> p j d", p=P))\
                        .then_inc(c_landed.sem, 16)
                with sp.Fori(0, TURNS) as t:
                    load(t)
                sp.wait_ge(c_landed.sem, 16 * TURNS)

        @block.gpsimd
        def _(pool):
            nc.gpsimd.memset(spread_q[:, :, :, :, :], 0.0).then_inc(constants, 1)
            nc.gpsimd.memset(spread_v[:, :, :, :, :, :], 0.0).then_inc(constants, 1)
            if not cross:
                nc.gpsimd.tensor_copy(ident_b[:, :], W["ident"]).then_inc(constants, 1)
                nc.gpsimd.tensor_copy(window[:, :, :], W["window"].unsqueeze(1).broadcast_to((P, 8, SEQ)))\
                    .then_inc(constants, 1)
            credit(pool, x_copied, normed, residual_done)
            tail.credit_pool(pool)

            def copy_x(t):
                pool.wait_ge(turned.sem, turned.before(t, 1))
                nc.gpsimd.tensor_copy(x_in[:, :, :], tiles(t)).then_inc(x_copied.sem, 1)

            def normalise(t, b):
                pool.wait_ge(probs_turned.sem, probs_turned.before(t, b + 1))
                pool.wait_ge(inverted.sem, inverted.now(t, b + 1))
                nc.gpsimd.tensor_tensor(probs_n[:, b, :, :], probs[:, b, :, :],
                                        rsum[:, b, :].unsqueeze(2).broadcast_to((P, 8, SEQ)), ALU.mult)\
                    .then_inc(normed.sem, 1)

            def keep_residual(t):
                if cross:
                    nc.gpsimd.tensor_copy(residual[:, :, :], tiles(t)).then_inc(residual_done.sem, 1)
                else:
                    nc.gpsimd.tensor_tensor(residual[:, :, :], tiles(t), W["out_b"].unsqueeze(1).broadcast_to((P, NT, D)),
                                            ALU.add).then_inc(residual_done.sem, 1)

            def turn(t, one, two):
                if two:
                    copy_x(t + 2)
                if one:
                    for b in range(NB - 1):
                        normalise(t + 1, b)
                keep_residual(t)
                tail.root_pool(pool, t, W["minus_half"])
                if one:
                    normalise(t + 1, NB - 1)

            copy_x(0)
            copy_x(1)
            for b in range(NB):
                normalise(0, b)
            all_turns(pool, turn)

        @block.tensor
        def _(pe):
            credit(pe, turned, qk_done, v_done, scored, probs_turned, weighted, projected)
            pe.wait_ge(constants, CONSTANTS)

            def transposes(t):
                pe.wait_ge(x_copied.sem, x_copied.now(t, 1))
                pe.wait_ge(feats_done.sem, feats_done.before(t, 1))
                for j in range(NT):
                    last = pe.transpose(p_t[:, 0, j * P:(j + 1) * P], x_in[:, j, :], W["ident"])
                if cross:
                    pe.wait_ge(c_landed.sem, (t + 1) * 16)
                    for j in range(NT):
                        last = pe.transpose(p_t[:, 1, j * P:(j + 1) * P], c_in[:, j, :], W["ident"])
                last.then_inc(turned.sem, 1)

            def queries_keys(t):
                pe.wait_ge(feats_done.sem, feats_done.now(t, 1))
                pe.wait_ge(q_spread.sem, q_spread.before(t, 1))
                pe.wait_ge(k_spread_a.sem, k_spread_a.before(t, 1))
                pe.wait_ge(k_spread_v.sem, k_spread_v.before(t, 1))
                pe.matmul(p_qk[:, 0, :], w_q, feats[:, 0, :], start=True, stop=True)
                pe.matmul(p_qk[:, 1, :], w_k, feats[:, 1 if cross else 0, :], start=True, stop=True)\
                    .then_inc(qk_done.sem, 1)

            def values(t):
                pe.wait_ge(v_spread.sem, v_spread.before(t, 1))
                for b in range(NB):
                    kv = feats[:, 1 if cross else 0, b * SEQ:(b + 1) * SEQ]
                    for half in range(2):
                        last = pe.matmul(p_v[SEQ * half:SEQ * half + SEQ, b, :], kv, w_v, start=True, stop=True)
                last.then_inc(v_done.sem, 1)

            def scores(t, b):
                if b == 0:
                    pe.wait_ge(q_spread.sem, q_spread.now(t, 1))
                    pe.wait_ge(k_spread_a.sem, k_spread_a.now(t, 1))
                    pe.wait_ge(k_spread_v.sem, k_spread_v.now(t, 1))
                pe.wait_ge(shift_done.sem, shift_done.now(t, b - 1) if b >= 2 else shift_done.before(t, b + 3))
                if not cross:
                    pe.matmul(p_s[:, b % 2, :, :], ident_b[:, :], window[:, :, :], start=True, stop=False,
                              skip_group_check=True)
                for half in range(2):
                    last = pe.matmul(p_s[:, b % 2, 4 * half:4 * half + 4, :], spread_q[:, b, half, :, :],
                                     spread_k[:, b, :, :], start=cross, stop=True, skip_group_check=True)
                last.then_inc(scored.sem, 1)

            def turn_probs(t, b):
                pe.wait_ge(normed.sem, normed.now(t, b + 1))
                pe.wait_ge(probs_copied.sem, probs_copied.now(t, b - 1) if b >= 2 else probs_copied.before(t, b + 3))
                for g2 in range(2):
                    for j2 in range(2):
                        last = pe.transpose(p_pt[:, b % 2, j2, g2 * P:(g2 + 1) * P],
                                            probs_n[:, b, 4 * g2 + 2 * j2:4 * g2 + 2 * j2 + 2, :], W["ident"])
                last.then_inc(probs_turned.sem, 1)

            def weigh(t, b):
                pe.wait_ge(probs_copied.sem, probs_copied.now(t, b + 1))
                if b == 0:
                    pe.wait_ge(v_spread.sem, v_spread.now(t, 1))
                    pe.wait_ge(tail.added.sem, tail.added.before(t, 1))
                if b % 2 == 0:
                    for m in (mixed_a, mixed_v):
                        pe.wait_ge(m.sem, m.now(t, 1) if b else m.before(t, 2))
                for j2 in range(2):
                    last = pe.matmul(p_o[:, b % 2, :, :], spread_v[:, b, j2, :, :, :], probs_t[:, b, j2, :],
                                     start=(j2 == 0), stop=(j2 == 1))
                last.then_inc(weighted.sem, 1)

            def project(t):
                pe.wait_ge(mixed_a.sem, mixed_a.now(t, 2))
                pe.wait_ge(mixed_v.sem, mixed_v.now(t, 2))
                for j in range(NT):
                    last = pe.matmul(p_y[:, j, :], mixed[:, SPT * j:SPT * j + SPT, :], w_o, start=True, stop=True)
                last.then_inc(projected.sem, 1)

            def turn(t, one, two):
                turn_probs(t, 0)
                if one:
                    scores(t + 1, 1)
                turn_probs(t, 1)
                weigh(t, 0)
                if one:
                    scores(t + 1, 2)
                    values(t + 1)
                if two:
                    transposes(t + 2)
                turn_probs(t, 2)
                weigh(t, 1)
                if one:
                    scores(t + 1, 3)
                if two:
                    queries_keys(t + 2)
                turn_probs(t, 3)
                weigh(t, 2)
                weigh(t, 3)
                if two:
                    scores(t + 2, 0)
                project(t)

            transposes(0)
            queries_keys(0)
            for b in range(NB):
                scores(0, b)
            values(0)
            transposes(1)
            queries_keys(1)
            scores(1, 0)
            all_turns(pe, turn)

        @block.scalar
        def _(act):
            credit(act, feats_done, q_spread, k_spread_a, v_spread, exped, probs_copied, mixed_a)
            act.wait_ge(constants, CONSTANTS)

            def copy_feats(t):
                n = 2 if cross else 1
                act.wait_ge(turned.sem, turned.now(t, 1))
                act.wait_ge(v_done.sem, v_done.before(t, 1))
                nc.scalar.activation(feats[:, 0:n, :], p_t[:, 0:n, :], ACT.Copy).then_inc(feats_done.sem, 1)

            def spread(t):
                act.wait_ge(scored.sem, scored.before(t, NB))
                act.wait_ge(qk_done.sem, qk_done.now(t, 1))
                nc.scalar.activation(spread_k[:, :, 0, :], p_qk[:, 1, :].rearrange("p (b s) -> p b s", s=SEQ),
                                     ACT.Identity, bias=k_bias[:, 0:1], scale=W["head_mask"][:, 0:1])\
                    .then_inc(k_spread_a.sem, 1)
                for g in range(4):
                    r = slice(32 * g, 32 * g + 32)
                    last = nc.scalar.activation(spread_q[r, :, g // 2, g % 2, :],
                                                p_qk[r, 0, :].rearrange("p (b s) -> p b s", s=SEQ), ACT.Identity,
                                                bias=q_bias[r, :], scale=HD ** -0.5)
                last.then_inc(q_spread.sem, 1)

            def spread_values(t):
                act.wait_ge(v_done.sem, v_done.now(t, 1))
                act.wait_ge(weighted.sem, weighted.before(t, NB))
                for half in range(2):
                    r = slice(SEQ * half, SEQ * half + SEQ)
                    values = p_v[r, :, :].rearrange("p b (g j d) -> p b g j d", g=4, j=4)
                    for j2 in range(2):
                        last = nc.scalar.activation(spread_v[r, :, j2, :, 2 * j2 + half, :], values[:, :, :, 2 * j2 + half, :],
                                                    ACT.Copy)
                last.then_inc(v_spread.sem, 1)

            def exp(t, b):
                act.wait_ge(normed.sem, normed.before(t, b + 1))
                act.wait_ge(shift_done.sem, shift_done.now(t, b + 1))
                nc.scalar.activation(probs[:, b, :, :], shifted[:, b, :, :], ACT.Exp).then_inc(exped.sem, 1)

            def copy_probs(t, b):
                act.wait_ge(weighted.sem, weighted.before(t, b + 1))
                act.wait_ge(probs_turned.sem, probs_turned.now(t, b + 1))
                nc.scalar.activation(probs_t[:, b, :, :], p_pt[:, b % 2, :, :], ACT.Copy).then_inc(probs_copied.sem, 1)

            def copy_mixed(t, pair):
                act.wait_ge(projected.sem, projected.before(t, 1))
                act.wait_ge(weighted.sem, weighted.now(t, 2 * pair + 2))
                for g in range(2):
                    r = slice(32 * g, 32 * g + 32)
                    last = nc.scalar.activation(mixed[r, 2 * pair:2 * pair + 2, :], p_o[r, :, g, :], ACT.Identity,
                                                bias=(0.0 if cross else W["v_b"][r, :]))
                last.then_inc(mixed_a.sem, 1)

            def turn(t, one, two):
                copy_probs(t, 0)
                spread_values(t)
                if one:
                    exp(t + 1, 0)
                copy_probs(t, 1)
                if one:
                    exp(t + 1, 1)
                if two:
                    copy_feats(t + 2)
                copy_probs(t, 2)
                copy_mixed(t, 0)
                if one:
                    exp(t + 1, 2)
                if two:
                    spread(t + 2)
                copy_probs(t, 3)
                if one:
                    exp(t + 1, 3)
                copy_mixed(t, 1)

            copy_feats(0)
            spread(0)
            for b in range(NB):
                exp(0, b)
            copy_feats(1)
            spread(1)
            all_turns(act, turn)

        @block.vector
        def _(dve):
            if cross:
                nc.vector.memset(q_bias[:, :], 0.0).then_inc(constants, 1)
                nc.vector.memset(k_bias[:, :], 0.0).then_inc(constants, 1)
            else:
                nc.vector.tensor_scalar(q_bias[:, :], W["qk_b"][:, 0:1], HD ** -0.5, None, ALU.mult).then_inc(constants, 2)
                nc.vector.tensor_scalar(k_bias[:, :], W["head_mask"], W["qk_b"][:, 1:2], None, ALU.mult).then_inc(constants, 2)
            credit(dve, k_spread_v, maxed, shift_done, summed, inverted, mixed_v)
            tail.credit_vector(dve)
            dve.wait_ge(constants, CONSTANTS)

            def spread_keys(t):
                dve.wait_ge(scored.sem, scored.before(t, NB))
                dve.wait_ge(qk_done.sem, qk_done.now(t, 1))
                dve.wait_ge(k_spread_a.sem, k_spread_a.now(t, 1))
                dve.wait_ge(q_spread.sem, q_spread.now(t, 1))
                for j in range(1, 4):
                    last = nc.vector.tensor_scalar(spread_k[:, :, j, :], p_qk[:, 1, :].rearrange("p (b s) -> p b s", s=SEQ),
                                                   W["head_mask"][:, j:j + 1], k_bias[:, j:j + 1], ALU.mult, ALU.add)
                last.then_inc(k_spread_v.sem, 1)

            def shift(t, b):
                dve.wait_ge(scored.sem, scored.now(t, b + 1))
                nc.vector.tensor_reduce(neg_max[:, b, :], p_s[:, b % 2, :, :], AX_X, ALU.max, negate=True)\
                    .then_inc(maxed.sem, 1)
                dve.wait_ge(maxed.sem, maxed.now(t, b + 1))
                dve.wait_ge(exped.sem, exped.before(t, b + 1))
                nc.vector.tensor_tensor(shifted[:, b, :, :], p_s[:, b % 2, :, :],
                                        neg_max[:, b, :].unsqueeze(2).broadcast_to((P, 8, SEQ)), ALU.add)\
                    .then_inc(shift_done.sem, 1)

            def sum_up(t, b):
                dve.wait_ge(exped.sem, exped.now(t, b + 1))
                nc.vector.tensor_reduce(sums[:, b, :], probs[:, b, :, :], AX_X, ALU.add).then_inc(summed.sem, 1)
                dve.wait_ge(summed.sem, summed.now(t, b + 1))
                dve.wait_ge(normed.sem, normed.before(t, b + 1))
                nc.vector.reciprocal(rsum[:, b, :], sums[:, b, :]).then_inc(inverted.sem, 1)

            def copy_mixed(t, pair):
                dve.wait_ge(projected.sem, projected.before(t, 1))
                dve.wait_ge(weighted.sem, weighted.now(t, 2 * pair + 2))
                for g in (2, 3):
                    r = slice(32 * g, 32 * g + 32)
                    out, src = mixed[r, 2 * pair:2 * pair + 2, :], p_o[r, :, g, :]
                    if cross:
                        last = nc.vector.tensor_copy(out, src)
                    else:
                        last = nc.vector.tensor_scalar(out, src, W["v_b"][r, :], None, ALU.add)
                last.then_inc(mixed_v.sem, 1)

            def turn(t, one, two):
                if one:
                    shift(t + 1, 1)
                    sum_up(t + 1, 0)
                    shift(t + 1, 2)
                    sum_up(t + 1, 1)
                copy_mixed(t, 0)
                if one:
                    shift(t + 1, 3)
                if two:
                    spread_keys(t + 2)
                if one:
                    sum_up(t + 1, 2)
                copy_mixed(t, 1)
                if two:
                    shift(t + 2, 0)
                dve.wait_ge(residual_done.sem, residual_done.now(t, 1))
                dve.wait_ge(projected.sem, projected.now(t, 1))
                tail.moments_vector(dve, t, p_y[:, :, :], residual[:, :, :])
                if one:
                    sum_up(t + 1, 3)
                tail.write_vector(dve, t, lambda j: X[:, bass.ds(t * NT + j, 1), :])

            spread_keys(0)
            shift(0, 0)
            for b in range(1, NB):
                shift(0, b)
                sum_up(0, b - 1)
            sum_up(0, NB - 1)
            spread_keys(1)
            shift(1, 0)
            all_turns(dve, turn)
def stage_soft_mixture(nc, X, W):
    C = SLOTS // P
    NH = C * SPT
    RING = 4
    TURNS = TILES
    ROOT = float(D) ** 0.5
    with ExitStack() as ctx:
        def sb(n, shape, dt=F32):
            return ctx.enter_context(nc.sbuf_tensor("sm_" + n, shape, dt))

        def ps(n, shape):
            return ctx.enter_context(nc.psum_tensor("sm_" + n, shape, F32))

        def sig(n, per=1):
            return Signal(ctx, nc, "sm_" + n, per)

        slots_t = sb("slots_t", [P, SLOTS])
        slot_sq = sb("slot_sq", [P, 2, C])
        slot_rn = sb("slot_rn", [P, C])
        slots_n = sb("slots_n", [P, C, D])
        gain_x = sb("gain_x", [P, 1])
        gain_s = sb("gain_s", [P, 1])
        squares = sb("squares", [P, D])
        ssq = sb("ssq", [P, 1])
        floor_ssq = sb("floor_ssq", [P, 1])
        rnorm = sb("rnorm", [P, 1])
        x_scaled = sb("x_scaled", [P, D])
        x_t = sb("x_t", [P, P])
        xw = sb("xw", [P, HIDDEN])
        neg_max = sb("neg_max", [P, 1 + NH])
        shifted = sb("shifted", [P, 2, SLOTS])
        exps = sb("exps", [P, 2, SLOTS])
        sums = sb("sums", [P, 1 + NH])
        rsums = sb("rsums", [P, 1 + NH])
        combine_t = sb("combine_t", [P, C, P])
        dispatch = sb("dispatch", [P, SLOTS])
        hidden = sb("hidden", [P, RING, HIDDEN])
        gathered = sb("gathered", [P, HIDDEN])
        gathered_t = sb("gathered_t", [P, C, P])
        residual = sb("residual", [P, 1, D])
        p_x = ps("p_x", [P, 4, P])
        p_l = ps("p_l", [P, SLOTS])
        p_lt = ps("p_lt", [P, C, P])
        p_tr = ps("p_tr", [P, C, P])
        p_xw = ps("p_xw", [P, HIDDEN])
        p_h = ps("p_h", [P, 2, HIDDEN])
        p_g = ps("p_g", [P, HIDDEN])

        tail = NormTail(ctx, nc, "sm_tail", 1)
        prep = nc.alloc_semaphore("sm_prep")
        prep_v = nc.alloc_semaphore("sm_prep_v")
        squared = sig("squared")
        floored = sig("floored")
        rooted = sig("rooted")
        scaled = sig("scaled")
        x_turned = sig("x_turned")
        x_ready = sig("x_ready")
        xw_done = sig("xw_done")
        xw_ready = sig("xw_ready")
        logits_done = sig("logits_done")
        logits_t_done = sig("logits_t_done")
        maxed = sig("maxed", 2)
        shift_done = sig("shift_done", 2)
        exped = sig("exped")
        summed = sig("summed", 2)
        inverted = sig("inverted")
        exps_turned = sig("exps_turned", 2)
        combine_ready = sig("combine_ready")
        dispatch_ready = sig("dispatch_ready")
        h_done = sig("h_done", NH)
        gelu_done = sig("gelu_done", NH)
        mixed = sig("mixed", NH)
        gathered_ready = sig("gathered_ready")
        gathered_turned = sig("gathered_turned")
        gathered_t_ready = sig("gathered_t_ready")
        y_done = sig("y_done")
        residual_done = sig("residual_done")

        block = ctx.enter_context(nc.Block())

        def tile(t):
            return X[:, bass.ds(t, 1), :]

        def all_turns(engine, turn):
            with engine.Fori(0, TURNS - 2) as t:
                turn(t, True, True)
            turn(TURNS - 2, True, False)
            turn(TURNS - 1, False, False)

        @block.gpsimd
        def _(pool):
            credit(pool, rooted, residual_done)
            tail.credit_pool(pool)
            pool.wait_ge(prep_v, 1)
            nc.gpsimd.tensor_tensor(slot_rn[:, :], slot_sq[:, 1, :], W["minus_half"][:, 0:C], ALU.pow).then_inc(prep, 1)

            def root(t):
                pool.wait_ge(scaled.sem, scaled.before(t, 1))
                pool.wait_ge(floored.sem, floored.now(t, 1))
                nc.gpsimd.tensor_tensor(rnorm[:, :], floor_ssq[:, :], W["minus_half"][:, 0:1], ALU.pow)\
                    .then_inc(rooted.sem, 1)

            def turn(t, one, two):
                pool.wait_ge(tail.added.sem, tail.added.before(t, 1))
                if two:
                    root(t + 2)
                nc.gpsimd.tensor_copy(residual[:, :, :], tile(t)).then_inc(residual_done.sem, 1)
                tail.root_pool(pool, t, W["minus_half"])

            root(0)
            root(1)
            all_turns(pool, turn)

        @block.scalar
        def _(act):
            credit(act, squared, x_ready, exped, dispatch_ready, gelu_done, gathered_t_ready)
            for c in range(C):
                last = nc.scalar.activation(slots_n[:, c, :], W["slots"][:, c, :], ACT.Square,
                                            accum_out=slot_sq[:, 0, c:c + 1])
            last.then_inc(prep, 1)
            act.wait_ge(prep, 3)
            act.wait_ge(prep_v, 4)
            nc.scalar.activation(slots_t[:, :], p_l[:, :], ACT.Copy, scale=gain_s[:, :]).then_inc(prep, 1)

            def square(t):
                act.wait_ge(floored.sem, floored.before(t, 1))
                nc.scalar.activation(squares[:, :].unsqueeze(1), tile(t), ACT.Square, accum_out=ssq[:, :])\
                    .then_inc(squared.sem, 1)

            def x_copy(t):
                act.wait_ge(x_turned.sem, x_turned.now(t, 1))
                act.wait_ge(xw_done.sem, xw_done.before(t, 1))
                act.wait_ge(logits_t_done.sem, logits_t_done.before(t, 1))
                nc.scalar.activation(x_t[:, :], p_x[:, 0, :], ACT.Copy, scale=gain_x[:, :]).then_inc(x_ready.sem, 1)

            def exp(t):
                act.wait_ge(exps_turned.sem, exps_turned.before(t, 2))
                act.wait_ge(inverted.sem, inverted.before(t, 1))
                act.wait_ge(shift_done.sem, shift_done.now(t, 2))
                nc.scalar.activation(exps[:, :, :], shifted[:, :, :], ACT.Exp).then_inc(exped.sem, 1)

            def dispatch_copy(t):
                act.wait_ge(exps_turned.sem, exps_turned.now(t, 2))
                act.wait_ge(h_done.sem, h_done.before(t, NH))
                nc.scalar.activation(dispatch[:, :], p_h[:, 1, :], ACT.Copy).then_inc(dispatch_ready.sem, 1)

            def gelu(t, i):
                if i == 0:
                    act.wait_ge(inverted.sem, inverted.now(t, 1))
                act.wait_ge(mixed.sem, mixed.now(t, i - RING + 1) if i >= RING else mixed.before(t, NH - RING + i + 1))
                act.wait_ge(h_done.sem, h_done.now(t, i + 1))
                nc.scalar.activation(hidden[:, i % RING, :], p_h[:, i % 2, :], ACT.Gelu, scale=rsums[:, 1 + i:2 + i])\
                    .then_inc(gelu_done.sem, 1)

            def turn(t, one, two):
                if two:
                    square(t + 2)
                for i in range(NH):
                    gelu(t, i)
                    if i == NH // 2 - 1 and two:
                        x_copy(t + 2)
                if one:
                    exp(t + 1)
                act.wait_ge(y_done.sem, y_done.before(t, 1))
                act.wait_ge(gathered_turned.sem, gathered_turned.now(t, 1))
                nc.scalar.activation(gathered_t[:, :, :], p_tr[:, :, :], ACT.Copy).then_inc(gathered_t_ready.sem, 1)
                if one:
                    dispatch_copy(t + 1)

            square(0)
            x_copy(0)
            square(1)
            exp(0)
            x_copy(1)
            dispatch_copy(0)
            all_turns(act, turn)

        @block.tensor
        def _(pe):
            credit(pe, x_turned, xw_done, logits_done, logits_t_done, exps_turned, h_done, mixed, gathered_turned, y_done)
            pe.wait_ge(prep_v, 3)
            for c in range(C):
                last = pe.transpose(p_l[:, c * P:(c + 1) * P], slots_n[:, c, :], W["ident"])
            last.then_inc(prep, 1)
            pe.wait_ge(prep, 4)

            def x_transpose(t):
                pe.wait_ge(scaled.sem, scaled.now(t, 1))
                pe.wait_ge(x_ready.sem, x_ready.before(t, 1))
                pe.transpose(p_x[:, 0, :], x_scaled[:, :], W["ident"]).then_inc(x_turned.sem, 1)

            def times_w1(t):
                pe.wait_ge(x_ready.sem, x_ready.now(t, 1))
                pe.wait_ge(xw_ready.sem, xw_ready.before(t, 1))
                pe.matmul(p_xw[:, :], x_t[:, :], W["moe_w1"], start=True, stop=True).then_inc(xw_done.sem, 1)

            def logits(t):
                pe.wait_ge(x_ready.sem, x_ready.now(t, 1))
                pe.wait_ge(shift_done.sem, shift_done.before(t, 2))
                pe.matmul(p_l[:, :], x_t[:, :], slots_t[:, :], start=True, stop=True).then_inc(logits_done.sem, 1)
                for c in range(C):
                    last = pe.matmul(p_lt[:, c, :], slots_t[:, c * P:(c + 1) * P], x_t[:, :], start=True, stop=True)
                last.then_inc(logits_t_done.sem, 1)

            def exps_transpose(t):
                pe.wait_ge(gelu_done.sem, gelu_done.before(t, NH))
                pe.wait_ge(exped.sem, exped.now(t, 1))
                for k in range(2):
                    for c in range(C):
                        last = pe.transpose(p_h[:, k, c * P:(c + 1) * P], exps[:, k, c * P:(c + 1) * P], W["ident"])
                    last.then_inc(exps_turned.sem, 1)

            def hidden_block(t, i):
                c, b = i // SPT, i % SPT
                r = slice(SEQ * b, SEQ * b + SEQ)
                if i == 0:
                    pe.wait_ge(xw_ready.sem, xw_ready.now(t, 1))
                    pe.wait_ge(combine_ready.sem, combine_ready.now(t, 1))
                    pe.wait_ge(dispatch_ready.sem, dispatch_ready.now(t, 1))
                if i >= 2:
                    pe.wait_ge(gelu_done.sem, gelu_done.now(t, i - 1))
                pe.matmul(p_h[:, i % 2, :], dispatch[r, c * P:(c + 1) * P], xw[r, :], start=True, stop=True)\
                    .then_inc(h_done.sem, 1)

            def gather_block(t, i):
                c, b = i // SPT, i % SPT
                r = slice(SEQ * b, SEQ * b + SEQ)
                if i == 0:
                    pe.wait_ge(gathered_ready.sem, gathered_ready.before(t, 1))
                pe.wait_ge(gelu_done.sem, gelu_done.now(t, i + 1))
                pe.matmul(p_g[r, :], combine_t[:, c, r], hidden[:, i % RING, :], start=(c == 0), stop=(c == C - 1))\
                    .then_inc(mixed.sem, 1)

            def turn(t, one, two):
                if one:
                    times_w1(t + 1)
                for c in range(C + 1):
                    if c < C:
                        hidden_block(t, 2 * c)
                        hidden_block(t, 2 * c + 1)
                    if c == C // 2 and two:
                        x_transpose(t + 2)
                    if c >= 1:
                        gather_block(t, 2 * c - 2)
                        gather_block(t, 2 * c - 1)
                if two:
                    logits(t + 2)
                pe.wait_ge(gathered_t_ready.sem, gathered_t_ready.before(t, 1))
                pe.wait_ge(gathered_ready.sem, gathered_ready.now(t, 1))
                for c in range(C):
                    last = pe.transpose(p_tr[:, c, :], gathered[:, c * P:(c + 1) * P], W["ident"])
                last.then_inc(gathered_turned.sem, 1)
                if one:
                    exps_transpose(t + 1)
                pe.wait_ge(tail.added.sem, tail.added.before(t, 1))
                pe.wait_ge(gathered_t_ready.sem, gathered_t_ready.now(t, 1))
                for c in range(C):
                    last = pe.matmul(p_x[:, 1, :], gathered_t[:, c, :], W["moe_w2"][:, c, :], start=(c == 0),
                                     stop=(c == C - 1))
                last.then_inc(y_done.sem, 1)

            x_transpose(0)
            times_w1(0)
            logits(0)
            x_transpose(1)
            exps_transpose(0)
            logits(1)
            all_turns(pe, turn)

        @block.vector
        def _(dve):
            credit(dve, floored, scaled, xw_ready, maxed, shift_done, summed, inverted, combine_ready, gathered_ready)
            tail.credit_vector(dve)
            dve.wait_ge(prep, 1)
            nc.vector.tensor_scalar(slot_sq[:, 1, :], slot_sq[:, 0, :], NORM_FLOOR, None, ALU.max).then_inc(prep_v, 1)
            dve.wait_ge(prep, 2)
            for c in range(C):
                last = nc.vector.tensor_scalar(slots_n[:, c, :], W["slots"][:, c, :], slot_rn[:, c:c + 1], None, ALU.mult)
            last.then_inc(prep_v, 2)
            nc.vector.tensor_scalar(gain_x[:, :], W["gamma_x"], ROOT, None, ALU.mult)
            nc.vector.tensor_scalar(gain_s[:, :], W["gamma_slot"], ROOT, None, ALU.mult).then_inc(prep_v, 1)

            def scale_row(t):
                dve.wait_ge(squared.sem, squared.now(t, 1))
                dve.wait_ge(rooted.sem, rooted.before(t, 1))
                nc.vector.tensor_scalar(floor_ssq[:, :], ssq[:, :], NORM_FLOOR, None, ALU.max).then_inc(floored.sem, 1)
                dve.wait_ge(x_turned.sem, x_turned.before(t, 1))
                dve.wait_ge(rooted.sem, rooted.now(t, 1))
                nc.vector.tensor_scalar(x_scaled[:, :].unsqueeze(1), tile(t), rnorm[:, :], None, ALU.mult)\
                    .then_inc(scaled.sem, 1)

            def xw_copy(t):
                dve.wait_ge(h_done.sem, h_done.before(t, NH))
                dve.wait_ge(xw_done.sem, xw_done.now(t, 1))
                nc.vector.tensor_copy(xw[:, :], p_xw[:, :]).then_inc(xw_ready.sem, 1)

            def shift(t):
                dve.wait_ge(exped.sem, exped.before(t, 1))
                dve.wait_ge(logits_done.sem, logits_done.now(t, 1))
                nc.vector.tensor_reduce(neg_max[:, 0:1], p_l[:, :], AX_X, ALU.max, negate=True).then_inc(maxed.sem, 1)
                dve.wait_ge(maxed.sem, maxed.now(t, 1))
                nc.vector.tensor_scalar(shifted[:, 0, :], p_l[:, :], neg_max[:, 0:1], None, ALU.add)\
                    .then_inc(shift_done.sem, 1)
                logits_t = p_lt[:, :, :].rearrange("p c (b s) -> p (c b) s", s=SEQ)
                dve.wait_ge(logits_t_done.sem, logits_t_done.now(t, 1))
                nc.vector.tensor_reduce(neg_max[:, 1:], logits_t, AX_X, ALU.max, negate=True).then_inc(maxed.sem, 1)
                dve.wait_ge(maxed.sem, maxed.now(t, 2))
                nc.vector.tensor_tensor(shifted[:, 1, :].rearrange("p (c s) -> p c s", s=SEQ), logits_t,
                                        neg_max[:, 1:].unsqueeze(2).broadcast_to((P, NH, SEQ)), ALU.add)\
                    .then_inc(shift_done.sem, 1)

            def sum_up(t):
                dve.wait_ge(inverted.sem, inverted.before(t, 1))
                dve.wait_ge(exped.sem, exped.now(t, 1))
                nc.vector.tensor_reduce(sums[:, 0:1], exps[:, 0, :], AX_X, ALU.add).then_inc(summed.sem, 1)
                nc.vector.tensor_reduce(sums[:, 1:], exps[:, 1, :].rearrange("p (c s) -> p c s", s=SEQ), AX_X, ALU.add)\
                    .then_inc(summed.sem, 1)
                dve.wait_ge(gelu_done.sem, gelu_done.before(t, NH))
                dve.wait_ge(gathered_ready.sem, gathered_ready.before(t, 1))
                dve.wait_ge(summed.sem, summed.now(t, 2))
                nc.vector.reciprocal(rsums[:, :], sums[:, :]).then_inc(inverted.sem, 1)

            def combine_copy(t):
                dve.wait_ge(mixed.sem, mixed.before(t, NH))
                dve.wait_ge(exps_turned.sem, exps_turned.now(t, 1))
                nc.vector.tensor_copy(combine_t[:, :, :], p_h[:, 0, :].rearrange("p (c s) -> p c s", s=P))\
                    .then_inc(combine_ready.sem, 1)

            def turn(t, one, two):
                if two:
                    scale_row(t + 2)
                dve.wait_ge(gathered_turned.sem, gathered_turned.before(t, 1))
                dve.wait_ge(mixed.sem, mixed.now(t, NH))
                nc.vector.tensor_scalar(gathered[:, :], p_g[:, :], rsums[:, 0:1], None, ALU.mult)\
                    .then_inc(gathered_ready.sem, 1)
                if one:
                    xw_copy(t + 1)
                    sum_up(t + 1)
                    combine_copy(t + 1)
                if two:
                    shift(t + 2)
                dve.wait_ge(residual_done.sem, residual_done.now(t, 1))
                dve.wait_ge(y_done.sem, y_done.now(t, 1))
                tail.moments_vector(dve, t, p_x[:, 1:2, :], residual[:, :, :])
                tail.write_vector(dve, t, lambda j: tile(t))

            scale_row(0)
            scale_row(1)
            xw_copy(0)
            shift(0)
            sum_up(0)
            combine_copy(0)
            shift(1)
            all_turns(dve, turn)
def stage_cross(nc, X, W, ctx_in, mask):
    NT = 2
    NB = NT * SPT
    TURNS = TILES // NT
    XHEADS, XHD = 2, 64
    SOURCES = 2
    MASKED = -float(np.finfo(np.float32).max)
    with ExitStack() as ctx:
        def sb(n, shape, dt=F32):
            return ctx.enter_context(nc.sbuf_tensor("cr_" + n, shape, dt))

        def ps(n, shape):
            return ctx.enter_context(nc.psum_tensor("cr_" + n, shape, F32))

        def sig(n, per=1):
            return Signal(ctx, nc, "cr_" + n, per)

        c_in = sb("c_in", [P, NT, D])
        masks = sb("masks", [P, BATCH, SEQ], U8)
        q_gain = sb("q_gain", [P, 1])
        stats = sb("stats", [P, NT, SOURCES, 6])
        moments = sb("moments", [P, NT, SOURCES, 2])
        var_eps = sb("var_eps", [P, NT, SOURCES])
        rstd = sb("rstd", [P, NT, SOURCES])
        scrap = sb("scrap", [P, 1])
        normed = sb("normed", [P, NT, SOURCES, D])
        feats = sb("feats", [P, SOURCES, NT, P])
        squares = sb("squares", [P, NT, 3, D])
        ssq = sb("ssq", [P, NT * 3 * XHEADS])
        floor_ssq = sb("floor_ssq", [P, NT * 3 * XHEADS])
        rnorm = sb("rnorm", [P, NT * 3 * XHEADS])
        scaled = sb("scaled", [P, NT, 3, D])
        spread_q = sb("spread_q", [P, NB, XHEADS, SEQ])
        keys = sb("keys", [P, NB, 2, SEQ])
        values = sb("values", [P, NB, D])
        neg_max = sb("neg_max", [P, NB])
        probs = sb("probs", [P, NB, P])
        sums = sb("sums", [P, NB])
        rsum = sb("rsum", [P, NB])
        probs_n = sb("probs_n", [P, NB, P])
        probs_t = sb("probs_t", [P, NB, P])
        mixed = sb("mixed", [P, NB, SEQ])
        residual = sb("residual", [P, NT, D])
        p_t = ps("p_t", [P, SOURCES * NT, P])
        p_kv = ps("p_kv", [P, NT, SOURCES, 2 * D])
        p_qy = ps("p_qy", [P, 2, NT, D])
        p_k = ps("p_k", [P, SOURCES, NT, P])
        p_s = ps("p_s", [P, NB, P])
        p_pt = ps("p_pt", [P, NB, P])
        p_o = ps("p_o", [P, NB, XHEADS, SEQ])

        tail = NormTail(ctx, nc, "cr_tail", NT)
        constants = nc.alloc_semaphore("cr_constants")
        mask_in = nc.alloc_semaphore("cr_mask_in")
        mask_ready = nc.alloc_semaphore("cr_mask_ready")
        c_landed = sig("c_landed", 16)
        counted, aggregated, floored, rooted = sig("counted"), sig("aggregated"), sig("floored"), sig("rooted")
        normed_done = sig("normed_done")
        turned = sig("turned")
        feats_done = sig("feats_done")
        qkv_done = sig("qkv_done")
        squared = sig("squared")
        summed_sq = sig("summed_sq")
        floored_sq = sig("floored_sq")
        rooted_sq = sig("rooted_sq")
        scale_done = sig("scale_done")
        qk_turned = sig("qk_turned")
        qk_ready = sig("qk_ready")
        values_ready = sig("values_ready")
        scored = sig("scored")
        masked = sig("masked")
        maxed = sig("maxed")
        exped = sig("exped")
        inverted = sig("inverted")
        probs_normed = sig("probs_normed")
        probs_turned = sig("probs_turned")
        probs_ready = sig("probs_ready")
        weighted = sig("weighted")
        mixed_ready = sig("mixed_ready")
        projected = sig("projected")
        residual_done = sig("residual_done")

        block = ctx.enter_context(nc.Block())

        def tiles(t):
            return X[:, bass.ds(t * NT, NT), :]

        def all_turns(engine, turn):
            with engine.Fori(0, TURNS - 2) as t:
                turn(t, True, True)
            turn(TURNS - 2, True, False)
            turn(TURNS - 1, False, False)

        @block.sync
        def _(sp):
            sp.dma_start(masks[:, :, :], mask.rearrange("b s -> (b s)").partition_broadcast(P)).then_inc(mask_in, 16)
            sp.dma_start(c_in[:, :, :], ctx_in[0:NT * P, :].rearrange("(j p) d -> p j d", p=P)).then_inc(c_landed.sem, 16)
            with sp.Fori(1, TURNS) as t:
                sp.wait_ge(normed_done.sem, normed_done.before(t, 1))
                sp.dma_start(c_in[:, :, :], ctx_in[bass.ds(t * (NT * P), NT * P), :].rearrange("(j p) d -> p j d", p=P))\
                    .then_inc(c_landed.sem, 16)
            sp.wait_ge(c_landed.sem, 16 * TURNS)
            sp.wait_ge(mask_in, 16)

        @block.gpsimd
        def _(pool):
            nc.gpsimd.memset(spread_q[:, :, :, :], 0.0).then_inc(constants, 1)
            credit(pool, rooted, rooted_sq, probs_normed, residual_done)
            tail.credit_pool(pool)

            pool.wait_ge(mask_in, 16)
            nc.gpsimd.tensor_scalar(masks[:, :, :], masks[:, :, :], -1.0, 1.0, ALU.mult, ALU.add).then_inc(mask_ready, 1)

            def root(t):
                pool.wait_ge(normed_done.sem, normed_done.before(t, 1))
                pool.wait_ge(floored.sem, floored.now(t, 1))
                nc.gpsimd.tensor_tensor(rstd[:, :, :], var_eps[:, :, :],
                                        W["minus_half"][:, 0:4].rearrange("p (a b) -> p a b", a=NT), ALU.pow)\
                    .then_inc(rooted.sem, 1)

            def root_sq(t):
                pool.wait_ge(scale_done.sem, scale_done.before(t, 1))
                pool.wait_ge(floored_sq.sem, floored_sq.now(t, 1))
                nc.gpsimd.tensor_tensor(rnorm[:, :], floor_ssq[:, :], W["minus_half"][:, 0:12], ALU.pow)\
                    .then_inc(rooted_sq.sem, 1)

            def turn(t, one, two):
                pool.wait_ge(tail.added.sem, tail.added.before(t, 1))
                pool.wait_ge(probs_turned.sem, probs_turned.before(t, 1))
                pool.wait_ge(inverted.sem, inverted.now(t, 1))
                nc.gpsimd.tensor_tensor(probs_n[:, :, :], probs[:, :, :],
                                        rsum[:, :].unsqueeze(2).broadcast_to((P, NB, P)), ALU.mult)\
                    .then_inc(probs_normed.sem, 1)
                nc.gpsimd.tensor_tensor(residual[:, :, :], tiles(t), W["xout_b"].unsqueeze(1).broadcast_to((P, NT, D)),
                                        ALU.add).then_inc(residual_done.sem, 1)
                if one:
                    root_sq(t + 1)
                if two:
                    root(t + 2)
                tail.root_pool(pool, t, W["minus_half"])

            root(0)
            root_sq(0)
            root(1)
            all_turns(pool, turn)

        @block.tensor
        def _(pe):
            credit(pe, turned, qkv_done, qk_turned, scored, probs_turned, weighted, projected)
            pe.wait_ge(constants, 2)

            def transposes(t):
                pe.wait_ge(normed_done.sem, normed_done.now(t, 1))
                pe.wait_ge(qk_ready.sem, qk_ready.before(t, 1))
                for j in range(NT):
                    for s in range(SOURCES):
                        last = pe.transpose(p_t[:, s * NT + j, :], normed[:, j, s, :], W["ident"])
                last.then_inc(turned.sem, 1)

            def projections(t):
                pe.wait_ge(feats_done.sem, feats_done.now(t, 1))
                pe.wait_ge(scale_done.sem, scale_done.before(t, 1))
                pe.wait_ge(values_ready.sem, values_ready.before(t, 1))
                if not (isinstance(t, int) and t == 0):
                    pe.wait_ge(tail.added.sem, tail.added.before(t - 1, 1))
                for j in range(NT):
                    pe.matmul(p_qy[:, 0, j, :], feats[:, 1, j, :], W["XWq"], start=True, stop=True)
                    for s in range(SOURCES):
                        last = pe.matmul(p_kv[:, j, s, :], feats[:, s, j, :], W["XWkv"], start=True, stop=True)
                last.then_inc(qkv_done.sem, 1)

            def qk_transposes(t):
                pe.wait_ge(scale_done.sem, scale_done.now(t, 1))
                pe.wait_ge(feats_done.sem, feats_done.now(t, 1))
                for j in range(NT):
                    pe.transpose(p_t[:, j, :], scaled[:, j, 0, :], W["ident"])
                    for s in range(SOURCES):
                        last = pe.transpose(p_k[:, s, j, :], scaled[:, j, 1 + s, :], W["ident"])
                last.then_inc(qk_turned.sem, 1)

            def scores(t):
                pe.wait_ge(qk_ready.sem, qk_ready.now(t, 1))
                pe.wait_ge(exped.sem, exped.before(t, 1))
                for b in range(NB):
                    last = pe.matmul(p_s[:, b, :], spread_q[:, b, :, :], keys[:, b, :, :], start=True, stop=True)
                last.then_inc(scored.sem, 1)

            def weigh(t):
                pe.wait_ge(probs_ready.sem, probs_ready.before(t, 1))
                pe.wait_ge(probs_normed.sem, probs_normed.now(t, 1))
                for b in range(NB):
                    last = pe.transpose(p_pt[:, b, :], probs_n[:, b, :], W["ident"])
                last.then_inc(probs_turned.sem, 1)

            def mix(t):
                pe.wait_ge(values_ready.sem, values_ready.now(t, 1))
                pe.wait_ge(mixed_ready.sem, mixed_ready.before(t, 1))
                pe.wait_ge(probs_ready.sem, probs_ready.now(t, 1))
                for b in range(NB):
                    last = pe.matmul(p_o[:, b, :, :], values[:, b, :], probs_t[:, b, :], start=True, stop=True)
                last.then_inc(weighted.sem, 1)

            def project(t, one):
                if one:
                    pe.wait_ge(scale_done.sem, scale_done.now(t + 1, 1))
                pe.wait_ge(mixed_ready.sem, mixed_ready.now(t, 1))
                for j in range(NT):
                    last = pe.matmul(p_qy[:, 1, j, :], mixed[:, SPT * j:SPT * j + SPT, :], W["XWout"], start=True, stop=True)
                last.then_inc(projected.sem, 1)

            def turn(t, one, two):
                scores(t)
                if one:
                    transposes(t + 1)
                    projections(t + 1)
                weigh(t)
                mix(t)
                if one:
                    qk_transposes(t + 1)
                project(t, one)

            transposes(0)
            projections(0)
            qk_transposes(0)
            all_turns(pe, turn)

        @block.scalar
        def _(act):
            credit(act, feats_done, squared, qk_ready, exped, probs_ready)
            act.wait_ge(constants, 2)

            def to_features(t):
                act.wait_ge(turned.sem, turned.now(t, 1))
                act.wait_ge(qkv_done.sem, qkv_done.before(t, 1))
                for s, n in ((0, "lnx"), (1, "lnl")):
                    last = nc.scalar.activation(feats[:, s, :, :], p_t[:, s * NT:s * NT + NT, :], ACT.Identity,
                                                bias=W[n + "_b"], scale=W[n + "_g"])
                last.then_inc(feats_done.sem, 1)

            def square(t):
                act.wait_ge(summed_sq.sem, summed_sq.before(t, 1))
                act.wait_ge(qkv_done.sem, qkv_done.now(t, 1))
                nc.scalar.activation(squares[:, :, 0, :], p_qy[:, 0, :, :], ACT.Square)
                for j in range(NT):
                    last = nc.scalar.activation(squares[:, j, 1:3, :], p_kv[:, j, :, 0:D], ACT.Square)
                last.then_inc(squared.sem, 1)

            def spread(t):
                act.wait_ge(scored.sem, scored.before(t, 1))
                act.wait_ge(qk_turned.sem, qk_turned.now(t, 1))
                for h in range(XHEADS):
                    r = slice(XHD * h, XHD * h + XHD)
                    nc.scalar.activation(spread_q[r, :, h, :], p_t[r, 0:NT, :].rearrange("p j (b s) -> p (j b) s", s=SEQ),
                                         ACT.Copy, scale=q_gain[r, :])
                for b in range(SPT):
                    for s in range(SOURCES):
                        out = keys[:, :, s ^ b, :].rearrange("p (j b) s -> p j b s", b=SPT)[:, :, b, :]
                        last = nc.scalar.activation(out, p_k[:, s, :, SEQ * b:SEQ * b + SEQ], ACT.Copy, scale=W["k_gamma"])
                last.then_inc(qk_ready.sem, 1)

            def turn(t, one, two):
                if one:
                    to_features(t + 1)
                act.wait_ge(probs_normed.sem, probs_normed.before(t, 1))
                act.wait_ge(inverted.sem, inverted.before(t, 1))
                act.wait_ge(maxed.sem, maxed.now(t, 1))
                for b in range(NB):
                    last = nc.scalar.activation(probs[:, b, :], p_s[:, b, :], ACT.Exp, bias=neg_max[:, b:b + 1],
                                                accum_out=sums[:, b:b + 1])
                last.then_inc(exped.sem, 1)
                if one:
                    square(t + 1)
                act.wait_ge(weighted.sem, weighted.before(t, 1))
                act.wait_ge(probs_turned.sem, probs_turned.now(t, 1))
                nc.scalar.activation(probs_t[:, :, :], p_pt[:, :, :], ACT.Copy).then_inc(probs_ready.sem, 1)
                if one:
                    spread(t + 1)

            to_features(0)
            square(0)
            spread(0)
            all_turns(act, turn)

        @block.vector
        def _(dve):
            nc.vector.tensor_scalar(q_gain[:, :], W["q_gamma"], XHD ** -0.5, None, ALU.mult).then_inc(constants, 1)
            credit(dve, counted, aggregated, floored, normed_done, summed_sq, floored_sq, scale_done, values_ready, masked,
                   maxed, inverted, mixed_ready)
            tail.credit_vector(dve)

            def norm_inputs(t):
                dve.wait_ge(aggregated.sem, aggregated.before(t, 1))
                dve.wait_ge(c_landed.sem, (t + 1) * 16)
                for j in range(NT):
                    nc.vector.bn_stats(stats[:, j, 0, :], c_in[:, j, :])
                    last = nc.vector.bn_stats(stats[:, j, 1, :], X[:, bass.ds(t * NT + j, 1), :])
                last.then_inc(counted.sem, 1)
                dve.wait_ge(counted.sem, counted.now(t, 1))
                nc.vector.memset(scrap[:, :], 0.0)
                for j in range(NT):
                    for s in range(SOURCES):
                        last = nc.vector.bn_aggr(moments[:, j, s, :], stats[:, j, s, :])
                last.then_inc(aggregated.sem, 1)
                dve.wait_ge(aggregated.sem, aggregated.now(t, 1))
                nc.vector.tensor_scalar(var_eps[:, :, :], moments[:, :, :, 1], LN_EPS, None, ALU.add).then_inc(floored.sem, 1)

            def write_inputs(t):
                dve.wait_ge(turned.sem, turned.before(t, 1))
                dve.wait_ge(rooted.sem, rooted.now(t, 1))
                for j in range(NT):
                    for s, src in ((0, c_in[:, j, :].unsqueeze(1)), (1, X[:, bass.ds(t * NT + j, 1), :])):
                        last = nc.vector.tensor_scalar(normed[:, j, s, :].unsqueeze(1), src, moments[:, j, s, 0:1],
                                                       rstd[:, j, s:s + 1], ALU.subtract, ALU.mult)
                last.then_inc(normed_done.sem, 1)

            def head_norms(t):
                dve.wait_ge(squared.sem, squared.now(t, 1))
                dve.wait_ge(floored_sq.sem, floored_sq.before(t, 1))
                nc.vector.tensor_reduce(ssq[:, :], squares[:, :, :, :].rearrange("p j k (h d) -> p (j k h) d", d=XHD),
                                        AX_X, ALU.add).then_inc(summed_sq.sem, 1)
                dve.wait_ge(summed_sq.sem, summed_sq.now(t, 1))
                dve.wait_ge(rooted_sq.sem, rooted_sq.before(t, 1))
                nc.vector.tensor_scalar(floor_ssq[:, :], ssq[:, :], 1.0 / XHD, 1e-16, ALU.mult, ALU.max)\
                    .then_inc(floored_sq.sem, 1)

            def scale_heads(t):
                dve.wait_ge(qk_turned.sem, qk_turned.before(t, 1))
                dve.wait_ge(rooted_sq.sem, rooted_sq.now(t, 1))
                for j in range(NT):
                    a = j * 3 * XHEADS
                    nc.vector.tensor_tensor(scaled[:, j, 0, :].rearrange("p (h d) -> p h d", d=XHD),
                                            p_qy[:, 0, j, :].rearrange("p (h d) -> p h d", d=XHD),
                                            rnorm[:, a:a + 2].unsqueeze(2).broadcast_to((P, 2, XHD)), ALU.mult)
                    last = nc.vector.tensor_tensor(scaled[:, j, 1:3, :].rearrange("p k (h d) -> p k h d", d=XHD),
                                                   p_kv[:, j, :, 0:D].rearrange("p k (h d) -> p k h d", d=XHD),
                                                   rnorm[:, a + 2:a + 6].rearrange("p (k h) -> p k h", h=2).unsqueeze(3)
                                                   .broadcast_to((P, 2, 2, XHD)), ALU.mult)
                last.then_inc(scale_done.sem, 1)

            def place_values(t):
                dve.wait_ge(weighted.sem, weighted.before(t, 1))
                for b in range(SPT):
                    for s in range(SOURCES):
                        src = p_kv[SEQ * b:SEQ * b + SEQ, :, s, D:]
                        to = SEQ * (s ^ b)
                        last = nc.vector.tensor_copy(
                            values[to:to + SEQ, :, :].rearrange("p (j b) d -> p j b d", b=SPT)[:, :, b, :], src)
                last.then_inc(values_ready.sem, 1)

            def turn(t, one, two):
                dve.wait_ge(scored.sem, scored.now(t, 1))
                for b in range(NB):
                    cols = slice(0, SEQ) if b % 2 == 0 else slice(SEQ, P)
                    last = nc.vector.scalar_tensor_tensor(out=p_s[:, b:b + 1, cols], in0=masks[:, bass.ds(t * NB + b, 1), :],
                                                          scalar=MASKED, in1=p_s[:, b:b + 1, cols], op0=ALU.mult, op1=ALU.add)
                last.then_inc(masked.sem, 1)
                dve.wait_ge(masked.sem, masked.now(t, 1))
                nc.vector.tensor_reduce(neg_max[:, :], p_s[:, :, :], AX_X, ALU.max, negate=True).then_inc(maxed.sem, 1)
                dve.wait_ge(probs_normed.sem, probs_normed.before(t, 1))
                dve.wait_ge(exped.sem, exped.now(t, 1))
                nc.vector.reciprocal(rsum[:, :], sums[:, :]).then_inc(inverted.sem, 1)
                if two:
                    norm_inputs(t + 2)
                if one:
                    head_norms(t + 1)
                if two:
                    write_inputs(t + 2)
                if one:
                    scale_heads(t + 1)
                dve.wait_ge(projected.sem, projected.before(t, 1))
                dve.wait_ge(weighted.sem, weighted.now(t, 1))
                for h in range(XHEADS):
                    r = slice(XHD * h, XHD * h + XHD)
                    last = nc.vector.tensor_copy(mixed[r, :, :], p_o[r, :, h, :])
                last.then_inc(mixed_ready.sem, 1)
                if one:
                    place_values(t + 1)
                dve.wait_ge(residual_done.sem, residual_done.now(t, 1))
                dve.wait_ge(projected.sem, projected.now(t, 1))
                tail.moments_vector(dve, t, p_qy[:, 1, :, :], residual[:, :, :])
                tail.write_vector(dve, t, lambda j: X[:, bass.ds(t * NT + j, 1), :])

            norm_inputs(0)
            write_inputs(0)
            head_norms(0)
            scale_heads(0)
            place_values(0)
            norm_inputs(1)
            write_inputs(1)
            dve.wait_ge(mask_ready, 1)
            all_turns(dve, turn)
def stage_experts(nc, X, W, rms_w, w1, w2, experts_in):
    GT = 4
    GN = GT * P
    TURNS = TILES // GT
    HC = EH // P
    ORDER = [ROUTED] + list(range(ROUTED)) + [ROUTED + 1]
    RMS_EPS = 1.1920929e-07
    with ExitStack() as ctx:
        def sb(n, shape, dt=F32):
            return ctx.enter_context(nc.sbuf_tensor("ex_" + n, shape, dt))

        def ps(n, shape):
            return ctx.enter_context(nc.psum_tensor("ex_" + n, shape, F32))

        def sig(n, per=1):
            return Signal(ctx, nc, "ex_" + n, per)

        squares = sb("squares", [P, GT, D])
        ssq = sb("ssq", [P, GT])
        mean_sq = sb("mean_sq", [P, GT])
        rnorm = sb("rnorm", [P, GT])
        x_raw = sb("x_raw", [P, GT, D])
        x_scaled = sb("x_scaled", [P, GT, D])
        x_raw_t = sb("x_raw_t", [P, GN])
        x_t = sb("x_t", [P, GN])
        hidden = sb("hidden", [P, 4, GN])
        acc = sb("acc", [P, GT, D])
        R = [P, GT, ROUTED]
        top = sb("top", [P, GT, 5])
        logits, exps, gates, hits, picks, rest, picks2 = (sb(n, R) for n in
                                                          ("logits", "exps", "gates", "hits", "picks", "rest", "picks2"))
        gate_next = sb("gate_next", R)
        gate = sb("gate", R)
        p_h = ps("p_h", [P, 3, GN])
        p_o = ps("p_o", [P, 2, GT, D])
        p_t = ps("p_t", [P, GN])
        p_x = ps("p_x", [P, GN])
        p_r = ps("p_r", [P, GT, P])

        tail = NormTail(ctx, nc, "ex_tail", GT)
        w1_scaled = nc.alloc_semaphore("ex_w1_scaled")
        squared, mean_done, rooted, scaled = sig("squared"), sig("mean_done"), sig("rooted"), sig("scaled")
        raw_copied = sig("raw_copied")
        turned = sig("turned")
        raw_turned = sig("raw_turned")
        raw_t_ready = sig("raw_t_ready")
        x_t_ready = sig("x_t_ready")
        routed = sig("routed")
        shifted = sig("shifted")
        exped = sig("exped")
        STEPS = 20
        step = sig("step", STEPS)
        gate_copied = sig("gate_copied")
        h_done = sig("h_done", EXPERTS * HC)
        silu_done = sig("silu_done", EXPERTS * HC)
        out_done = sig("out_done", EXPERTS)
        acc_done = sig("acc_done", EXPERTS - 1)

        block = ctx.enter_context(nc.Block())

        def group(t):
            return X[:, bass.ds(t * GT, GT), :]

        def all_turns(engine, turn):
            with engine.Fori(0, TURNS - 1) as t:
                turn(t, True)
            turn(TURNS - 1, False)

        @block.gpsimd
        def _(pool):
            credit(pool, rooted, raw_copied)
            tail.credit_pool(pool)

            def front(t, first=False):
                pool.wait_ge(raw_turned.sem, raw_turned.before(t, 1))
                if not first:
                    pool.wait_ge(acc_done.sem, acc_done.before(t, 1))
                pool.wait_ge(scaled.sem, scaled.before(t, 1))
                pool.wait_ge(mean_done.sem, mean_done.now(t, 1))
                nc.gpsimd.tensor_tensor(rnorm[:, :], mean_sq[:, :], W["minus_half"][:, 0:GT], ALU.pow)\
                    .then_inc(rooted.sem, 1)
                nc.gpsimd.tensor_copy(x_raw[:, :, :], group(t)).then_inc(raw_copied.sem, 1)

            def turn(t, one):
                if one:
                    front(t + 1)
                tail.root_pool(pool, t, W["minus_half"])

            front(0, True)
            all_turns(pool, turn)

        @block.tensor
        def _(pe):
            credit(pe, turned, raw_turned, routed, h_done, out_done)

            def transpose_raw(t):
                pe.wait_ge(raw_copied.sem, raw_copied.now(t, 1))
                pe.wait_ge(raw_t_ready.sem, raw_t_ready.before(t, 1))
                for j in range(GT):
                    last = pe.transpose(p_x[:, j * P:(j + 1) * P], x_raw[:, j, :], W["ident"])
                last.then_inc(raw_turned.sem, 1)

            def transpose_scaled(t):
                pe.wait_ge(scaled.sem, scaled.now(t, 1))
                pe.wait_ge(x_t_ready.sem, x_t_ready.before(t, 1))
                for j in range(GT):
                    last = pe.transpose(p_t[:, j * P:(j + 1) * P], x_scaled[:, j, :], W["ident"])
                last.then_inc(turned.sem, 1)

            def route(t):
                pe.wait_ge(raw_t_ready.sem, raw_t_ready.now(t, 1))
                pe.wait_ge(shifted.sem, shifted.before(t, 1))
                for j in range(GT):
                    last = pe.matmul(p_r[:, j, 0:ROUTED], x_raw_t[:, j * P:(j + 1) * P], W["router"], start=True, stop=True)
                last.then_inc(routed.sem, 1)

            def up(t, n):
                if n == 0:
                    pe.wait_ge(x_t_ready.sem, x_t_ready.now(t, 1))
                for c in range(HC):
                    i = HC * n + c
                    pe.wait_ge(silu_done.sem, silu_done.now(t, i - 2) if i >= 3 else silu_done.before(t, EXPERTS * HC + i - 2))
                    pe.matmul(p_h[:, i % 3, :], w1[:, ORDER[n], c * P:(c + 1) * P], x_t[:, :], start=True, stop=True)\
                        .then_inc(h_done.sem, 1)

            def down(t, n):
                pe.wait_ge(silu_done.sem, silu_done.now(t, HC * n + HC))
                if n >= 2:
                    pe.wait_ge(acc_done.sem, acc_done.now(t, n - 1))
                elif n == 0:
                    pe.wait_ge(acc_done.sem, acc_done.before(t, EXPERTS - 1))
                else:
                    pe.wait_ge(tail.added.sem, tail.added.before(t, 1))
                for j in range(GT):
                    for c in range(HC):
                        last = pe.matmul(p_o[:, n % 2, j, :], hidden[:, (HC * n + c) % 4, j * P:(j + 1) * P],
                                         w2[:, ORDER[n], c, :], start=(c == 0), stop=(c == HC - 1))
                last.then_inc(out_done.sem, 1)

            def turn(t, one):
                for n in range(EXPERTS + 1):
                    if n < EXPERTS:
                        up(t, n)
                    if n >= 1:
                        down(t, n - 1)
                    if one and n == 5:
                        transpose_raw(t + 1)
                        transpose_scaled(t + 1)
                    if one and n == 7:
                        route(t + 1)

            transpose_raw(0)
            transpose_scaled(0)
            route(0)
            pe.wait_ge(w1_scaled, EXPERTS)
            all_turns(pe, turn)

        @block.scalar
        def _(act):
            credit(act, squared, raw_t_ready, x_t_ready, exped, silu_done)

            def square(t):
                act.wait_ge(mean_done.sem, mean_done.before(t, 1))
                for j in range(GT):
                    last = nc.scalar.activation(squares[:, j, :].unsqueeze(1), X[:, bass.ds(t * GT + j, 1), :], ACT.Square,
                                                accum_out=ssq[:, j:j + 1])
                last.then_inc(squared.sem, 1)

            def raw_copy(t):
                act.wait_ge(raw_turned.sem, raw_turned.now(t, 1))
                act.wait_ge(routed.sem, routed.before(t, 1))
                nc.scalar.activation(x_raw_t[:, :], p_x[:, :], ACT.Copy).then_inc(raw_t_ready.sem, 1)

            def x_copy(t):
                act.wait_ge(turned.sem, turned.now(t, 1))
                act.wait_ge(h_done.sem, h_done.before(t, EXPERTS * HC))
                nc.scalar.activation(x_t[:, :], p_t[:, :], ACT.Copy).then_inc(x_t_ready.sem, 1)

            def exp(t):
                act.wait_ge(step.sem, step.before(t, STEPS))
                act.wait_ge(shifted.sem, shifted.now(t, 1))
                nc.scalar.activation(exps[:, :, :], logits[:, :, :], ACT.Exp).then_inc(exped.sem, 1)

            def turn(t, one):
                if one:
                    square(t + 1)
                for i in range(EXPERTS * HC):
                    n = i // HC
                    if n >= 2:
                        act.wait_ge(out_done.sem, out_done.now(t, n - 1))
                    else:
                        act.wait_ge(out_done.sem, out_done.before(t, EXPERTS - 1 + n))
                    act.wait_ge(h_done.sem, h_done.now(t, i + 1))
                    nc.scalar.activation(hidden[:, i % 4, :], p_h[:, i % 3, :], ACT.Silu).then_inc(silu_done.sem, 1)
                    if one and i == 13:
                        raw_copy(t + 1)
                    if one and i == 25:
                        exp(t + 1)
                if one:
                    x_copy(t + 1)

            square(0)
            raw_copy(0)
            x_copy(0)
            exp(0)
            all_turns(act, turn)

        @block.vector
        def _(dve):
            credit(dve, mean_done, scaled, shifted, step, gate_copied, acc_done)
            tail.credit_vector(dve)

            def mean_rows(t):
                dve.wait_ge(squared.sem, squared.now(t, 1))
                dve.wait_ge(rooted.sem, rooted.before(t, 1))
                nc.vector.tensor_scalar(mean_sq[:, :], ssq[:, :], 1.0 / D, RMS_EPS, ALU.mult, ALU.add)\
                    .then_inc(mean_done.sem, 1)

            def scale_rows(t):
                dve.wait_ge(turned.sem, turned.before(t, 1))
                dve.wait_ge(rooted.sem, rooted.now(t, 1))
                for j in range(GT):
                    last = nc.vector.tensor_scalar(x_scaled[:, j, :].unsqueeze(1), X[:, bass.ds(t * GT + j, 1), :],
                                                   rnorm[:, j:j + 1], None, ALU.mult)
                last.then_inc(scaled.sem, 1)

            def gates_of(t):
                done = [0]

                def small(ins):
                    done[0] += 1
                    ins.then_inc(step.sem, 1)
                    dve.wait_ge(step.sem, step.now(t, done[0]))

                def wide(k):
                    return top[:, :, k:k + 1].broadcast_to((P, GT, ROUTED))

                tt, reduce = nc.vector.tensor_tensor, nc.vector.tensor_reduce
                dve.wait_ge(exped.sem, exped.before(t, 1))
                dve.wait_ge(routed.sem, routed.now(t, 1))
                small(reduce(top[:, :, 0:1], p_r[:, :, 0:ROUTED], AX_X, ALU.max, negate=True))
                tt(logits[:, :, :], p_r[:, :, 0:ROUTED], wide(0), ALU.add).then_inc(shifted.sem, 1)
                dve.wait_ge(exped.sem, exped.now(t, 1))
                small(reduce(top[:, :, 1:2], exps[:, :, :], AX_X, ALU.add))
                small(nc.vector.reciprocal(top[:, :, 1:2], top[:, :, 1:2]))
                small(tt(gates[:, :, :], exps[:, :, :], wide(1), ALU.mult))
                rank = W["first_rank"].unsqueeze(1).broadcast_to((P, GT, ROUTED))

                def best_of(values, picked):
                    small(reduce(top[:, :, 2:3], values[:, :, :], AX_X, ALU.max))
                    small(tt(hits[:, :, :], values[:, :, :], wide(2), ALU.is_equal))
                    small(tt(hits[:, :, :], hits[:, :, :], rank, ALU.mult))
                    small(reduce(top[:, :, 3:4], hits[:, :, :], AX_X, ALU.max))
                    small(tt(picked[:, :, :], hits[:, :, :], wide(3), ALU.is_equal))

                best_of(gates, picks)
                small(nc.vector.scalar_tensor_tensor(out=rest[:, :, :], in0=picks[:, :, :], scalar=-2.0, in1=gates[:, :, :],
                                                     op0=ALU.mult, op1=ALU.add))
                best_of(rest, picks2)
                small(tt(picks[:, :, :], picks[:, :, :], picks2[:, :, :], ALU.add))
                small(tt(gates[:, :, :], gates[:, :, :], picks[:, :, :], ALU.mult))
                small(reduce(top[:, :, 4:5], gates[:, :, :], AX_X, ALU.add))
                small(nc.vector.tensor_scalar(top[:, :, 4:5], top[:, :, 4:5], 1e-9, None, ALU.add))
                small(nc.vector.reciprocal(top[:, :, 4:5], top[:, :, 4:5]))
                assert done[0] == STEPS

            def gate_ready(t):
                dve.wait_ge(acc_done.sem, acc_done.before(t, EXPERTS - 1))
                nc.vector.tensor_tensor(gate[:, :, :], gates[:, :, :], top[:, :, 4:5].broadcast_to((P, GT, ROUTED)), ALU.mult)\
                    .then_inc(gate_copied.sem, 1)
                dve.wait_ge(gate_copied.sem, gate_copied.now(t, 1))

            def accumulate(t, n):
                dve.wait_ge(out_done.sem, out_done.now(t, n + 1))
                out = p_o[:, n % 2, :, :]
                if n == 0:
                    dve.wait_ge(tail.added.sem, tail.added.before(t, 1))
                    nc.vector.tensor_tensor(acc[:, :, :], out, x_raw[:, :, :], ALU.add).then_inc(acc_done.sem, 1)
                else:
                    dve.wait_ge(acc_done.sem, acc_done.now(t, n))
                    for j in range(GT):
                        last = nc.vector.scalar_tensor_tensor(out=acc[:, j, :], in0=out[:, j, :],
                                                              scalar=gate[:, j, ORDER[n]:ORDER[n] + 1], in1=acc[:, j, :],
                                                              op0=ALU.mult, op1=ALU.add)
                    last.then_inc(acc_done.sem, 1)

            def turn(t, one):
                gate_ready(t)
                for n in range(EXPERTS - 1):
                    accumulate(t, n)
                    if one and n == 0:
                        mean_rows(t + 1)
                    if one and n == 2:
                        scale_rows(t + 1)
                    if one and n == 11:
                        gates_of(t + 1)
                dve.wait_ge(acc_done.sem, acc_done.now(t, EXPERTS - 1))
                dve.wait_ge(out_done.sem, out_done.now(t, EXPERTS))
                tail.moments_vector(dve, t, p_o[:, (EXPERTS - 1) % 2, :, :], acc[:, :, :])
                tail.write_vector(dve, t, lambda j: X[:, bass.ds(t * GT + j, 1), :])

            mean_rows(0)
            scale_rows(0)
            dve.wait_ge(experts_in, 48)
            for e in range(EXPERTS):
                nc.vector.tensor_scalar(w1[:, e, :], w1[:, e, :], rms_w[:, e:e + 1], None, ALU.mult).then_inc(w1_scaled, 1)
            gates_of(0)
            all_turns(dve, turn)
def weight_layout():
    sizes = [("ident", P), ("pwT", D), ("gruT", 2 * D), ("ff1T", HIDDEN), ("ff2T", HIDDEN),
             ("dw", 3), ("dw_b", 1), ("gains_raw", 3), ("ff_b1", 4), ("pw_b", D), ("ff_b2", D),
             ("WqT", D), ("WkT", D), ("WvT", D), ("WoT", D),
             ("gamma_x", 1), ("gamma_slot", 1), ("slots", SLOTS), ("moe_w1", HIDDEN), ("moe_w2", HIDDEN),
             ("Wqkv", 3 * D), ("qk_b", 2), ("v_b", 1), ("Wout", D), ("out_b", D),
             ("lnx_g", 1), ("lnx_b", 1), ("lnl_g", 1), ("lnl_b", 1), ("q_gamma", 1), ("k_gamma", 1),
             ("XWq", D), ("XWkv", 2 * D), ("XWout", D), ("xout_b", D),
             ("router", ROUTED), ("head_mask", 4), ("window", SEQ), ("first_rank", ROUTED)]
    at, out = 0, {}
    for name, n in sizes:
        out[name] = (at, n)
        at += n
    return out, at


def build(nc, x, ctx_in, mask, weights, rms_w, w1, w2, out, stages=6):
    layout, columns = weight_layout()
    with ExitStack() as ctx:
        X = ctx.enter_context(nc.sbuf_tensor("X", [P, TILES, D], F32))
        pack = ctx.enter_context(nc.sbuf_tensor("pack", [P, columns], F32))
        prepared = ctx.enter_context(nc.sbuf_tensor("prepared", [P, 32], F32))
        ew1 = ctx.enter_context(nc.sbuf_tensor("ew1", [P, EXPERTS, EH], F32))
        ew2 = ctx.enter_context(nc.sbuf_tensor("ew2", [P, EXPERTS, EH // P, D], F32))
        erms = ctx.enter_context(nc.sbuf_tensor("erms", [P, EXPERTS], F32))
        experts_in = ctx.enter_context(nc.semaphore("experts_in"))
        W = {n: pack[:, a:a + k] for n, (a, k) in layout.items()}
        W["ff2T"] = W["ff2T"].rearrange("p (c d) -> p c d", c=4)
        W["moe_w2"] = W["moe_w2"].rearrange("p (c d) -> p c d", c=4)
        W["slots"] = W["slots"].rearrange("p (c d) -> p c d", c=4)
        W["gains"] = prepared[:, 0:3]
        W["minus_half"] = prepared[:, 8:24]
        load(nc, X, pack, prepared, W, x, weights, (rms_w, w1, w2), (erms, ew1, ew2), experts_in)
        chain = (lambda: stage_conv_gru(nc, X, W), lambda: stage_attention(nc, X, W, 0, ctx_in),
                 lambda: stage_soft_mixture(nc, X, W), lambda: stage_attention(nc, X, W, 1, ctx_in),
                 lambda: stage_cross(nc, X, W, ctx_in, mask), lambda: stage_experts(nc, X, W, erms, ew1, ew2, experts_in))
        for k, stage in enumerate(chain):
            if k < stages or k == -stages - 1:
                with nc.cleanup_on_exit():
                    stage()
        store(nc, X, out)


def load(nc, X, pack, prepared, W, x, weights, expert_weights, expert_tiles, experts_in):
    with ExitStack() as ctx:
        x_in = ctx.enter_context(nc.semaphore("x_in"))
        w_in = ctx.enter_context(nc.semaphore("w_in"))
        block = ctx.enter_context(nc.Block())

        @block.sync
        def _(sp):
            sp.dma_start(X[:, :, :], x.rearrange("(t p) d -> p t d", p=P)).then_inc(x_in, 16)
            sp.wait_ge(x_in, 16)
            (rms_w, w1, w2), (erms, ew1, ew2) = expert_weights, expert_tiles
            sp.dma_start(erms[:, :], rms_w).then_inc(experts_in, 16)
            sp.dma_start(ew1[:, :, :], w1.rearrange("e d h -> d e h")).then_inc(experts_in, 16)
            sp.dma_start(ew2[:, :, :, :], w2.rearrange("e (c p) d -> p e c d", p=P)).then_inc(experts_in, 16)

        @block.scalar
        def _(act):
            act.dma_start(pack[:, :], weights).then_inc(w_in, 16)

        @block.vector
        def _(dve):
            nc.vector.memset(W["minus_half"], -0.5)
            dve.wait_ge(w_in, 16)
            nc.vector.tensor_scalar(W["gains"], W["gains_raw"], 1.0, float(D) ** 0.5, ALU.add, ALU.mult)


def store(nc, X, out):
    with ExitStack() as ctx:
        stored = ctx.enter_context(nc.semaphore("stored"))
        block = ctx.enter_context(nc.Block())

        @block.sync
        def _(sp):
            sp.dma_start(out.rearrange("(t p) d -> p t d", p=P), X[:, :, :]).then_inc(stored, 16)
            sp.wait_ge(stored, 16)


def pack_weights(v):
    def rows(a):
        return np.broadcast_to(np.asarray(a).reshape(1, -1), (P, np.asarray(a).size))

    def chunks(a):
        a = np.asarray(a)
        return a.reshape(4, P, a.shape[1]).transpose(1, 0, 2).reshape(P, -1)

    def col(a):
        return np.asarray(a).reshape(-1, 1)

    f, q = np.arange(P), np.arange(P)[:, None] % SEQ
    k = np.arange(SEQ)[None, :]
    allowed = (q - k >= 0) & (q - k < WINDOW)
    parts = {
        "ident": np.eye(P, dtype=np.float32),
        "pwT": v["L0_attn_conv_pw_w"].T, "gruT": v["L0_attn_gru_w"].T, "ff1T": v["L0_attn_ff_w1"].T,
        "ff2T": chunks(v["L0_attn_ff_w2"].T), "dw": v["L0_attn_conv_dw_w"].reshape(D, 3),
        "dw_b": col(v["L0_attn_conv_dw_b"]),
        "gains_raw": np.stack([v["L0_attn_conv_norm_g"], v["L0_attn_gru_norm_g"], v["L0_attn_ff_norm_g"]], 1),
        "ff_b1": v["L0_attn_ff_b1"].reshape(4, P).T, "pw_b": rows(v["L0_attn_conv_pw_b"]), "ff_b2": rows(v["L0_attn_ff_b2"]),
        "WqT": v["L0_xattn_Wq"].T, "WkT": v["L0_xattn_Wk"].T, "WvT": v["L0_xattn_Wv"].T, "WoT": v["L0_xattn_Wo"].T,
        "gamma_x": col(v["L0_ffn_gamma_x"]), "gamma_slot": col(v["L0_ffn_gamma_slot"]),
        "slots": chunks(v["L0_ffn_slot_embeds"].reshape(SLOTS, D)), "moe_w1": v["L0_ffn_w1"], "moe_w2": chunks(v["L0_ffn_w2"]),
        "Wqkv": v["L1_attn_W_qkv"], "qk_b": v["L1_attn_b_qkv"][:2 * D].reshape(2, D).T, "v_b": col(v["L1_attn_b_qkv"][2 * D:]),
        "Wout": v["L1_attn_W_out"], "out_b": rows(v["L1_attn_b_out"]),
        "lnx_g": col(v["L1_xattn_ln_x_g"]), "lnx_b": col(v["L1_xattn_ln_x_b"]),
        "lnl_g": col(v["L1_xattn_ln_l_g"]), "lnl_b": col(v["L1_xattn_ln_l_b"]),
        "q_gamma": col(np.concatenate([v["L1_xattn_q_gamma"]] * 2)), "k_gamma": col(np.concatenate([v["L1_xattn_k_gamma"]] * 2)),
        "XWq": v["L1_xattn_W_q"], "XWkv": v["L1_xattn_W_kv"], "XWout": v["L1_xattn_W_out"], "xout_b": rows(v["L1_xattn_b_out"]),
        "router": v["L1_ffn_router_w"],
        "head_mask": (f[:, None] % 32 // HD == np.arange(4)[None, :]).astype(np.float32),
        "window": np.where(allowed, np.float32(0), np.float32(-1e30)),
        "first_rank": rows(np.arange(ROUTED, 0, -1).astype(np.float32)),
    }
    layout, columns = weight_layout()
    packed = np.zeros((P, columns), np.float32)
    for name, (a, n) in layout.items():
        packed[:, a:a + n] = parts[name]
    return packed


_OUT = ((BATCH, SEQ, D), "float32")


def kernel(**inputs):
    import concourse.bacc as _bacc
    from concourse.bass_utils import run_bass_kernel_spmd as _run

    v = {n: np.asarray(a) for n, a in inputs.items()}
    arrays = {
        "x": v["x"].reshape(BATCH * SEQ, D), "ctx": v["ctx_1024"].reshape(BATCH * SEQ, D),
        "mask": v["mask_BxS2_bk0"], "weights": pack_weights(v),
        "rms_w": np.ascontiguousarray(np.concatenate([v["L1_ffn_rms_w"], v["L1_ffn_rms_w_s"]]).T),
        "w1": np.concatenate([v["L1_ffn_w1"], v["L1_ffn_w1_s"]]), "w2": np.concatenate([v["L1_ffn_w2"], v["L1_ffn_w2_s"]]),
    }
    arrays = {n: np.ascontiguousarray(a) for n, a in arrays.items()}
    nc = _bacc.Bacc("TRN2", target_bir_lowering=False, num_devices=1)
    aps = [nc.dram_tensor(n, a.shape, mybir.dt.from_np(a.dtype), kind="ExternalInput").ap() for n, a in arrays.items()]
    out = nc.dram_tensor("out", [BATCH * SEQ, D], F32, kind="ExternalOutput").ap()
    build(nc, *aps, out)
    r = _run(nc, [arrays], core_ids=[0])
    return r.results[0]["out"].reshape(_OUT[0])
```

```python
from contextlib import ExitStack

import numpy as np

import concourse.bass as bass
from concourse import mybir

ALU = mybir.AluOpType
ACT = mybir.ActivationFunctionType
F32 = mybir.dt.float32
F32R = mybir.dt.float32r
BF16 = mybir.dt.bfloat16
U8 = mybir.dt.uint8
AX_X = mybir.AxisListType.X

P = 128
D = 128
BATCH, SEQ = 64, 64
SPT = P // SEQ
TILES = BATCH // SPT
HIDDEN = 4 * D
SLOTS = 512
HEADS, HD = 16, 8
ROUTED, SHARED, EH = 14, 2, 256
EXPERTS = ROUTED + SHARED
WINDOW = 32
LN_EPS = 1e-5
NORM_FLOOR = 1e-24


class Signal:

    def __init__(self, ctx, nc, name, per):
        self.sem, self.per = nc.alloc_semaphore(name), per

    def now(self, turn, n):
        return (turn + 1) * self.per + n

    def before(self, turn, n):
        return turn * self.per + n


def credit(engine, *signals):
    for s in signals:
        engine.nop().then_inc(s.sem, s.per)
class NormTail:

    def __init__(self, ctx, nc, name, n):
        def sb(part, shape):
            return ctx.enter_context(nc.sbuf_tensor(f"{name}_{part}", shape, F32))

        def sig(part):
            return Signal(ctx, nc, f"{name}_{part}", 1)

        self.nc, self.n = nc, n
        self.total = sb("total", [P, n, D])
        self.stats = sb("stats", [P, n, 6])
        self.moments = sb("moments", [P, n, 2])
        self.var_eps = sb("var_eps", [P, n])
        self.rstd = sb("rstd", [P, n])
        self.scrap = sb("scrap", [P, 1])
        self.added, self.counted, self.aggregated, self.floored = sig("added"), sig("counted"), sig("aggregated"), sig("floored")
        self.rooted, self.done = sig("rooted"), sig("done")

    def credit_vector(self, dve):
        credit(dve, self.added, self.counted, self.aggregated, self.floored, self.done)

    def credit_pool(self, pool):
        credit(pool, self.rooted)

    def moments_vector(self, dve, t, branch, residual):
        nc = self.nc
        dve.wait_ge(self.done.sem, self.done.before(t, 1))
        nc.vector.tensor_tensor(self.total[:, :, :], branch, residual, ALU.add).then_inc(self.added.sem, 1)
        dve.wait_ge(self.added.sem, self.added.now(t, 1))
        for j in range(self.n):
            last = nc.vector.bn_stats(self.stats[:, j, :], self.total[:, j, :])
        last.then_inc(self.counted.sem, 1)
        dve.wait_ge(self.counted.sem, self.counted.now(t, 1))
        nc.vector.memset(self.scrap[:, :], 0.0)
        for j in range(self.n):
            last = nc.vector.bn_aggr(self.moments[:, j, :], self.stats[:, j, :])
        last.then_inc(self.aggregated.sem, 1)
        dve.wait_ge(self.aggregated.sem, self.aggregated.now(t, 1))
        dve.wait_ge(self.rooted.sem, self.rooted.before(t, 1))
        nc.vector.tensor_scalar(self.var_eps[:, :], self.moments[:, :, 1], LN_EPS, None, ALU.add)\
            .then_inc(self.floored.sem, 1)

    def root_pool(self, pool, t, minus_half):
        pool.wait_ge(self.done.sem, self.done.before(t, 1))
        pool.wait_ge(self.floored.sem, self.floored.now(t, 1))
        self.nc.gpsimd.tensor_tensor(self.rstd[:, :], self.var_eps[:, :], minus_half[:, 0:self.n], ALU.pow)\
            .then_inc(self.rooted.sem, 1)

    def write_vector(self, dve, t, out_tile):
        dve.wait_ge(self.rooted.sem, self.rooted.now(t, 1))
        for j in range(self.n):
            last = self.nc.vector.tensor_scalar(out_tile(j), self.total[:, j, :].unsqueeze(1), self.moments[:, j, 0:1],
                                                self.rstd[:, j:j + 1], ALU.subtract, ALU.mult)
        last.then_inc(self.done.sem, 1)
def stage_conv_gru(nc, X, W):
    GT = 4
    GN = GT * P
    U = 2
    TURNS = TILES // (GT * U)
    NSEQ = GN // SEQ
    with ExitStack() as ctx:
        def sb(name, shape, dt=F32):
            return ctx.enter_context(nc.sbuf_tensor("cg_" + name, shape, dt))

        def sig(name, per=U):
            return Signal(ctx, nc, "cg_" + name, per)

        squares = sb("squares", [P, U, GT, D])
        ssq = sb("ssq", [P, U, 3, GT])
        floored = sb("floored", [P, U, 3, GT])
        rnorm = sb("rnorm", [P, U, 3, GT])
        x_bias = sb("x_bias", [P, U, GT, D])
        x_conv = sb("x_conv", [P, U, GT, D])
        x_gru = sb("x_gru", [P, U, GT, D])
        x_twice = sb("x_twice", [P, U, GT, D])
        x_scaled = sb("x_scaled", [P, U, GT, D])
        padded = sb("padded", [P, U, NSEQ, SEQ + 2])
        conv = sb("conv", [P, U, GN])
        xn = sb("xn", [P, U, GN])
        sig_hidden = sb("sig_hidden", [P, U, GN])
        update = sb("update", [P, U, GN])
        keep = sb("keep", [P, U, GN])
        hgru = sb("hgru", [P, U, GN])
        hff = sb("hff", [P, U, 4, GN])
        total = sb("total", [P, U, GT, D])
        stats = sb("stats", [P, U, GT, 6])
        moments = sb("moments", [P, U, GT, 2])
        var_eps = sb("var_eps", [P, U, GT])
        rstd = sb("rstd", [P, U, GT])
        scrap = sb("scrap", [P, 1])
        ps = ctx.enter_context(nc.psum_tensor("cg_ps", [P, U, 4, GN], F32))
        gain1, gain2, gain3 = (W["gains"][:, k:k + 1] for k in range(3))

        zeroed = nc.alloc_semaphore("cg_zeroed")
        s_sq = [sig(f"sq{k}") for k in range(3)]
        s_fl = [sig(f"fl{k}") for k in range(3)]
        s_rn = [sig(f"rn{k}") for k in range(3)]
        s_xs = [sig(f"xs{k}") for k in range(3)]
        s_xt = [sig(f"xt{k}") for k in range(3)]
        s_xn = [sig(f"xn{k}") for k in range(3)]
        s_xb = sig("xb")
        s_cv = sig("cv", 3 * U)
        s_pw = sig("pw")
        s_x1 = sig("x1")
        s_hg = sig("hg")
        s_sg = sig("sg", 2 * U)
        s_gr = sig("gr", 2 * U)
        s_sc = sig("sc")
        s_ht = sig("ht")
        s_x2 = sig("x2")
        s_x2b = sig("x2b", 2 * U)
        s_f1 = sig("f1", 4 * U)
        s_ge = sig("ge", 4 * U)
        s_f2 = sig("f2")
        s_tt = sig("tt")
        s_bs = sig("bs")
        s_mv = sig("mv")
        s_ve = sig("ve")
        s_rs = sig("rs")
        s_out = sig("out")

        block = ctx.enter_context(nc.Block())

        def group(t, u):
            return X[:, bass.ds((t * U + u) * GT, GT), :]

        def tile_of(t, u, j):
            return X[:, bass.ds((t * U + u) * GT + j, 1), :]

        @block.scalar
        def _(act):
            credit(act, *s_sq, *s_xn, s_sg, s_ge)
            act.wait_ge(zeroed, 2)
            with act.Fori(0, TURNS) as t:
                def sum_squares(k, source):
                    for u in range(U):
                        if k == 1:
                            act.wait_ge(s_x1.sem, s_x1.now(t, u + 1))
                        if k == 2:
                            act.wait_ge(s_x2.sem, s_x2.now(t, u + 1))
                        act.wait_ge(s_fl[k].sem, s_fl[k].before(t, u + 1))
                        for j in range(GT):
                            last = nc.scalar.activation(squares[:, u, j, :].unsqueeze(1), source(u, j), ACT.Square,
                                                        accum_out=ssq[:, u, k, j:j + 1])
                        last.then_inc(s_sq[k].sem, 1)

                def to_features(k):
                    for u in range(U):
                        act.wait_ge(s_xt[k].sem, s_xt[k].now(t, u + 1))
                        if k == 0:
                            act.wait_ge(s_cv.sem, s_cv.before(t, 3 * u + 3))
                            out = padded[:, u, :, 2:]
                            src = ps[:, u, 0, :].rearrange("p (b s) -> p b s", s=SEQ)
                        else:
                            if k == 1:
                                act.wait_ge(s_f1.sem, s_f1.before(t, 4 * u + 4))
                            else:
                                act.wait_ge(s_hg.sem, s_hg.now(t, u + 1))
                            out, src = xn[:, u, :], ps[:, u, 0, :]
                        nc.scalar.activation(out, src, ACT.Copy, scale=(gain1, gain2, gain3)[k])\
                            .then_inc(s_xn[k].sem, 1)

                sum_squares(0, lambda u, j: tile_of(t, u, j))
                to_features(0)
                sum_squares(1, lambda u, j: x_conv[:, u, j, :].unsqueeze(1))
                to_features(1)
                for u in range(U):
                    act.wait_ge(s_hg.sem, s_hg.now(t, u + 1))
                    act.wait_ge(s_gr.sem, s_gr.before(t, 2 * u + 2))
                    nc.scalar.activation(sig_hidden[:, u, :], ps[:, u, 1, :], ACT.Sigmoid).then_inc(s_sg.sem, 1)
                    nc.scalar.activation(update[:, u, :], ps[:, u, 2, :], ACT.Sigmoid)
                    act.wait_ge(s_sc.sem, s_sc.before(t, u + 1))
                    nc.scalar.activation(keep[:, u, :].rearrange("p (b s) -> p b s", s=SEQ)[:, :, 1:],
                                         ps[:, u, 2, :].rearrange("p (b s) -> p b s", s=SEQ)[:, :, 1:],
                                         ACT.Sigmoid, scale=-1.0).then_inc(s_sg.sem, 1)
                sum_squares(2, lambda u, j: x_gru[:, u, j, :].unsqueeze(1))
                to_features(2)
                for u in range(U):
                    act.wait_ge(s_f2.sem, s_f2.before(t, u + 1))
                    for c in range(4):
                        act.wait_ge(s_f1.sem, s_f1.now(t, 4 * u + c + 1))
                        nc.scalar.activation(hff[:, u, c, :], ps[:, u, 1 + c % 3, :], ACT.Gelu,
                                             bias=W["ff_b1"][:, c:c + 1]).then_inc(s_ge.sem, 1)

        @block.gpsimd
        def _(pool):
            nc.gpsimd.memset(padded[:, :, :, 0:2], 0.0).then_inc(zeroed, 1)
            nc.gpsimd.memset(keep[:, :, :].rearrange("p u (b s) -> p u b s", s=SEQ)[:, :, :, 0:1], 0.0)\
                .then_inc(zeroed, 1)
            credit(pool, *s_rn, s_xb, s_x2b, s_rs)
            with pool.Fori(0, TURNS) as t:
                def reciprocal_norm(k):
                    for u in range(U):
                        pool.wait_ge(s_xs[k].sem, s_xs[k].before(t, u + 1))
                        if k == 0:
                            pool.wait_ge(s_out.sem, s_out.before(t, u + 1))
                        pool.wait_ge(s_fl[k].sem, s_fl[k].now(t, u + 1))
                        nc.gpsimd.tensor_tensor(rnorm[:, u, k, :], floored[:, u, k, :], W["minus_half"][:, 0:GT],
                                                ALU.pow).then_inc(s_rn[k].sem, 1)

                reciprocal_norm(0)
                for u in range(U):
                    nc.gpsimd.tensor_tensor(x_bias[:, u, :, :], group(t, u),
                                            W["pw_b"].unsqueeze(1).broadcast_to((P, GT, D)), ALU.add).then_inc(s_xb.sem, 1)
                    nc.gpsimd.tensor_tensor(x_twice[:, u, :, :], group(t, u),
                                            W["ff_b2"].unsqueeze(1).broadcast_to((P, GT, D)), ALU.add)\
                        .then_inc(s_x2b.sem, 1)
                reciprocal_norm(1)
                reciprocal_norm(2)
                for u in range(U):
                    pool.wait_ge(s_x2b.sem, s_x2b.now(t, U + u))
                    pool.wait_ge(s_x2.sem, s_x2.now(t, u + 1))
                    nc.gpsimd.tensor_tensor(x_twice[:, u, :, :], x_twice[:, u, :, :], x_gru[:, u, :, :], ALU.add)\
                        .then_inc(s_x2b.sem, 1)
                for u in range(U):
                    pool.wait_ge(s_ve.sem, s_ve.now(t, u + 1))
                    nc.gpsimd.tensor_tensor(rstd[:, u, :], var_eps[:, u, :], W["minus_half"][:, 0:GT], ALU.pow)\
                        .then_inc(s_rs.sem, 1)

        @block.tensor
        def _(pe):
            credit(pe, *s_xt, s_pw, s_hg, s_ht, s_f1, s_f2)
            with pe.Fori(0, TURNS) as t:
                def transposes(k):
                    for u in range(U):
                        pe.wait_ge(s_xs[k].sem, s_xs[k].now(t, u + 1))
                        if k == 0:
                            pe.wait_ge(s_tt.sem, s_tt.before(t, u + 1))
                        for j in range(GT):
                            last = pe.transpose(ps[:, u, 0, j * P:(j + 1) * P], x_scaled[:, u, j, :], W["ident"])
                        last.then_inc(s_xt[k].sem, 1)

                transposes(0)
                for u in range(U):
                    pe.wait_ge(s_cv.sem, s_cv.now(t, 3 * u + 3))
                    for j in range(GT):
                        last = pe.matmul(ps[:, u, 0, j * P:(j + 1) * P], conv[:, u, j * P:(j + 1) * P], W["pwT"],
                                         start=True, stop=True)
                    last.then_inc(s_pw.sem, 1)
                transposes(1)
                for u in range(U):
                    pe.wait_ge(s_xn[1].sem, s_xn[1].now(t, u + 1))
                    pe.wait_ge(s_ge.sem, s_ge.before(t, 4 * u + 4))
                    pe.matmul(ps[:, u, 1, :], W["gruT"][:, 0:D], xn[:, u, :], start=True, stop=True)
                    pe.matmul(ps[:, u, 2, :], W["gruT"][:, D:2 * D], xn[:, u, :], start=True, stop=True)\
                        .then_inc(s_hg.sem, 1)
                for u in range(U):
                    pe.wait_ge(s_sc.sem, s_sc.now(t, u + 1))
                    for j in range(GT):
                        last = pe.transpose(ps[:, u, 0, j * P:(j + 1) * P], hgru[:, u, j * P:(j + 1) * P], W["ident"])
                    last.then_inc(s_ht.sem, 1)
                transposes(2)
                for u in range(U):
                    pe.wait_ge(s_xn[2].sem, s_xn[2].now(t, u + 1))
                    for c in range(4):
                        if c == 3:
                            pe.wait_ge(s_ge.sem, s_ge.now(t, 4 * u + 1))
                        pe.matmul(ps[:, u, 1 + c % 3, :], W["ff1T"][:, c * P:(c + 1) * P], xn[:, u, :],
                                  start=True, stop=True).then_inc(s_f1.sem, 1)
                for u in range(U):
                    pe.wait_ge(s_ge.sem, s_ge.now(t, 4 * u + 4))
                    for j in range(GT):
                        for c in range(4):
                            last = pe.matmul(ps[:, u, 0, j * P:(j + 1) * P], hff[:, u, c, j * P:(j + 1) * P],
                                             W["ff2T"][:, c, :], start=(c == 0), stop=(c == 3))
                    last.then_inc(s_f2.sem, 1)

        @block.vector
        def _(dve):
            credit(dve, *s_xs, *s_fl, s_ve, s_cv, s_x1, s_gr, s_sc, s_x2, s_tt, s_bs, s_mv, s_out)
            dve.wait_ge(zeroed, 2)
            with dve.Fori(0, TURNS) as t:
                def scale_rows(k, source):
                    for u in range(U):
                        dve.wait_ge(s_sq[k].sem, s_sq[k].now(t, u + 1))
                        nc.vector.tensor_scalar(floored[:, u, k, :], ssq[:, u, k, :], NORM_FLOOR, None, ALU.max)\
                            .then_inc(s_fl[k].sem, 1)
                    for u in range(U):
                        dve.wait_ge(s_rn[k].sem, s_rn[k].now(t, u + 1))
                        if k == 0:
                            dve.wait_ge(s_xt[2].sem, s_xt[2].before(t, u + 1))
                            dve.wait_ge(s_out.sem, s_out.before(t, u + 1))
                        else:
                            dve.wait_ge(s_xt[k - 1].sem, s_xt[k - 1].now(t, u + 1))
                        for j in range(GT):
                            last = nc.vector.tensor_scalar(x_scaled[:, u, j, :].unsqueeze(1), source(u, j),
                                                           rnorm[:, u, k, j:j + 1], None, ALU.mult)
                        last.then_inc(s_xs[k].sem, 1)

                scale_rows(0, lambda u, j: tile_of(t, u, j))
                for u in range(U):
                    y = conv[:, u, :].rearrange("p (b s) -> p b s", s=SEQ)
                    dve.wait_ge(s_xn[0].sem, s_xn[0].now(t, u + 1))
                    dve.wait_ge(s_pw.sem, s_pw.before(t, u + 1))
                    nc.vector.tensor_scalar(y, padded[:, u, :, 0:SEQ], W["dw"][:, 0:1], W["dw_b"], ALU.mult, ALU.add)\
                        .then_inc(s_cv.sem, 1)
                    for k in (1, 2):
                        dve.wait_ge(s_cv.sem, s_cv.now(t, 3 * u + k))
                        nc.vector.scalar_tensor_tensor(out=y, in0=padded[:, u, :, k:k + SEQ], scalar=W["dw"][:, k:k + 1],
                                                       in1=y, op0=ALU.mult, op1=ALU.add).then_inc(s_cv.sem, 1)
                for u in range(U):
                    dve.wait_ge(s_pw.sem, s_pw.now(t, u + 1))
                    dve.wait_ge(s_xb.sem, s_xb.now(t, u + 1))
                    nc.vector.tensor_tensor(x_conv[:, u, :, :], ps[:, u, 0, :].rearrange("p (j d) -> p j d", d=D),
                                            x_bias[:, u, :, :], ALU.add).then_inc(s_x1.sem, 1)
                    dve.wait_ge(s_x1.sem, s_x1.now(t, u + 1))
                scale_rows(1, lambda u, j: x_conv[:, u, j, :].unsqueeze(1))
                for u in range(U):
                    dve.wait_ge(s_sg.sem, s_sg.now(t, 2 * u + 1))
                    nc.vector.scalar_tensor_tensor(out=sig_hidden[:, u, :], in0=ps[:, u, 1, :], scalar=0.5,
                                                   in1=sig_hidden[:, u, :], op0=ALU.add, op1=ALU.max)\
                        .then_inc(s_gr.sem, 1)
                    dve.wait_ge(s_gr.sem, s_gr.now(t, 2 * u + 1))
                    dve.wait_ge(s_sg.sem, s_sg.now(t, 2 * u + 2))
                    nc.vector.tensor_tensor(update[:, u, :], update[:, u, :], sig_hidden[:, u, :], ALU.mult)\
                        .then_inc(s_gr.sem, 1)
                    dve.wait_ge(s_gr.sem, s_gr.now(t, 2 * u + 2))
                    dve.wait_ge(s_ht.sem, s_ht.before(t, u + 1))
                    nc.vector.tensor_tensor_scan(hgru[:, u, :], keep[:, u, :], update[:, u, :], 0.0, ALU.mult, ALU.add)\
                        .then_inc(s_sc.sem, 1)
                for u in range(U):
                    dve.wait_ge(s_ht.sem, s_ht.now(t, u + 1))
                    nc.vector.tensor_tensor(x_gru[:, u, :, :], ps[:, u, 0, :].rearrange("p (j d) -> p j d", d=D),
                                            x_conv[:, u, :, :], ALU.add).then_inc(s_x2.sem, 1)
                    dve.wait_ge(s_x2.sem, s_x2.now(t, u + 1))
                scale_rows(2, lambda u, j: x_gru[:, u, j, :].unsqueeze(1))
                for u in range(U):
                    dve.wait_ge(s_f2.sem, s_f2.now(t, u + 1))
                    dve.wait_ge(s_x2b.sem, s_x2b.now(t, U + u + 1))
                    nc.vector.tensor_tensor(total[:, u, :, :], ps[:, u, 0, :].rearrange("p (j d) -> p j d", d=D),
                                            x_twice[:, u, :, :], ALU.add).then_inc(s_tt.sem, 1)
                    dve.wait_ge(s_tt.sem, s_tt.now(t, u + 1))
                    for j in range(GT):
                        last = nc.vector.bn_stats(stats[:, u, j, :], total[:, u, j, :])
                    last.then_inc(s_bs.sem, 1)
                    dve.wait_ge(s_bs.sem, s_bs.now(t, u + 1))
                    nc.vector.memset(scrap[:, :], 0.0)
                    for j in range(GT):
                        last = nc.vector.bn_aggr(moments[:, u, j, :], stats[:, u, j, :])
                    last.then_inc(s_mv.sem, 1)
                    dve.wait_ge(s_mv.sem, s_mv.now(t, u + 1))
                    nc.vector.tensor_scalar(var_eps[:, u, :], moments[:, u, :, 1], LN_EPS, None, ALU.add)\
                        .then_inc(s_ve.sem, 1)
                for u in range(U):
                    dve.wait_ge(s_rs.sem, s_rs.now(t, u + 1))
                    for j in range(GT):
                        last = nc.vector.tensor_scalar(tile_of(t, u, j), total[:, u, j, :].unsqueeze(1),
                                                       moments[:, u, j, 0:1], rstd[:, u, j:j + 1],
                                                       ALU.subtract, ALU.mult)
                    last.then_inc(s_out.sem, 1)
def stage_attention(nc, X, W, layer, ctx_in):
    NT = 2
    NB = NT * SPT
    TN = NT * P
    TURNS = TILES // NT
    cross = layer == 0
    if cross:
        w_q, w_k, w_v, w_o = W["WqT"], W["WkT"], W["WvT"], W["WoT"]
    else:
        w_q, w_k, w_v, w_o = W["Wqkv"][:, 0:D], W["Wqkv"][:, D:2 * D], W["Wqkv"][:, 2 * D:], W["Wout"]
    name = f"at{layer}_"
    with ExitStack() as ctx:
        def sb(n, shape, dt=F32):
            return ctx.enter_context(nc.sbuf_tensor(name + n, shape, dt))

        def ps(n, shape):
            return ctx.enter_context(nc.psum_tensor(name + n, shape, F32))

        def sig(n, per=1):
            return Signal(ctx, nc, name + n, per)

        x_in = sb("x_in", [P, NT, D])
        c_in = sb("c_in", [P, NT, D]) if cross else None
        feats = sb("feats", [P, 2, TN])
        spread_q = sb("spread_q", [P, NB, 2, 2, SEQ])
        spread_k = sb("spread_k", [P, NB, 4, SEQ])
        spread_v = sb("spread_v", [P, NB, 2, 4, 4, HD])
        neg_max = sb("neg_max", [P, NB, 8])
        shifted = sb("shifted", [P, NB, 8, SEQ])
        probs = sb("probs", [P, NB, 8, SEQ])
        sums = sb("sums", [P, NB, 8])
        rsum = sb("rsum", [P, NB, 8])
        probs_n = sb("probs_n", [P, NB, 8, SEQ])
        probs_t = sb("probs_t", [P, NB, 2, 2 * P])
        mixed = sb("mixed", [P, NB, SEQ])
        residual = sb("residual", [P, NT, D])
        q_bias = sb("q_bias", [P, 1])
        k_bias = sb("k_bias", [P, 4])
        window = sb("window", [P, 8, SEQ], BF16) if not cross else None
        ident_b = sb("ident_b", [P, P], BF16) if not cross else None
        p_t = ps("p_t", [P, 2, TN])
        p_qk = ps("p_qk", [P, 2, TN])
        p_v = ps("p_v", [P, NB, D])
        p_s = ps("p_s", [P, 2, 8, SEQ])
        p_pt = ps("p_pt", [P, 2, 2, 2 * P])
        p_o = ps("p_o", [P, 2, 4, SEQ])
        p_y = p_o[:, 0, :, :].rearrange("p g s -> p (g s)").rearrange("p (j d) -> p j d", j=NT)

        tail = NormTail(ctx, nc, name + "tail", NT)
        constants = nc.alloc_semaphore(name + "constants")
        x_copied = sig("x_copied")
        c_landed = sig("c_landed", 16)
        turned = sig("turned")
        feats_done = sig("feats_done")
        qk_done = sig("qk_done")
        q_spread = sig("q_spread")
        k_spread_a, k_spread_v = sig("k_spread_a"), sig("k_spread_v")
        v_done = sig("v_done")
        v_spread = sig("v_spread")
        scored = sig("scored", NB)
        maxed = sig("maxed", NB)
        shift_done = sig("shift_done", NB)
        exped = sig("exped", NB)
        summed = sig("summed", NB)
        inverted = sig("inverted", NB)
        normed = sig("normed", NB)
        probs_turned = sig("probs_turned", NB)
        probs_copied = sig("probs_copied", NB)
        weighted = sig("weighted", NB)
        mixed_a, mixed_v = sig("mixed_a", 2), sig("mixed_v", 2)
        projected = sig("projected")
        residual_done = sig("residual_done")

        block = ctx.enter_context(nc.Block())
        CONSTANTS = 4 if cross else 8

        def tiles(t):
            return X[:, bass.ds(t * NT, NT), :]

        def all_turns(engine, turn):
            with engine.Fori(0, TURNS - 2) as t:
                turn(t, True, True)
            turn(TURNS - 2, True, False)
            turn(TURNS - 1, False, False)

        @block.sync
        def _(sp):
            if cross:
                def load(t):
                    sp.wait_ge(turned.sem, turned.before(t, 1))
                    sp.dma_start(c_in[:, :, :], ctx_in[bass.ds(t * TN, TN), :].rearrange("(j p) d -> p j d", p=P))\
                        .then_inc(c_landed.sem, 16)
                with sp.Fori(0, TURNS) as t:
                    load(t)
                sp.wait_ge(c_landed.sem, 16 * TURNS)

        @block.gpsimd
        def _(pool):
            nc.gpsimd.memset(spread_q[:, :, :, :, :], 0.0).then_inc(constants, 1)
            nc.gpsimd.memset(spread_v[:, :, :, :, :, :], 0.0).then_inc(constants, 1)
            if not cross:
                nc.gpsimd.tensor_copy(ident_b[:, :], W["ident"]).then_inc(constants, 1)
                nc.gpsimd.tensor_copy(window[:, :, :], W["window"].unsqueeze(1).broadcast_to((P, 8, SEQ)))\
                    .then_inc(constants, 1)
            credit(pool, x_copied, normed, residual_done)
            tail.credit_pool(pool)

            def copy_x(t):
                pool.wait_ge(turned.sem, turned.before(t, 1))
                nc.gpsimd.tensor_copy(x_in[:, :, :], tiles(t)).then_inc(x_copied.sem, 1)

            def normalise(t, b):
                pool.wait_ge(probs_turned.sem, probs_turned.before(t, b + 1))
                pool.wait_ge(inverted.sem, inverted.now(t, b + 1))
                nc.gpsimd.tensor_tensor(probs_n[:, b, :, :], probs[:, b, :, :],
                                        rsum[:, b, :].unsqueeze(2).broadcast_to((P, 8, SEQ)), ALU.mult)\
                    .then_inc(normed.sem, 1)

            def keep_residual(t):
                if cross:
                    nc.gpsimd.tensor_copy(residual[:, :, :], tiles(t)).then_inc(residual_done.sem, 1)
                else:
                    nc.gpsimd.tensor_tensor(residual[:, :, :], tiles(t), W["out_b"].unsqueeze(1).broadcast_to((P, NT, D)),
                                            ALU.add).then_inc(residual_done.sem, 1)

            def turn(t, one, two):
                if two:
                    copy_x(t + 2)
                if one:
                    for b in range(NB - 1):
                        normalise(t + 1, b)
                keep_residual(t)
                tail.root_pool(pool, t, W["minus_half"])
                if one:
                    normalise(t + 1, NB - 1)

            copy_x(0)
            copy_x(1)
            for b in range(NB):
                normalise(0, b)
            all_turns(pool, turn)

        @block.tensor
        def _(pe):
            credit(pe, turned, qk_done, v_done, scored, probs_turned, weighted, projected)
            pe.wait_ge(constants, CONSTANTS)

            def transposes(t):
                pe.wait_ge(x_copied.sem, x_copied.now(t, 1))
                pe.wait_ge(feats_done.sem, feats_done.before(t, 1))
                for j in range(NT):
                    last = pe.transpose(p_t[:, 0, j * P:(j + 1) * P], x_in[:, j, :], W["ident"])
                if cross:
                    pe.wait_ge(c_landed.sem, (t + 1) * 16)
                    for j in range(NT):
                        last = pe.transpose(p_t[:, 1, j * P:(j + 1) * P], c_in[:, j, :], W["ident"])
                last.then_inc(turned.sem, 1)

            def queries_keys(t):
                pe.wait_ge(feats_done.sem, feats_done.now(t, 1))
                pe.wait_ge(q_spread.sem, q_spread.before(t, 1))
                pe.wait_ge(k_spread_a.sem, k_spread_a.before(t, 1))
                pe.wait_ge(k_spread_v.sem, k_spread_v.before(t, 1))
                pe.matmul(p_qk[:, 0, :], w_q, feats[:, 0, :], start=True, stop=True)
                pe.matmul(p_qk[:, 1, :], w_k, feats[:, 1 if cross else 0, :], start=True, stop=True)\
                    .then_inc(qk_done.sem, 1)

            def values(t):
                pe.wait_ge(v_spread.sem, v_spread.before(t, 1))
                for b in range(NB):
                    kv = feats[:, 1 if cross else 0, b * SEQ:(b + 1) * SEQ]
                    for half in range(2):
                        last = pe.matmul(p_v[SEQ * half:SEQ * half + SEQ, b, :], kv, w_v, start=True, stop=True)
                last.then_inc(v_done.sem, 1)

            def scores(t, b):
                if b == 0:
                    pe.wait_ge(q_spread.sem, q_spread.now(t, 1))
                    pe.wait_ge(k_spread_a.sem, k_spread_a.now(t, 1))
                    pe.wait_ge(k_spread_v.sem, k_spread_v.now(t, 1))
                pe.wait_ge(shift_done.sem, shift_done.now(t, b - 1) if b >= 2 else shift_done.before(t, b + 3))
                if not cross:
                    pe.matmul(p_s[:, b % 2, :, :], ident_b[:, :], window[:, :, :], start=True, stop=False,
                              skip_group_check=True)
                for half in range(2):
                    last = pe.matmul(p_s[:, b % 2, 4 * half:4 * half + 4, :], spread_q[:, b, half, :, :],
                                     spread_k[:, b, :, :], start=cross, stop=True, skip_group_check=True)
                last.then_inc(scored.sem, 1)

            def turn_probs(t, b):
                pe.wait_ge(normed.sem, normed.now(t, b + 1))
                pe.wait_ge(probs_copied.sem, probs_copied.now(t, b - 1) if b >= 2 else probs_copied.before(t, b + 3))
                for g2 in range(2):
                    for j2 in range(2):
                        last = pe.transpose(p_pt[:, b % 2, j2, g2 * P:(g2 + 1) * P],
                                            probs_n[:, b, 4 * g2 + 2 * j2:4 * g2 + 2 * j2 + 2, :], W["ident"])
                last.then_inc(probs_turned.sem, 1)

            def weigh(t, b):
                pe.wait_ge(probs_copied.sem, probs_copied.now(t, b + 1))
                if b == 0:
                    pe.wait_ge(v_spread.sem, v_spread.now(t, 1))
                    pe.wait_ge(tail.added.sem, tail.added.before(t, 1))
                if b % 2 == 0:
                    for m in (mixed_a, mixed_v):
                        pe.wait_ge(m.sem, m.now(t, 1) if b else m.before(t, 2))
                for j2 in range(2):
                    last = pe.matmul(p_o[:, b % 2, :, :], spread_v[:, b, j2, :, :, :], probs_t[:, b, j2, :],
                                     start=(j2 == 0), stop=(j2 == 1))
                last.then_inc(weighted.sem, 1)

            def project(t):
                pe.wait_ge(mixed_a.sem, mixed_a.now(t, 2))
                pe.wait_ge(mixed_v.sem, mixed_v.now(t, 2))
                for j in range(NT):
                    last = pe.matmul(p_y[:, j, :], mixed[:, SPT * j:SPT * j + SPT, :], w_o, start=True, stop=True)
                last.then_inc(projected.sem, 1)

            def turn(t, one, two):
                turn_probs(t, 0)
                if one:
                    scores(t + 1, 1)
                turn_probs(t, 1)
                weigh(t, 0)
                if one:
                    scores(t + 1, 2)
                    values(t + 1)
                if two:
                    transposes(t + 2)
                turn_probs(t, 2)
                weigh(t, 1)
                if one:
                    scores(t + 1, 3)
                if two:
                    queries_keys(t + 2)
                turn_probs(t, 3)
                weigh(t, 2)
                weigh(t, 3)
                if two:
                    scores(t + 2, 0)
                project(t)

            transposes(0)
            queries_keys(0)
            for b in range(NB):
                scores(0, b)
            values(0)
            transposes(1)
            queries_keys(1)
            scores(1, 0)
            all_turns(pe, turn)

        @block.scalar
        def _(act):
            credit(act, feats_done, q_spread, k_spread_a, v_spread, exped, probs_copied, mixed_a)
            act.wait_ge(constants, CONSTANTS)

            def copy_feats(t):
                n = 2 if cross else 1
                act.wait_ge(turned.sem, turned.now(t, 1))
                act.wait_ge(v_done.sem, v_done.before(t, 1))
                nc.scalar.activation(feats[:, 0:n, :], p_t[:, 0:n, :], ACT.Copy).then_inc(feats_done.sem, 1)

            def spread(t):
                act.wait_ge(scored.sem, scored.before(t, NB))
                act.wait_ge(qk_done.sem, qk_done.now(t, 1))
                nc.scalar.activation(spread_k[:, :, 0, :], p_qk[:, 1, :].rearrange("p (b s) -> p b s", s=SEQ),
                                     ACT.Identity, bias=k_bias[:, 0:1], scale=W["head_mask"][:, 0:1])\
                    .then_inc(k_spread_a.sem, 1)
                for g in range(4):
                    r = slice(32 * g, 32 * g + 32)
                    last = nc.scalar.activation(spread_q[r, :, g // 2, g % 2, :],
                                                p_qk[r, 0, :].rearrange("p (b s) -> p b s", s=SEQ), ACT.Identity,
                                                bias=q_bias[r, :], scale=HD ** -0.5)
                last.then_inc(q_spread.sem, 1)

            def spread_values(t):
                act.wait_ge(v_done.sem, v_done.now(t, 1))
                act.wait_ge(weighted.sem, weighted.before(t, NB))
                for half in range(2):
                    r = slice(SEQ * half, SEQ * half + SEQ)
                    values = p_v[r, :, :].rearrange("p b (g j d) -> p b g j d", g=4, j=4)
                    for j2 in range(2):
                        last = nc.scalar.activation(spread_v[r, :, j2, :, 2 * j2 + half, :], values[:, :, :, 2 * j2 + half, :],
                                                    ACT.Copy)
                last.then_inc(v_spread.sem, 1)

            def exp(t, b):
                act.wait_ge(normed.sem, normed.before(t, b + 1))
                act.wait_ge(shift_done.sem, shift_done.now(t, b + 1))
                nc.scalar.activation(probs[:, b, :, :], shifted[:, b, :, :], ACT.Exp).then_inc(exped.sem, 1)

            def copy_probs(t, b):
                act.wait_ge(weighted.sem, weighted.before(t, b + 1))
                act.wait_ge(probs_turned.sem, probs_turned.now(t, b + 1))
                nc.scalar.activation(probs_t[:, b, :, :], p_pt[:, b % 2, :, :], ACT.Copy).then_inc(probs_copied.sem, 1)

            def copy_mixed(t, pair):
                act.wait_ge(projected.sem, projected.before(t, 1))
                act.wait_ge(weighted.sem, weighted.now(t, 2 * pair + 2))
                for g in range(2):
                    r = slice(32 * g, 32 * g + 32)
                    last = nc.scalar.activation(mixed[r, 2 * pair:2 * pair + 2, :], p_o[r, :, g, :], ACT.Identity,
                                                bias=(0.0 if cross else W["v_b"][r, :]))
                last.then_inc(mixed_a.sem, 1)

            def turn(t, one, two):
                copy_probs(t, 0)
                spread_values(t)
                if one:
                    exp(t + 1, 0)
                copy_probs(t, 1)
                if one:
                    exp(t + 1, 1)
                if two:
                    copy_feats(t + 2)
                copy_probs(t, 2)
                copy_mixed(t, 0)
                if one:
                    exp(t + 1, 2)
                if two:
                    spread(t + 2)
                copy_probs(t, 3)
                if one:
                    exp(t + 1, 3)
                copy_mixed(t, 1)

            copy_feats(0)
            spread(0)
            for b in range(NB):
                exp(0, b)
            copy_feats(1)
            spread(1)
            all_turns(act, turn)

        @block.vector
        def _(dve):
            if cross:
                nc.vector.memset(q_bias[:, :], 0.0).then_inc(constants, 1)
                nc.vector.memset(k_bias[:, :], 0.0).then_inc(constants, 1)
            else:
                nc.vector.tensor_scalar(q_bias[:, :], W["qk_b"][:, 0:1], HD ** -0.5, None, ALU.mult).then_inc(constants, 2)
                nc.vector.tensor_scalar(k_bias[:, :], W["head_mask"], W["qk_b"][:, 1:2], None, ALU.mult).then_inc(constants, 2)
            credit(dve, k_spread_v, maxed, shift_done, summed, inverted, mixed_v)
            tail.credit_vector(dve)
            dve.wait_ge(constants, CONSTANTS)

            def spread_keys(t):
                dve.wait_ge(scored.sem, scored.before(t, NB))
                dve.wait_ge(qk_done.sem, qk_done.now(t, 1))
                dve.wait_ge(k_spread_a.sem, k_spread_a.now(t, 1))
                dve.wait_ge(q_spread.sem, q_spread.now(t, 1))
                for j in range(1, 4):
                    last = nc.vector.tensor_scalar(spread_k[:, :, j, :], p_qk[:, 1, :].rearrange("p (b s) -> p b s", s=SEQ),
                                                   W["head_mask"][:, j:j + 1], k_bias[:, j:j + 1], ALU.mult, ALU.add)
                last.then_inc(k_spread_v.sem, 1)

            def shift(t, b):
                dve.wait_ge(scored.sem, scored.now(t, b + 1))
                nc.vector.tensor_reduce(neg_max[:, b, :], p_s[:, b % 2, :, :], AX_X, ALU.max, negate=True)\
                    .then_inc(maxed.sem, 1)
                dve.wait_ge(maxed.sem, maxed.now(t, b + 1))
                dve.wait_ge(exped.sem, exped.before(t, b + 1))
                nc.vector.tensor_tensor(shifted[:, b, :, :], p_s[:, b % 2, :, :],
                                        neg_max[:, b, :].unsqueeze(2).broadcast_to((P, 8, SEQ)), ALU.add)\
                    .then_inc(shift_done.sem, 1)

            def sum_up(t, b):
                dve.wait_ge(exped.sem, exped.now(t, b + 1))
                nc.vector.tensor_reduce(sums[:, b, :], probs[:, b, :, :], AX_X, ALU.add).then_inc(summed.sem, 1)
                dve.wait_ge(summed.sem, summed.now(t, b + 1))
                dve.wait_ge(normed.sem, normed.before(t, b + 1))
                nc.vector.reciprocal(rsum[:, b, :], sums[:, b, :]).then_inc(inverted.sem, 1)

            def copy_mixed(t, pair):
                dve.wait_ge(projected.sem, projected.before(t, 1))
                dve.wait_ge(weighted.sem, weighted.now(t, 2 * pair + 2))
                for g in (2, 3):
                    r = slice(32 * g, 32 * g + 32)
                    out, src = mixed[r, 2 * pair:2 * pair + 2, :], p_o[r, :, g, :]
                    if cross:
                        last = nc.vector.tensor_copy(out, src)
                    else:
                        last = nc.vector.tensor_scalar(out, src, W["v_b"][r, :], None, ALU.add)
                last.then_inc(mixed_v.sem, 1)

            def turn(t, one, two):
                if one:
                    shift(t + 1, 1)
                    sum_up(t + 1, 0)
                    shift(t + 1, 2)
                    sum_up(t + 1, 1)
                copy_mixed(t, 0)
                if one:
                    shift(t + 1, 3)
                if two:
                    spread_keys(t + 2)
                if one:
                    sum_up(t + 1, 2)
                copy_mixed(t, 1)
                if two:
                    shift(t + 2, 0)
                dve.wait_ge(residual_done.sem, residual_done.now(t, 1))
                dve.wait_ge(projected.sem, projected.now(t, 1))
                tail.moments_vector(dve, t, p_y[:, :, :], residual[:, :, :])
                if one:
                    sum_up(t + 1, 3)
                tail.write_vector(dve, t, lambda j: X[:, bass.ds(t * NT + j, 1), :])

            spread_keys(0)
            shift(0, 0)
            for b in range(1, NB):
                shift(0, b)
                sum_up(0, b - 1)
            sum_up(0, NB - 1)
            spread_keys(1)
            shift(1, 0)
            all_turns(dve, turn)
def stage_soft_mixture(nc, X, W):
    C = SLOTS // P
    NH = C * SPT
    RING = 4
    TURNS = TILES
    ROOT = float(D) ** 0.5
    HI, LO = 0, 1
    with ExitStack() as ctx:
        def sb(n, shape, dt=F32):
            return ctx.enter_context(nc.sbuf_tensor("sm_" + n, shape, dt))

        def ps(n, shape):
            return ctx.enter_context(nc.psum_tensor("sm_" + n, shape, F32))

        def sig(n, per=1):
            return Signal(ctx, nc, "sm_" + n, per)

        slots_t = sb("slots_t", [P, SLOTS])
        slots_p = sb("slots_p", [P, 2, SLOTS], F32R)
        w1_p = sb("w1_p", [P, 2, HIDDEN], F32R)
        slot_sq = sb("slot_sq", [P, 2, C])
        slot_rn = sb("slot_rn", [P, C])
        slots_n = sb("slots_n", [P, C, D])
        gain_x = sb("gain_x", [P, 1])
        gain_s = sb("gain_s", [P, 1])
        squares = sb("squares", [P, D])
        ssq = sb("ssq", [P, 1])
        floor_ssq = sb("floor_ssq", [P, 1])
        rnorm = sb("rnorm", [P, 1])
        x_scaled = sb("x_scaled", [P, D])
        x_t = sb("x_t", [P, P])
        x_p = sb("x_p", [P, 2, 2, 2 * P], F32R)
        xw = sb("xw", [P, 2, SPT, 2, HIDDEN], F32R)
        neg_max = sb("neg_max", [P, 1 + NH])
        shifted = sb("shifted", [P, 2, SLOTS])
        exps = sb("exps", [P, 2, SLOTS])
        sums = sb("sums", [P, 1 + NH])
        rsums = sb("rsums", [P, 2, 1 + NH])
        combine_t = sb("combine_t", [P, 2, C, P])
        dispatch = sb("dispatch", [P, 2, SPT, SLOTS], F32R)
        hidden = sb("hidden", [P, RING, HIDDEN])
        gathered = sb("gathered", [P, HIDDEN])
        gathered_t = sb("gathered_t", [P, C, P])
        residual = sb("residual", [P, 1, D])
        p_x = ps("p_x", [P, 4, P])
        p_l = ps("p_l", [P, SLOTS])
        p_lt = ps("p_lt", [P, C, P])
        p_tr = ps("p_tr", [P, C, P])
        p_xw = ps("p_xw", [P, HIDDEN])
        p_h = ps("p_h", [P, 2, HIDDEN])
        p_g = ps("p_g", [P, HIDDEN])

        tail = NormTail(ctx, nc, "sm_tail", 1)
        prep = nc.alloc_semaphore("sm_prep")
        prep_v = nc.alloc_semaphore("sm_prep_v")
        parts_hi = nc.alloc_semaphore("sm_parts_hi")
        parts_lo = nc.alloc_semaphore("sm_parts_lo")
        squared = sig("squared")
        floored = sig("floored")
        rooted = sig("rooted")
        scaled = sig("scaled")
        x_turned = sig("x_turned")
        x_ready = sig("x_ready")
        x_low_ready = sig("x_low_ready")
        xw_done = sig("xw_done", SPT)
        xw_high = sig("xw_high", SPT)
        xw_low = sig("xw_low", SPT)
        logits_done = sig("logits_done")
        logits_t_done = sig("logits_t_done")
        maxed = sig("maxed", 2)
        shift_done = sig("shift_done", 2)
        exped = sig("exped")
        summed = sig("summed")
        inverted = sig("inverted")
        exps_turned = sig("exps_turned", 2)
        combine_ready = sig("combine_ready")
        dispatch_high = sig("dispatch_high", SPT)
        dispatch_low = sig("dispatch_low", SPT)
        h_done = sig("h_done", NH)
        gelu_done = sig("gelu_done", NH)
        mixed = sig("mixed", NH)
        gathered_ready = sig("gathered_ready")
        gathered_turned = sig("gathered_turned")
        gathered_t_ready = sig("gathered_t_ready")
        y_done = sig("y_done")
        residual_done = sig("residual_done")

        block = ctx.enter_context(nc.Block())

        def tile(t):
            return X[:, bass.ds(t, 1), :]

        def rows(b):
            return slice(SEQ * b, SEQ * b + SEQ)

        def all_turns(engine, turn):
            with engine.Fori(0, TURNS // 2 - 2) as k:
                turn(2 * k, 0, True, True, True)
                turn(2 * k + 1, 1, True, True, True)
            turn(TURNS - 4, 0, True, True, True)
            turn(TURNS - 3, 1, True, True, False)
            turn(TURNS - 2, 0, True, False, False)
            turn(TURNS - 1, 1, False, False, False)

        @block.gpsimd
        def _(pool):
            credit(pool, rooted, residual_done)
            tail.credit_pool(pool)
            pool.wait_ge(prep_v, 1)
            nc.gpsimd.tensor_tensor(slot_rn[:, :], slot_sq[:, 1, :], W["minus_half"][:, 0:C], ALU.pow).then_inc(prep, 1)

            def root(t):
                pool.wait_ge(scaled.sem, scaled.before(t, 1))
                pool.wait_ge(floored.sem, floored.now(t, 1))
                nc.gpsimd.tensor_tensor(rnorm[:, :], floor_ssq[:, :], W["minus_half"][:, 0:1], ALU.pow)\
                    .then_inc(rooted.sem, 1)

            def turn(t, par, one, two, three):
                pool.wait_ge(tail.added.sem, tail.added.before(t, 1))
                nc.gpsimd.tensor_copy(residual[:, :, :], tile(t)).then_inc(residual_done.sem, 1)
                if three:
                    root(t + 3)
                tail.root_pool(pool, t, W["minus_half"])

            root(0)
            root(1)
            root(2)
            all_turns(pool, turn)

        @block.scalar
        def _(act):
            credit(act, squared, x_ready, exped, xw_high, dispatch_high, gelu_done)
            nc.scalar.activation(w1_p[:, HI, :], W["moe_w1"], ACT.Copy).then_inc(parts_hi, 1)
            for c in range(C):
                last = nc.scalar.activation(slots_n[:, c, :], W["slots"][:, c, :], ACT.Square,
                                            accum_out=slot_sq[:, 0, c:c + 1])
            last.then_inc(prep, 1)
            act.wait_ge(prep, 3)
            act.wait_ge(prep_v, 4)
            nc.scalar.activation(slots_t[:, :], p_l[:, :], ACT.Copy, scale=gain_s[:, :]).then_inc(prep, 1)
            act.wait_ge(prep, 4)
            nc.scalar.activation(slots_p[:, HI, :], slots_t[:, :], ACT.Copy).then_inc(parts_hi, 1)

            def square(t):
                act.wait_ge(floored.sem, floored.before(t, 1))
                nc.scalar.activation(squares[:, :].unsqueeze(1), tile(t), ACT.Square, accum_out=ssq[:, :])\
                    .then_inc(squared.sem, 1)

            def x_copy(t, par, first=False, fenced=True):
                act.wait_ge(x_turned.sem, x_turned.now(t, 1))
                act.wait_ge(logits_t_done.sem, logits_t_done.before(t, 1))
                if not first:
                    act.wait_ge(xw_done.sem, xw_done.before(t - 1, SPT))
                if fenced:
                    act.wait_ge(tail.added.sem, tail.added.before(t - 2, 1))
                twice = p_x[:, 0, :].rearrange("p (b s) -> p b s", s=SEQ).unsqueeze(2).broadcast_to((P, SPT, 2, SEQ))
                nc.scalar.activation(x_t[:, :], p_x[:, 0, :], ACT.Copy, scale=gain_x[:, :])
                nc.scalar.activation(x_p[:, par, HI, :].rearrange("p (b k s) -> p b k s", b=SPT, k=2), twice, ACT.Copy,
                                     scale=gain_x[:, :]).then_inc(x_ready.sem, 1)

            def exp(t):
                act.wait_ge(exps_turned.sem, exps_turned.before(t, 2))
                act.wait_ge(summed.sem, summed.before(t, 1))
                act.wait_ge(inverted.sem, inverted.before(t, 1))
                act.wait_ge(shift_done.sem, shift_done.now(t, 2))
                nc.scalar.activation(exps[:, 0, :], shifted[:, 0, :], ACT.Exp, accum_out=sums[:, 0:1])
                nc.scalar.activation(exps[:, 1, :], shifted[:, 1, :], ACT.Exp).then_inc(exped.sem, 1)

            def xw_copy(t, par, b, first=False):
                if not first:
                    act.wait_ge(h_done.sem, h_done.before(t - 1, NH))
                act.wait_ge(xw_done.sem, xw_done.now(t, b + 1))
                nc.scalar.activation(xw[:, par, b, HI, :], p_xw[:, :], ACT.Copy).then_inc(xw_high.sem, 1)

            def dispatch_copy(t, par, b, first=False):
                if not first:
                    act.wait_ge(h_done.sem, h_done.before(t - 1, NH))
                act.wait_ge(exps_turned.sem, exps_turned.now(t, 2))
                nc.scalar.activation(dispatch[rows(b), par, b, :], p_lt[rows(b), :, :].rearrange("p c s -> p (c s)"), ACT.Copy)\
                    .then_inc(dispatch_high.sem, 1)

            def gelu(t, par, i):
                if i == 0:
                    act.wait_ge(inverted.sem, inverted.now(t, 1))
                act.wait_ge(mixed.sem, mixed.now(t, i - RING + 1) if i >= RING else mixed.before(t, NH - RING + i + 1))
                act.wait_ge(h_done.sem, h_done.now(t, i + 1))
                nc.scalar.activation(hidden[:, i % RING, :], p_h[:, i % 2, :], ACT.Gelu, scale=rsums[:, par, 1 + i:2 + i])\
                    .then_inc(gelu_done.sem, 1)

            def turn(t, par, one, two, three):
                for i in range(NH):
                    gelu(t, par, i)
                    if i == 0 and one:
                        dispatch_copy(t + 1, 1 - par, 0)
                    if i == 1 and one:
                        dispatch_copy(t + 1, 1 - par, 1)
                    if i == 1 and two:
                        x_copy(t + 2, par)
                    if i == 2 and one:
                        xw_copy(t + 1, 1 - par, 0)
                    if i == 3 and three:
                        square(t + 3)
                    if i == 7 and one:
                        xw_copy(t + 1, 1 - par, 1)
                if two:
                    exp(t + 2)

            square(0)
            x_copy(0, 0, True, False)
            square(1)
            xw_copy(0, 0, 0, True)
            xw_copy(0, 0, 1, True)
            exp(0)
            dispatch_copy(0, 0, 0, True)
            dispatch_copy(0, 0, 1, True)
            x_copy(1, 1, fenced=False)
            square(2)
            exp(1)
            all_turns(act, turn)

        @block.tensor
        def _(pe):
            credit(pe, x_turned, xw_done, logits_done, logits_t_done, exps_turned, h_done, mixed, gathered_turned, y_done)
            pe.wait_ge(prep_v, 3)
            for c in range(C):
                last = pe.transpose(p_l[:, c * P:(c + 1) * P], slots_n[:, c, :], W["ident"])
            last.then_inc(prep, 1)
            pe.wait_ge(parts_lo, 2)

            def three_passes(out, left_hi, left_lo, right):
                pe.matmul(out, left_hi, right[:, HI, :], start=True, stop=False)
                pe.matmul(out, left_lo, right[:, HI, :], start=False, stop=False)
                return pe.matmul(out, left_hi, right[:, LO, :], start=False, stop=True)

            def x_transpose(t, first=False):
                pe.wait_ge(scaled.sem, scaled.now(t, 1))
                pe.wait_ge(x_low_ready.sem, x_low_ready.before(t, 1))
                if not first:
                    pe.wait_ge(tail.added.sem, tail.added.before(t - 3, 1))
                pe.transpose(p_x[:, 0, :], x_scaled[:, :], W["ident"]).then_inc(x_turned.sem, 1)

            def times_w1(t, par, b):
                pe.wait_ge(x_low_ready.sem, x_low_ready.now(t, 1))
                pe.wait_ge(xw_low.sem, xw_low.now(t, 1) if b else xw_low.before(t, SPT))
                cols = slice(P * b, P * b + P)
                three_passes(p_xw[:, :], x_p[:, par, HI, cols], x_p[:, par, LO, cols], w1_p).then_inc(xw_done.sem, 1)

            def logits(t, par, first=False):
                pe.wait_ge(x_low_ready.sem, x_low_ready.now(t, 1))
                if not first:
                    pe.wait_ge(combine_ready.sem, combine_ready.before(t, 1))
                    pe.wait_ge(dispatch_low.sem, dispatch_low.before(t, SPT))
                cols = slice(SEQ, SEQ + P)
                three_passes(p_l[:, :], x_p[:, par, HI, cols], x_p[:, par, LO, cols], slots_p).then_inc(logits_done.sem, 1)
                for c in range(C):
                    last = pe.matmul(p_lt[:, c, :], slots_t[:, c * P:(c + 1) * P], x_t[:, :], start=True, stop=True)
                last.then_inc(logits_t_done.sem, 1)

            def exps_transpose(t):
                pe.wait_ge(exped.sem, exped.now(t, 1))
                for k in range(2):
                    for c in range(C):
                        out = p_lt[:, c, :] if k else p_l[:, c * P:(c + 1) * P]
                        last = pe.transpose(out, exps[:, k, c * P:(c + 1) * P], W["ident"])
                    last.then_inc(exps_turned.sem, 1)

            def hidden_block(t, par, i):
                c, b = i // SPT, i % SPT
                if i < SPT:
                    pe.wait_ge(xw_low.sem, xw_low.now(t, b + 1))
                    pe.wait_ge(dispatch_low.sem, dispatch_low.now(t, b + 1))
                pe.wait_ge(gelu_done.sem, gelu_done.now(t, i - 1) if i >= 2 else gelu_done.before(t, NH - 1 + i))
                for part in (HI, LO):
                    last = pe.matmul(p_h[:, i % 2, :], dispatch[:, par, b, c * P:(c + 1) * P], xw[:, par, b, part, :],
                                     start=(part == HI), stop=(part == LO))
                last.then_inc(h_done.sem, 1)

            def gather_block(t, par, i):
                c, b = i // SPT, i % SPT
                if i == 0:
                    pe.wait_ge(combine_ready.sem, combine_ready.now(t, 1))
                    pe.wait_ge(gathered_ready.sem, gathered_ready.before(t, 1))
                pe.wait_ge(gelu_done.sem, gelu_done.now(t, i + 1))
                pe.matmul(p_g[rows(b), :], combine_t[:, par, c, rows(b)], hidden[:, i % RING, :], start=(c == 0),
                          stop=(c == C - 1)).then_inc(mixed.sem, 1)

            def turn(t, par, one, two, three):
                hidden_block(t, par, 2)
                hidden_block(t, par, 3)
                gather_block(t, par, 0)
                gather_block(t, par, 1)
                hidden_block(t, par, 4)
                hidden_block(t, par, 5)
                gather_block(t, par, 2)
                gather_block(t, par, 3)
                hidden_block(t, par, 6)
                if two:
                    logits(t + 2, par)
                hidden_block(t, par, 7)
                if one:
                    times_w1(t + 1, 1 - par, 1)
                gather_block(t, par, 4)
                gather_block(t, par, 5)
                gather_block(t, par, 6)
                gather_block(t, par, 7)
                if one:
                    hidden_block(t + 1, 1 - par, 0)
                pe.wait_ge(gathered_t_ready.sem, gathered_t_ready.before(t, 1))
                pe.wait_ge(gathered_ready.sem, gathered_ready.now(t, 1))
                for c in range(C):
                    last = pe.transpose(p_tr[:, c, :], gathered[:, c * P:(c + 1) * P], W["ident"])
                last.then_inc(gathered_turned.sem, 1)
                if one:
                    hidden_block(t + 1, 1 - par, 1)
                if two:
                    times_w1(t + 2, par, 0)
                if three:
                    x_transpose(t + 3)
                if two:
                    exps_transpose(t + 2)
                pe.wait_ge(gathered_t_ready.sem, gathered_t_ready.now(t, 1))
                for c in range(C):
                    last = pe.matmul(p_x[:, 1, :], gathered_t[:, c, :], W["moe_w2"][:, c, :], start=(c == 0),
                                     stop=(c == C - 1))
                last.then_inc(y_done.sem, 1)

            x_transpose(0, True)
            times_w1(0, 0, 0)
            logits(0, 0, True)
            x_transpose(1, True)
            times_w1(0, 0, 1)
            exps_transpose(0)
            logits(1, 1)
            times_w1(1, 1, 0)
            x_transpose(2, True)
            hidden_block(0, 0, 0)
            hidden_block(0, 0, 1)
            exps_transpose(1)
            all_turns(pe, turn)

        @block.vector
        def _(dve):
            credit(dve, floored, scaled, x_low_ready, xw_low, maxed, shift_done, summed, inverted, combine_ready,
                   dispatch_low, gathered_ready, gathered_t_ready)
            tail.credit_vector(dve)
            dve.wait_ge(prep, 1)
            nc.vector.tensor_scalar(slot_sq[:, 1, :], slot_sq[:, 0, :], NORM_FLOOR, None, ALU.max).then_inc(prep_v, 1)
            dve.wait_ge(prep, 2)
            for c in range(C):
                last = nc.vector.tensor_scalar(slots_n[:, c, :], W["slots"][:, c, :], slot_rn[:, c:c + 1], None, ALU.mult)
            last.then_inc(prep_v, 2)
            nc.vector.tensor_scalar(gain_x[:, :], W["gamma_x"], ROOT, None, ALU.mult)
            nc.vector.tensor_scalar(gain_s[:, :], W["gamma_slot"], ROOT, None, ALU.mult).then_inc(prep_v, 1)
            dve.wait_ge(parts_hi, 1)
            nc.vector.tensor_tensor(w1_p[:, LO, :], W["moe_w1"], w1_p[:, HI, :].bitcast(F32), ALU.subtract).then_inc(parts_lo, 1)
            dve.wait_ge(parts_hi, 2)
            nc.vector.tensor_tensor(slots_p[:, LO, :], slots_t[:, :], slots_p[:, HI, :].bitcast(F32), ALU.subtract)\
                .then_inc(parts_lo, 1)

            def floor_row(t):
                dve.wait_ge(squared.sem, squared.now(t, 1))
                dve.wait_ge(rooted.sem, rooted.before(t, 1))
                nc.vector.tensor_scalar(floor_ssq[:, :], ssq[:, :], NORM_FLOOR, None, ALU.max).then_inc(floored.sem, 1)

            def scale_row(t):
                dve.wait_ge(x_turned.sem, x_turned.before(t, 1))
                dve.wait_ge(rooted.sem, rooted.now(t, 1))
                nc.vector.tensor_scalar(x_scaled[:, :].unsqueeze(1), tile(t), rnorm[:, :], None, ALU.mult)\
                    .then_inc(scaled.sem, 1)

            def x_low(t, par):
                dve.wait_ge(x_ready.sem, x_ready.now(t, 1))
                hi, lo = (x_p[:, par, k, :].rearrange("p (b k s) -> p b k s", b=SPT, k=2) for k in (HI, LO))
                for b in range(SPT):
                    twice = p_x[:, 0, SEQ * b:SEQ * b + SEQ].unsqueeze(1).broadcast_to((P, 2, SEQ))
                    last = nc.vector.scalar_tensor_tensor(out=lo[:, b, :, :], in0=twice, scalar=gain_x[:, :],
                                                          in1=hi[:, b, :, :].bitcast(F32), op0=ALU.mult, op1=ALU.subtract)
                last.then_inc(x_low_ready.sem, 1)

            def xw_rest(t, par, b):
                dve.wait_ge(xw_high.sem, xw_high.now(t, b + 1))
                nc.vector.tensor_tensor(xw[:, par, b, LO, :], p_xw[:, :], xw[:, par, b, HI, :].bitcast(F32), ALU.subtract)\
                    .then_inc(xw_low.sem, 1)

            def dispatch_rest(t, par, b):
                dve.wait_ge(dispatch_high.sem, dispatch_high.now(t, b + 1))
                nc.vector.tensor_tensor(dispatch[rows(1 - b), par, b, :], p_lt[rows(b), :, :].rearrange("p c s -> p (c s)"),
                                        dispatch[rows(b), par, b, :].bitcast(F32), ALU.subtract).then_inc(dispatch_low.sem, 1)

            def shift(t):
                dve.wait_ge(exped.sem, exped.before(t, 1))
                dve.wait_ge(logits_done.sem, logits_done.now(t, 1))
                nc.vector.tensor_reduce(neg_max[:, 0:1], p_l[:, :], AX_X, ALU.max, negate=True).then_inc(maxed.sem, 1)
                dve.wait_ge(maxed.sem, maxed.now(t, 1))
                nc.vector.tensor_scalar(shifted[:, 0, :], p_l[:, :], neg_max[:, 0:1], None, ALU.add)\
                    .then_inc(shift_done.sem, 1)
                logits_t = p_lt[:, :, :].rearrange("p c (b s) -> p (c b) s", s=SEQ)
                dve.wait_ge(logits_t_done.sem, logits_t_done.now(t, 1))
                nc.vector.tensor_reduce(neg_max[:, 1:], logits_t, AX_X, ALU.max, negate=True).then_inc(maxed.sem, 1)
                dve.wait_ge(maxed.sem, maxed.now(t, 2))
                nc.vector.tensor_tensor(shifted[:, 1, :].rearrange("p (c s) -> p c s", s=SEQ), logits_t,
                                        neg_max[:, 1:].unsqueeze(2).broadcast_to((P, NH, SEQ)), ALU.add)\
                    .then_inc(shift_done.sem, 1)

            def sum_up(t, par, first=False):
                dve.wait_ge(inverted.sem, inverted.before(t, 1))
                dve.wait_ge(exped.sem, exped.now(t, 1))
                nc.vector.tensor_reduce(sums[:, 1:], exps[:, 1, :].rearrange("p (c s) -> p c s", s=SEQ), AX_X, ALU.add)\
                    .then_inc(summed.sem, 1)
                if not first:
                    dve.wait_ge(gelu_done.sem, gelu_done.before(t - 1, NH))
                    dve.wait_ge(gathered_ready.sem, gathered_ready.before(t - 1, 1))
                dve.wait_ge(summed.sem, summed.now(t, 1))
                nc.vector.reciprocal(rsums[:, par, :], sums[:, :]).then_inc(inverted.sem, 1)

            def combine_copy(t, par, first=False):
                if not first:
                    dve.wait_ge(mixed.sem, mixed.before(t - 1, NH))
                dve.wait_ge(exps_turned.sem, exps_turned.now(t, 1))
                nc.vector.tensor_copy(combine_t[:, par, :, :], p_l[:, :].rearrange("p (c s) -> p c s", s=P))\
                    .then_inc(combine_ready.sem, 1)

            def turn(t, par, one, two, three):
                if two:
                    x_low(t + 2, par)
                if one:
                    xw_rest(t + 1, 1 - par, 0)
                if three:
                    floor_row(t + 3)
                if two:
                    shift(t + 2)
                if three:
                    scale_row(t + 3)
                if one:
                    xw_rest(t + 1, 1 - par, 1)
                dve.wait_ge(gathered_turned.sem, gathered_turned.before(t, 1))
                dve.wait_ge(mixed.sem, mixed.now(t, NH))
                nc.vector.tensor_scalar(gathered[:, :], p_g[:, :], rsums[:, par, 0:1], None, ALU.mult)                    .then_inc(gathered_ready.sem, 1)
                dve.wait_ge(y_done.sem, y_done.before(t, 1))
                dve.wait_ge(gathered_turned.sem, gathered_turned.now(t, 1))
                nc.vector.tensor_copy(gathered_t[:, :, :], p_tr[:, :, :]).then_inc(gathered_t_ready.sem, 1)
                if two:
                    sum_up(t + 2, par)
                    combine_copy(t + 2, par)
                    dispatch_rest(t + 2, par, 0)
                dve.wait_ge(residual_done.sem, residual_done.now(t, 1))
                dve.wait_ge(y_done.sem, y_done.now(t, 1))
                tail.moments_vector(dve, t, p_x[:, 1:2, :], residual[:, :, :])
                if two:
                    dispatch_rest(t + 2, par, 1)
                tail.write_vector(dve, t, lambda j: tile(t))

            floor_row(0)
            scale_row(0)
            x_low(0, 0)
            floor_row(1)
            scale_row(1)
            xw_rest(0, 0, 0)
            shift(0)
            xw_rest(0, 0, 1)
            sum_up(0, 0, True)
            combine_copy(0, 0, True)
            dispatch_rest(0, 0, 0)
            dispatch_rest(0, 0, 1)
            x_low(1, 1)
            shift(1)
            floor_row(2)
            scale_row(2)
            sum_up(1, 1)
            combine_copy(1, 1)
            dispatch_rest(1, 1, 0)
            dispatch_rest(1, 1, 1)
            all_turns(dve, turn)
def stage_cross(nc, X, W, ctx_in, mask):
    NT = 2
    NB = NT * SPT
    TURNS = TILES // NT
    XHEADS, XHD = 2, 64
    SOURCES = 2
    MASKED = -float(np.finfo(np.float32).max)
    with ExitStack() as ctx:
        def sb(n, shape, dt=F32):
            return ctx.enter_context(nc.sbuf_tensor("cr_" + n, shape, dt))

        def ps(n, shape):
            return ctx.enter_context(nc.psum_tensor("cr_" + n, shape, F32))

        def sig(n, per=1):
            return Signal(ctx, nc, "cr_" + n, per)

        c_in = sb("c_in", [P, NT, D])
        masks = sb("masks", [P, BATCH, SEQ], U8)
        q_gain = sb("q_gain", [P, 1])
        stats = sb("stats", [P, NT, SOURCES, 6])
        moments = sb("moments", [P, NT, SOURCES, 2])
        var_eps = sb("var_eps", [P, NT, SOURCES])
        rstd = sb("rstd", [P, NT, SOURCES])
        scrap = sb("scrap", [P, 1])
        normed = sb("normed", [P, NT, SOURCES, D])
        feats = sb("feats", [P, SOURCES, NT, P])
        squares = sb("squares", [P, NT, 3, D])
        ssq = sb("ssq", [P, NT * 3 * XHEADS])
        floor_ssq = sb("floor_ssq", [P, NT * 3 * XHEADS])
        rnorm = sb("rnorm", [P, NT * 3 * XHEADS])
        scaled = sb("scaled", [P, NT, 3, D])
        spread_q = sb("spread_q", [P, NB, XHEADS, SEQ])
        keys = sb("keys", [P, NB, 2, SEQ])
        values = sb("values", [P, NB, D])
        neg_max = sb("neg_max", [P, NB])
        probs = sb("probs", [P, NB, P])
        sums = sb("sums", [P, NB])
        rsum = sb("rsum", [P, NB])
        probs_n = sb("probs_n", [P, NB, P])
        probs_t = sb("probs_t", [P, NB, P])
        mixed = sb("mixed", [P, NB, SEQ])
        residual = sb("residual", [P, NT, D])
        p_t = ps("p_t", [P, SOURCES * NT, P])
        p_q = ps("p_q", [P, NT, D])
        p_key = ps("p_key", [P, NT, SOURCES, D])
        p_v = ps("p_v", [P, NT, SOURCES, D])
        p_k = ps("p_k", [P, SOURCES, NT, P])
        p_s = ps("p_s", [P, NB, P])
        p_pt = ps("p_pt", [P, NB, P])
        p_o = ps("p_o", [P, NB, XHEADS, SEQ])
        p_y = p_o[:, 0:NT, :, :].rearrange("p j h s -> p j (h s)")

        tail = NormTail(ctx, nc, "cr_tail", NT)
        constants = nc.alloc_semaphore("cr_constants")
        mask_in = nc.alloc_semaphore("cr_mask_in")
        mask_ready = nc.alloc_semaphore("cr_mask_ready")
        c_landed = sig("c_landed", 16)
        counted, aggregated, floored, rooted = sig("counted"), sig("aggregated"), sig("floored"), sig("rooted")
        normed_done = sig("normed_done")
        turned = sig("turned")
        feats_done = sig("feats_done")
        qk_done = sig("qk_done")
        v_done = sig("v_done")
        squared = sig("squared")
        summed_sq = sig("summed_sq")
        floored_sq = sig("floored_sq")
        rooted_sq = sig("rooted_sq")
        scale_done = sig("scale_done")
        qk_turned = sig("qk_turned")
        qk_ready = sig("qk_ready")
        values_ready = sig("values_ready")
        scored = sig("scored")
        masked = sig("masked")
        maxed = sig("maxed")
        exped = sig("exped")
        inverted = sig("inverted")
        probs_normed = sig("probs_normed")
        probs_turned = sig("probs_turned")
        probs_ready = sig("probs_ready")
        weighted = sig("weighted")
        mixed_ready = sig("mixed_ready")
        projected = sig("projected")
        residual_done = sig("residual_done")

        block = ctx.enter_context(nc.Block())

        def tiles(t):
            return X[:, bass.ds(t * NT, NT), :]

        def all_turns(engine, turn):
            with engine.Fori(0, TURNS - 3) as t:
                turn(t, True, True, True)
            turn(TURNS - 3, True, True, False)
            turn(TURNS - 2, True, False, False)
            turn(TURNS - 1, False, False, False)

        @block.sync
        def _(sp):
            sp.dma_start(masks[:, :, :], mask.rearrange("b s -> (b s)").partition_broadcast(P)).then_inc(mask_in, 16)
            sp.dma_start(c_in[:, :, :], ctx_in[0:NT * P, :].rearrange("(j p) d -> p j d", p=P)).then_inc(c_landed.sem, 16)
            with sp.Fori(1, TURNS) as t:
                sp.wait_ge(normed_done.sem, normed_done.before(t, 1))
                sp.dma_start(c_in[:, :, :], ctx_in[bass.ds(t * (NT * P), NT * P), :].rearrange("(j p) d -> p j d", p=P))\
                    .then_inc(c_landed.sem, 16)
            sp.wait_ge(c_landed.sem, 16 * TURNS)
            sp.wait_ge(mask_in, 16)

        @block.gpsimd
        def _(pool):
            nc.gpsimd.memset(spread_q[:, :, :, :], 0.0).then_inc(constants, 1)
            credit(pool, rooted, rooted_sq, probs_normed, residual_done)
            tail.credit_pool(pool)

            pool.wait_ge(mask_in, 16)
            nc.gpsimd.tensor_scalar(masks[:, :, :], masks[:, :, :], -1.0, 1.0, ALU.mult, ALU.add).then_inc(mask_ready, 1)

            def root(t):
                pool.wait_ge(normed_done.sem, normed_done.before(t, 1))
                pool.wait_ge(floored.sem, floored.now(t, 1))
                nc.gpsimd.tensor_tensor(rstd[:, :, :], var_eps[:, :, :],
                                        W["minus_half"][:, 0:4].rearrange("p (a b) -> p a b", a=NT), ALU.pow)\
                    .then_inc(rooted.sem, 1)

            def root_sq(t):
                pool.wait_ge(scale_done.sem, scale_done.before(t, 1))
                pool.wait_ge(floored_sq.sem, floored_sq.now(t, 1))
                nc.gpsimd.tensor_tensor(rnorm[:, :], floor_ssq[:, :], W["minus_half"][:, 0:12], ALU.pow)\
                    .then_inc(rooted_sq.sem, 1)

            def normalise(t):
                pool.wait_ge(probs_turned.sem, probs_turned.before(t, 1))
                pool.wait_ge(inverted.sem, inverted.now(t, 1))
                nc.gpsimd.tensor_tensor(probs_n[:, :, :], probs[:, :, :],
                                        rsum[:, :].unsqueeze(2).broadcast_to((P, NB, P)), ALU.mult)\
                    .then_inc(probs_normed.sem, 1)

            def turn(t, one, two, three):
                nc.gpsimd.tensor_tensor(residual[:, :, :], tiles(t), W["xout_b"].unsqueeze(1).broadcast_to((P, NT, D)),
                                        ALU.add).then_inc(residual_done.sem, 1)
                if three:
                    root(t + 3)
                if two:
                    root_sq(t + 2)
                if one:
                    normalise(t + 1)
                tail.root_pool(pool, t, W["minus_half"])

            root(0)
            root(1)
            root_sq(0)
            root(2)
            root_sq(1)
            normalise(0)
            all_turns(pool, turn)

        @block.tensor
        def _(pe):
            credit(pe, turned, qk_done, v_done, qk_turned, scored, probs_turned, weighted, projected)
            pe.wait_ge(constants, 2)

            def transposes(t, queries=None):
                pe.wait_ge(normed_done.sem, normed_done.now(t, 1))
                if queries is not None:
                    pe.wait_ge(qk_ready.sem, qk_ready.now(queries, 1))
                pe.wait_ge(feats_done.sem, feats_done.before(t, 1))
                for j in range(NT):
                    for s in range(SOURCES):
                        last = pe.transpose(p_t[:, s * NT + j, :], normed[:, j, s, :], W["ident"])
                last.then_inc(turned.sem, 1)

            def project_heads(t):
                pe.wait_ge(feats_done.sem, feats_done.now(t, 1))
                pe.wait_ge(scale_done.sem, scale_done.before(t, 1))
                for j in range(NT):
                    pe.matmul(p_q[:, j, :], feats[:, 1, j, :], W["XWq"], start=True, stop=True)
                    for s in range(SOURCES):
                        last = pe.matmul(p_key[:, j, s, :], feats[:, s, j, :], W["XWkv"][:, 0:D], start=True, stop=True)
                last.then_inc(qk_done.sem, 1)

            def project_values(t):
                pe.wait_ge(values_ready.sem, values_ready.before(t, 1))
                for j in range(NT):
                    for s in range(SOURCES):
                        last = pe.matmul(p_v[:, j, s, :], feats[:, s, j, :], W["XWkv"][:, D:], start=True, stop=True)
                last.then_inc(v_done.sem, 1)

            def qk_transposes(t, sources):
                pe.wait_ge(scale_done.sem, scale_done.now(t, 1))
                pe.wait_ge(qk_ready.sem, qk_ready.before(t, 1))
                pe.wait_ge(feats_done.sem, feats_done.now(sources, 1))
                for j in range(NT):
                    pe.transpose(p_t[:, j, :], scaled[:, j, 0, :], W["ident"])
                    for s in range(SOURCES):
                        last = pe.transpose(p_k[:, s, j, :], scaled[:, j, 1 + s, :], W["ident"])
                last.then_inc(qk_turned.sem, 1)

            def scores(t):
                pe.wait_ge(qk_ready.sem, qk_ready.now(t, 1))
                pe.wait_ge(exped.sem, exped.before(t, 1))
                for b in range(NB):
                    last = pe.matmul(p_s[:, b, :], spread_q[:, b, :, :], keys[:, b, :, :], start=True, stop=True)
                last.then_inc(scored.sem, 1)

            def weigh(t):
                pe.wait_ge(probs_ready.sem, probs_ready.before(t, 1))
                pe.wait_ge(probs_normed.sem, probs_normed.now(t, 1))
                for b in range(NB):
                    last = pe.transpose(p_pt[:, b, :], probs_n[:, b, :], W["ident"])
                last.then_inc(probs_turned.sem, 1)

            def mix(t):
                pe.wait_ge(values_ready.sem, values_ready.now(t, 1))
                pe.wait_ge(mixed_ready.sem, mixed_ready.before(t, 1))
                pe.wait_ge(tail.added.sem, tail.added.before(t, 1))
                pe.wait_ge(probs_ready.sem, probs_ready.now(t, 1))
                for b in range(NB):
                    last = pe.matmul(p_o[:, b, :, :], values[:, b, :], probs_t[:, b, :], start=True, stop=True)
                last.then_inc(weighted.sem, 1)

            def project(t):
                pe.wait_ge(mixed_ready.sem, mixed_ready.now(t, 1))
                for j in range(NT):
                    last = pe.matmul(p_y[:, j, :], mixed[:, SPT * j:SPT * j + SPT, :], W["XWout"], start=True, stop=True)
                last.then_inc(projected.sem, 1)

            def turn(t, one, two, three):
                if one:
                    qk_transposes(t + 1, t + 2 if two else t + 1)
                if two:
                    project_heads(t + 2)
                weigh(t)
                mix(t)
                if one:
                    scores(t + 1)
                project(t)
                if two:
                    project_values(t + 2)
                if three:
                    transposes(t + 3, queries=t + 1)

            transposes(0)
            project_heads(0)
            project_values(0)
            transposes(1)
            qk_transposes(0, 1)
            project_heads(1)
            scores(0)
            project_values(1)
            transposes(2, queries=0)
            all_turns(pe, turn)

        @block.scalar
        def _(act):
            credit(act, feats_done, squared, qk_ready, exped, values_ready, mixed_ready)
            act.wait_ge(constants, 2)

            def to_features(t):
                act.wait_ge(turned.sem, turned.now(t, 1))
                act.wait_ge(v_done.sem, v_done.before(t, 1))
                for s, n in ((0, "lnx"), (1, "lnl")):
                    last = nc.scalar.activation(feats[:, s, :, :], p_t[:, s * NT:s * NT + NT, :], ACT.Identity,
                                                bias=W[n + "_b"], scale=W[n + "_g"])
                last.then_inc(feats_done.sem, 1)

            def square(t):
                act.wait_ge(summed_sq.sem, summed_sq.before(t, 1))
                act.wait_ge(qk_done.sem, qk_done.now(t, 1))
                nc.scalar.activation(squares[:, :, 0, :], p_q[:, :, :], ACT.Square)
                nc.scalar.activation(squares[:, :, 1:3, :], p_key[:, :, :, :], ACT.Square).then_inc(squared.sem, 1)

            def spread(t):
                act.wait_ge(scored.sem, scored.before(t, 1))
                act.wait_ge(qk_turned.sem, qk_turned.now(t, 1))
                for h in range(XHEADS):
                    r = slice(XHD * h, XHD * h + XHD)
                    nc.scalar.activation(spread_q[r, :, h, :], p_t[r, 0:NT, :].rearrange("p j (b s) -> p (j b) s", s=SEQ),
                                         ACT.Copy, scale=q_gain[r, :])
                for b in range(SPT):
                    for s in range(SOURCES):
                        out = keys[:, :, s ^ b, :].rearrange("p (j b) s -> p j b s", b=SPT)[:, :, b, :]
                        last = nc.scalar.activation(out, p_k[:, s, :, SEQ * b:SEQ * b + SEQ], ACT.Copy, scale=W["k_gamma"])
                last.then_inc(qk_ready.sem, 1)

            def place_values(t):
                act.wait_ge(v_done.sem, v_done.now(t, 1))
                act.wait_ge(weighted.sem, weighted.before(t, 1))
                for b in range(SPT):
                    for s in range(SOURCES):
                        src = p_v[SEQ * b:SEQ * b + SEQ, :, s, :]
                        to = SEQ * (s ^ b)
                        last = nc.scalar.activation(
                            values[to:to + SEQ, :, :].rearrange("p (j b) d -> p j b d", b=SPT)[:, :, b, :], src, ACT.Copy)
                last.then_inc(values_ready.sem, 1)

            def copy_mixed(t):
                act.wait_ge(projected.sem, projected.before(t, 1))
                act.wait_ge(weighted.sem, weighted.now(t, 1))
                for h in range(XHEADS):
                    r = slice(XHD * h, XHD * h + XHD)
                    last = nc.scalar.activation(mixed[r, :, :], p_o[r, :, h, :], ACT.Copy)
                last.then_inc(mixed_ready.sem, 1)

            def exp(t):
                act.wait_ge(probs_normed.sem, probs_normed.before(t, 1))
                act.wait_ge(inverted.sem, inverted.before(t, 1))
                act.wait_ge(maxed.sem, maxed.now(t, 1))
                for b in range(NB):
                    last = nc.scalar.activation(probs[:, b, :], p_s[:, b, :], ACT.Exp, bias=neg_max[:, b:b + 1],
                                                accum_out=sums[:, b:b + 1])
                last.then_inc(exped.sem, 1)

            def turn(t, one, two, three):
                if one:
                    spread(t + 1)
                if two:
                    square(t + 2)
                copy_mixed(t)
                if one:
                    place_values(t + 1)
                    exp(t + 1)
                if three:
                    to_features(t + 3)

            to_features(0)
            square(0)
            to_features(1)
            spread(0)
            square(1)
            place_values(0)
            exp(0)
            to_features(2)
            all_turns(act, turn)

        @block.vector
        def _(dve):
            nc.vector.tensor_scalar(q_gain[:, :], W["q_gamma"], XHD ** -0.5, None, ALU.mult).then_inc(constants, 1)
            credit(dve, counted, aggregated, floored, normed_done, summed_sq, floored_sq, scale_done, masked,
                   maxed, inverted, probs_ready)
            tail.credit_vector(dve)

            def norm_inputs(t):
                dve.wait_ge(aggregated.sem, aggregated.before(t, 1))
                dve.wait_ge(c_landed.sem, (t + 1) * 16)
                for j in range(NT):
                    nc.vector.bn_stats(stats[:, j, 0, :], c_in[:, j, :])
                    last = nc.vector.bn_stats(stats[:, j, 1, :], X[:, bass.ds(t * NT + j, 1), :])
                last.then_inc(counted.sem, 1)
                dve.wait_ge(counted.sem, counted.now(t, 1))
                nc.vector.memset(scrap[:, :], 0.0)
                for j in range(NT):
                    for s in range(SOURCES):
                        last = nc.vector.bn_aggr(moments[:, j, s, :], stats[:, j, s, :])
                last.then_inc(aggregated.sem, 1)
                dve.wait_ge(aggregated.sem, aggregated.now(t, 1))
                nc.vector.tensor_scalar(var_eps[:, :, :], moments[:, :, :, 1], LN_EPS, None, ALU.add).then_inc(floored.sem, 1)

            def write_inputs(t):
                dve.wait_ge(turned.sem, turned.before(t, 1))
                dve.wait_ge(rooted.sem, rooted.now(t, 1))
                for j in range(NT):
                    for s, src in ((0, c_in[:, j, :].unsqueeze(1)), (1, X[:, bass.ds(t * NT + j, 1), :])):
                        last = nc.vector.tensor_scalar(normed[:, j, s, :].unsqueeze(1), src, moments[:, j, s, 0:1],
                                                       rstd[:, j, s:s + 1], ALU.subtract, ALU.mult)
                last.then_inc(normed_done.sem, 1)

            def head_norms(t):
                dve.wait_ge(squared.sem, squared.now(t, 1))
                dve.wait_ge(floored_sq.sem, floored_sq.before(t, 1))
                nc.vector.tensor_reduce(ssq[:, :], squares[:, :, :, :].rearrange("p j k (h d) -> p (j k h) d", d=XHD),
                                        AX_X, ALU.add).then_inc(summed_sq.sem, 1)
                dve.wait_ge(summed_sq.sem, summed_sq.now(t, 1))
                dve.wait_ge(rooted_sq.sem, rooted_sq.before(t, 1))
                nc.vector.tensor_scalar(floor_ssq[:, :], ssq[:, :], 1.0 / XHD, 1e-16, ALU.mult, ALU.max)\
                    .then_inc(floored_sq.sem, 1)

            def scale_heads(t):
                dve.wait_ge(qk_turned.sem, qk_turned.before(t, 1))
                dve.wait_ge(rooted_sq.sem, rooted_sq.now(t, 1))
                for j in range(NT):
                    a = j * 3 * XHEADS
                    nc.vector.tensor_tensor(scaled[:, j, 0, :].rearrange("p (h d) -> p h d", d=XHD),
                                            p_q[:, j, :].rearrange("p (h d) -> p h d", d=XHD),
                                            rnorm[:, a:a + 2].unsqueeze(2).broadcast_to((P, 2, XHD)), ALU.mult)
                    last = nc.vector.tensor_tensor(scaled[:, j, 1:3, :].rearrange("p k (h d) -> p k h d", d=XHD),
                                                   p_key[:, j, :, :].rearrange("p k (h d) -> p k h d", d=XHD),
                                                   rnorm[:, a + 2:a + 6].rearrange("p (k h) -> p k h", h=2).unsqueeze(3)
                                                   .broadcast_to((P, 2, 2, XHD)), ALU.mult)
                last.then_inc(scale_done.sem, 1)

            def mask_scores(t):
                dve.wait_ge(scored.sem, scored.now(t, 1))
                for b in range(NB):
                    cols = slice(0, SEQ) if b % 2 == 0 else slice(SEQ, P)
                    last = nc.vector.scalar_tensor_tensor(out=p_s[:, b:b + 1, cols], in0=masks[:, bass.ds(t * NB + b, 1), :],
                                                          scalar=MASKED, in1=p_s[:, b:b + 1, cols], op0=ALU.mult, op1=ALU.add)
                last.then_inc(masked.sem, 1)
                dve.wait_ge(masked.sem, masked.now(t, 1))
                nc.vector.tensor_reduce(neg_max[:, :], p_s[:, :, :], AX_X, ALU.max, negate=True).then_inc(maxed.sem, 1)

            def invert(t):
                dve.wait_ge(probs_normed.sem, probs_normed.before(t, 1))
                dve.wait_ge(exped.sem, exped.now(t, 1))
                nc.vector.reciprocal(rsum[:, :], sums[:, :]).then_inc(inverted.sem, 1)

            def copy_probs(t):
                dve.wait_ge(weighted.sem, weighted.before(t, 1))
                dve.wait_ge(probs_turned.sem, probs_turned.now(t, 1))
                nc.vector.tensor_copy(probs_t[:, :, :], p_pt[:, :, :]).then_inc(probs_ready.sem, 1)

            def turn(t, one, two, three):
                copy_probs(t)
                if three:
                    norm_inputs(t + 3)
                if two:
                    head_norms(t + 2)
                if one:
                    mask_scores(t + 1)
                if three:
                    write_inputs(t + 3)
                if two:
                    scale_heads(t + 2)
                if one:
                    invert(t + 1)
                dve.wait_ge(residual_done.sem, residual_done.now(t, 1))
                dve.wait_ge(projected.sem, projected.now(t, 1))
                tail.moments_vector(dve, t, p_y, residual[:, :, :])
                tail.write_vector(dve, t, lambda j: X[:, bass.ds(t * NT + j, 1), :])

            norm_inputs(0)
            write_inputs(0)
            norm_inputs(1)
            write_inputs(1)
            dve.wait_ge(mask_ready, 1)
            head_norms(0)
            scale_heads(0)
            norm_inputs(2)
            write_inputs(2)
            head_norms(1)
            mask_scores(0)
            scale_heads(1)
            invert(0)
            all_turns(dve, turn)
def stage_experts(nc, X, W, rms_w, w1, w2, experts_in):
    GT = 4
    GN = GT * P
    TURNS = TILES // GT
    HC = EH // P
    ORDER = [ROUTED] + list(range(ROUTED)) + [ROUTED + 1]
    RMS_EPS = 1.1920929e-07
    with ExitStack() as ctx:
        def sb(n, shape, dt=F32):
            return ctx.enter_context(nc.sbuf_tensor("ex_" + n, shape, dt))

        def ps(n, shape):
            return ctx.enter_context(nc.psum_tensor("ex_" + n, shape, F32))

        def sig(n, per=1):
            return Signal(ctx, nc, "ex_" + n, per)

        squares = sb("squares", [P, GT, D])
        ssq = sb("ssq", [P, GT])
        mean_sq = sb("mean_sq", [P, GT])
        rnorm = sb("rnorm", [P, GT])
        x_raw = sb("x_raw", [P, GT, D])
        x_scaled = sb("x_scaled", [P, GT, D])
        x_raw_t = sb("x_raw_t", [P, GN])
        x_hi = sb("x_hi", [P, GN], F32R)
        x_lo = sb("x_lo", [P, GN], F32R)
        w1_hi = sb("w1_hi", [P, EXPERTS, EH], F32R)
        w1_lo = sb("w1_lo", [P, EXPERTS, EH], F32R)
        hidden = sb("hidden", [P, 4, GN])
        acc = sb("acc", [P, GT, D])
        R = [P, GT, ROUTED]
        top = sb("top", [P, GT, 5])
        logits, exps, gates, hits, picks, rest, picks2 = (sb(n, R) for n in
                                                          ("logits", "exps", "gates", "hits", "picks", "rest", "picks2"))
        gate_next = sb("gate_next", R)
        gate = sb("gate", R)
        p_h = ps("p_h", [P, 3, GN])
        p_o = ps("p_o", [P, 2, GT, D])
        p_t = ps("p_t", [P, GN])
        p_x = ps("p_x", [P, GN])
        p_r = ps("p_r", [P, GT, P])

        tail = NormTail(ctx, nc, "ex_tail", GT)
        w1_scaled = nc.alloc_semaphore("ex_w1_scaled")
        w1_hi_ready = nc.alloc_semaphore("ex_w1_hi_ready")
        w1_lo_ready = nc.alloc_semaphore("ex_w1_lo_ready")
        squared, mean_done, rooted, scaled = sig("squared"), sig("mean_done"), sig("rooted"), sig("scaled")
        raw_copied = sig("raw_copied")
        turned = sig("turned")
        raw_turned = sig("raw_turned")
        raw_t_ready = sig("raw_t_ready")
        x_hi_ready = sig("x_hi_ready")
        x_lo_ready = sig("x_lo_ready")
        routed = sig("routed")
        shifted = sig("shifted")
        exped = sig("exped")
        STEPS = 20
        step = sig("step", STEPS)
        gate_copied = sig("gate_copied")
        h_done = sig("h_done", EXPERTS * HC)
        silu_done = sig("silu_done", EXPERTS * HC)
        out_done = sig("out_done", EXPERTS)
        acc_done = sig("acc_done", EXPERTS - 1)

        block = ctx.enter_context(nc.Block())

        def group(t):
            return X[:, bass.ds(t * GT, GT), :]

        def all_turns(engine, turn):
            with engine.Fori(0, TURNS - 1) as t:
                turn(t, True)
            turn(TURNS - 1, False)

        @block.gpsimd
        def _(pool):
            credit(pool, rooted, raw_copied)
            tail.credit_pool(pool)

            def front(t, first=False):
                pool.wait_ge(raw_turned.sem, raw_turned.before(t, 1))
                if not first:
                    pool.wait_ge(acc_done.sem, acc_done.before(t, 1))
                pool.wait_ge(scaled.sem, scaled.before(t, 1))
                pool.wait_ge(mean_done.sem, mean_done.now(t, 1))
                nc.gpsimd.tensor_tensor(rnorm[:, :], mean_sq[:, :], W["minus_half"][:, 0:GT], ALU.pow)\
                    .then_inc(rooted.sem, 1)
                nc.gpsimd.tensor_copy(x_raw[:, :, :], group(t)).then_inc(raw_copied.sem, 1)

            def turn(t, one):
                if one:
                    front(t + 1)
                tail.root_pool(pool, t, W["minus_half"])

            front(0, True)
            all_turns(pool, turn)

        @block.tensor
        def _(pe):
            credit(pe, turned, raw_turned, routed, h_done, out_done)

            def transpose_raw(t):
                pe.wait_ge(raw_copied.sem, raw_copied.now(t, 1))
                pe.wait_ge(raw_t_ready.sem, raw_t_ready.before(t, 1))
                for j in range(GT):
                    last = pe.transpose(p_x[:, j * P:(j + 1) * P], x_raw[:, j, :], W["ident"])
                last.then_inc(raw_turned.sem, 1)

            def transpose_scaled(t):
                pe.wait_ge(scaled.sem, scaled.now(t, 1))
                pe.wait_ge(x_lo_ready.sem, x_lo_ready.before(t, 1))
                for j in range(GT):
                    last = pe.transpose(p_t[:, j * P:(j + 1) * P], x_scaled[:, j, :], W["ident"])
                last.then_inc(turned.sem, 1)

            def route(t):
                pe.wait_ge(raw_t_ready.sem, raw_t_ready.now(t, 1))
                pe.wait_ge(shifted.sem, shifted.before(t, 1))
                for j in range(GT):
                    last = pe.matmul(p_r[:, j, 0:ROUTED], x_raw_t[:, j * P:(j + 1) * P], W["router"], start=True, stop=True)
                last.then_inc(routed.sem, 1)

            def up(t, n):
                if n == 0:
                    pe.wait_ge(x_hi_ready.sem, x_hi_ready.now(t, 1))
                    pe.wait_ge(x_lo_ready.sem, x_lo_ready.now(t, 1))
                for c in range(HC):
                    i = HC * n + c
                    pe.wait_ge(silu_done.sem, silu_done.now(t, i - 2) if i >= 3 else silu_done.before(t, EXPERTS * HC + i - 2))
                    w_hi, w_lo = (w[:, ORDER[n], c * P:(c + 1) * P] for w in (w1_hi, w1_lo))
                    pe.matmul(p_h[:, i % 3, :], w_hi, x_hi[:, :], start=True, stop=False)
                    pe.matmul(p_h[:, i % 3, :], w_hi, x_lo[:, :], start=False, stop=False)
                    pe.matmul(p_h[:, i % 3, :], w_lo, x_hi[:, :], start=False, stop=True).then_inc(h_done.sem, 1)

            def down(t, n):
                pe.wait_ge(silu_done.sem, silu_done.now(t, HC * n + HC))
                if n >= 2:
                    pe.wait_ge(acc_done.sem, acc_done.now(t, n - 1))
                elif n == 0:
                    pe.wait_ge(acc_done.sem, acc_done.before(t, EXPERTS - 1))
                else:
                    pe.wait_ge(tail.added.sem, tail.added.before(t, 1))
                for j in range(GT):
                    for c in range(HC):
                        last = pe.matmul(p_o[:, n % 2, j, :], hidden[:, (HC * n + c) % 4, j * P:(j + 1) * P],
                                         w2[:, ORDER[n], c, :], start=(c == 0), stop=(c == HC - 1))
                last.then_inc(out_done.sem, 1)

            def turn(t, one):
                for n in range(EXPERTS + 1):
                    if n < EXPERTS:
                        up(t, n)
                    if n >= 1:
                        down(t, n - 1)
                    if one and n == 6:
                        transpose_raw(t + 1)
                        transpose_scaled(t + 1)
                    if one and n == 7:
                        route(t + 1)

            transpose_raw(0)
            transpose_scaled(0)
            route(0)
            pe.wait_ge(w1_lo_ready, EXPERTS)
            all_turns(pe, turn)

        @block.scalar
        def _(act):
            credit(act, squared, raw_t_ready, x_hi_ready, exped, silu_done)

            def square(t):
                act.wait_ge(mean_done.sem, mean_done.before(t, 1))
                for j in range(GT):
                    last = nc.scalar.activation(squares[:, j, :].unsqueeze(1), X[:, bass.ds(t * GT + j, 1), :], ACT.Square,
                                                accum_out=ssq[:, j:j + 1])
                last.then_inc(squared.sem, 1)

            def raw_copy(t):
                act.wait_ge(raw_turned.sem, raw_turned.now(t, 1))
                act.wait_ge(routed.sem, routed.before(t, 1))
                nc.scalar.activation(x_raw_t[:, :], p_x[:, :], ACT.Copy).then_inc(raw_t_ready.sem, 1)

            def x_copy(t):
                act.wait_ge(turned.sem, turned.now(t, 1))
                act.wait_ge(h_done.sem, h_done.before(t, EXPERTS * HC))
                nc.scalar.activation(x_hi[:, :], p_t[:, :], ACT.Copy).then_inc(x_hi_ready.sem, 1)

            def exp(t):
                act.wait_ge(step.sem, step.before(t, STEPS))
                act.wait_ge(shifted.sem, shifted.now(t, 1))
                nc.scalar.activation(exps[:, :, :], logits[:, :, :], ACT.Exp).then_inc(exped.sem, 1)

            def turn(t, one):
                for i in range(EXPERTS * HC):
                    n = i // HC
                    if n >= 2:
                        act.wait_ge(out_done.sem, out_done.now(t, n - 1))
                    else:
                        act.wait_ge(out_done.sem, out_done.before(t, EXPERTS - 1 + n))
                    act.wait_ge(h_done.sem, h_done.now(t, i + 1))
                    nc.scalar.activation(hidden[:, i % 4, :], p_h[:, i % 3, :], ACT.Silu).then_inc(silu_done.sem, 1)
                    if one and i == 2:
                        square(t + 1)
                    if one and i == 14:
                        raw_copy(t + 1)
                    if one and i == 19:
                        exp(t + 1)
                    if one and i == 30:
                        x_copy(t + 1)

            square(0)
            raw_copy(0)
            x_copy(0)
            for e in range(EXPERTS):
                act.wait_ge(w1_scaled, e + 1)
                nc.scalar.activation(w1_hi[:, e, :], w1[:, e, :], ACT.Copy).then_inc(w1_hi_ready, 1)
            exp(0)
            all_turns(act, turn)

        @block.vector
        def _(dve):
            credit(dve, x_lo_ready, mean_done, scaled, shifted, step, gate_copied, acc_done)
            tail.credit_vector(dve)

            def mean_rows(t):
                dve.wait_ge(squared.sem, squared.now(t, 1))
                dve.wait_ge(rooted.sem, rooted.before(t, 1))
                nc.vector.tensor_scalar(mean_sq[:, :], ssq[:, :], 1.0 / D, RMS_EPS, ALU.mult, ALU.add)\
                    .then_inc(mean_done.sem, 1)

            def scale_rows(t):
                dve.wait_ge(turned.sem, turned.before(t, 1))
                dve.wait_ge(rooted.sem, rooted.now(t, 1))
                for j in range(GT):
                    last = nc.vector.tensor_scalar(x_scaled[:, j, :].unsqueeze(1), X[:, bass.ds(t * GT + j, 1), :],
                                                   rnorm[:, j:j + 1], None, ALU.mult)
                last.then_inc(scaled.sem, 1)

            rank = W["first_rank"].unsqueeze(1).broadcast_to((P, GT, ROUTED))
            tt, reduce = nc.vector.tensor_tensor, nc.vector.tensor_reduce

            def wide(k):
                return top[:, :, k:k + 1].broadcast_to((P, GT, ROUTED))

            def small(t, n, ins):
                ins.then_inc(step.sem, 1)
                dve.wait_ge(step.sem, step.now(t, n))

            def best_of(t, n, values, picked):
                small(t, n, reduce(top[:, :, 2:3], values[:, :, :], AX_X, ALU.max))
                small(t, n + 1, tt(hits[:, :, :], values[:, :, :], wide(2), ALU.is_equal))
                small(t, n + 2, tt(hits[:, :, :], hits[:, :, :], rank, ALU.mult))
                small(t, n + 3, reduce(top[:, :, 3:4], hits[:, :, :], AX_X, ALU.max))
                small(t, n + 4, tt(picked[:, :, :], hits[:, :, :], wide(3), ALU.is_equal))

            def shift_logits(t):
                dve.wait_ge(exped.sem, exped.before(t, 1))
                dve.wait_ge(routed.sem, routed.now(t, 1))
                small(t, 1, reduce(top[:, :, 0:1], p_r[:, :, 0:ROUTED], AX_X, ALU.max, negate=True))
                tt(logits[:, :, :], p_r[:, :, 0:ROUTED], wide(0), ALU.add).then_inc(shifted.sem, 1)

            def softmax(t):
                dve.wait_ge(exped.sem, exped.now(t, 1))
                small(t, 2, reduce(top[:, :, 1:2], exps[:, :, :], AX_X, ALU.add))
                small(t, 3, nc.vector.reciprocal(top[:, :, 1:2], top[:, :, 1:2]))
                small(t, 4, tt(gates[:, :, :], exps[:, :, :], wide(1), ALU.mult))

            def first_best(t):
                best_of(t, 5, gates, picks)

            def second_best(t):
                small(t, 10, nc.vector.scalar_tensor_tensor(out=rest[:, :, :], in0=picks[:, :, :], scalar=-2.0,
                                                            in1=gates[:, :, :], op0=ALU.mult, op1=ALU.add))
                best_of(t, 11, rest, picks2)

            def keep_two(t):
                small(t, 16, tt(picks[:, :, :], picks[:, :, :], picks2[:, :, :], ALU.add))
                small(t, 17, tt(gates[:, :, :], gates[:, :, :], picks[:, :, :], ALU.mult))
                small(t, 18, reduce(top[:, :, 4:5], gates[:, :, :], AX_X, ALU.add))
                small(t, 19, nc.vector.tensor_scalar(top[:, :, 4:5], top[:, :, 4:5], 1e-9, None, ALU.add))
                small(t, 20, nc.vector.reciprocal(top[:, :, 4:5], top[:, :, 4:5]))

            ROUTER = {8: shift_logits, 10: softmax, 11: first_best, 12: second_best, 13: keep_two}

            def gate_ready(t):
                dve.wait_ge(acc_done.sem, acc_done.before(t, EXPERTS - 1))
                nc.vector.tensor_tensor(gate[:, :, :], gates[:, :, :], top[:, :, 4:5].broadcast_to((P, GT, ROUTED)), ALU.mult)\
                    .then_inc(gate_copied.sem, 1)
                dve.wait_ge(gate_copied.sem, gate_copied.now(t, 1))

            def accumulate(t, n):
                dve.wait_ge(out_done.sem, out_done.now(t, n + 1))
                out = p_o[:, n % 2, :, :]
                if n == 0:
                    dve.wait_ge(tail.added.sem, tail.added.before(t, 1))
                    nc.vector.tensor_tensor(acc[:, :, :], out, x_raw[:, :, :], ALU.add).then_inc(acc_done.sem, 1)
                else:
                    dve.wait_ge(acc_done.sem, acc_done.now(t, n))
                    for j in range(GT):
                        last = nc.vector.scalar_tensor_tensor(out=acc[:, j, :], in0=out[:, j, :],
                                                              scalar=gate[:, j, ORDER[n]:ORDER[n] + 1], in1=acc[:, j, :],
                                                              op0=ALU.mult, op1=ALU.add)
                    last.then_inc(acc_done.sem, 1)

            def low_part(t):
                dve.wait_ge(h_done.sem, h_done.before(t, EXPERTS * HC))
                dve.wait_ge(x_hi_ready.sem, x_hi_ready.now(t, 1))
                nc.vector.tensor_tensor(x_lo[:, :], p_t[:, :], x_hi[:, :].bitcast(F32), ALU.subtract)\
                    .then_inc(x_lo_ready.sem, 1)

            def turn(t, one):
                gate_ready(t)
                for n in range(EXPERTS - 1):
                    accumulate(t, n)
                    if one and n == 2:
                        mean_rows(t + 1)
                    if one and n == 4:
                        scale_rows(t + 1)
                    if one and n in ROUTER:
                        ROUTER[n](t + 1)
                    if one and n == EXPERTS - 3:
                        low_part(t + 1)
                dve.wait_ge(acc_done.sem, acc_done.now(t, EXPERTS - 1))
                dve.wait_ge(out_done.sem, out_done.now(t, EXPERTS))
                tail.moments_vector(dve, t, p_o[:, (EXPERTS - 1) % 2, :, :], acc[:, :, :])
                tail.write_vector(dve, t, lambda j: X[:, bass.ds(t * GT + j, 1), :])

            mean_rows(0)
            scale_rows(0)
            dve.wait_ge(experts_in, 48)
            for e in range(EXPERTS):
                nc.vector.tensor_scalar(w1[:, e, :], w1[:, e, :], rms_w[:, e:e + 1], None, ALU.mult).then_inc(w1_scaled, 1)
            low_part(0)
            for e in range(EXPERTS):
                dve.wait_ge(w1_hi_ready, e + 1)
                nc.vector.tensor_tensor(w1_lo[:, e, :], w1[:, e, :], w1_hi[:, e, :].bitcast(F32), ALU.subtract)\
                    .then_inc(w1_lo_ready, 1)
            for part in ROUTER.values():
                part(0)
            all_turns(dve, turn)
def weight_layout():
    sizes = [("ident", P), ("pwT", D), ("gruT", 2 * D), ("ff1T", HIDDEN), ("ff2T", HIDDEN),
             ("dw", 3), ("dw_b", 1), ("gains_raw", 3), ("ff_b1", 4), ("pw_b", D), ("ff_b2", D),
             ("WqT", D), ("WkT", D), ("WvT", D), ("WoT", D),
             ("gamma_x", 1), ("gamma_slot", 1), ("slots", SLOTS), ("moe_w1", HIDDEN), ("moe_w2", HIDDEN),
             ("Wqkv", 3 * D), ("qk_b", 2), ("v_b", 1), ("Wout", D), ("out_b", D),
             ("lnx_g", 1), ("lnx_b", 1), ("lnl_g", 1), ("lnl_b", 1), ("q_gamma", 1), ("k_gamma", 1),
             ("XWq", D), ("XWkv", 2 * D), ("XWout", D), ("xout_b", D),
             ("router", ROUTED), ("head_mask", 4), ("window", SEQ), ("first_rank", ROUTED)]
    at, out = 0, {}
    for name, n in sizes:
        out[name] = (at, n)
        at += n
    return out, at


def build(nc, x, ctx_in, mask, weights, rms_w, w1, w2, out, stages=6):
    layout, columns = weight_layout()
    with ExitStack() as ctx:
        X = ctx.enter_context(nc.sbuf_tensor("X", [P, TILES, D], F32))
        pack = ctx.enter_context(nc.sbuf_tensor("pack", [P, columns], F32))
        prepared = ctx.enter_context(nc.sbuf_tensor("prepared", [P, 32], F32))
        ew1 = ctx.enter_context(nc.sbuf_tensor("ew1", [P, EXPERTS, EH], F32))
        ew2 = ctx.enter_context(nc.sbuf_tensor("ew2", [P, EXPERTS, EH // P, D], F32))
        erms = ctx.enter_context(nc.sbuf_tensor("erms", [P, EXPERTS], F32))
        experts_in = ctx.enter_context(nc.semaphore("experts_in"))
        W = {n: pack[:, a:a + k] for n, (a, k) in layout.items()}
        W["ff2T"] = W["ff2T"].rearrange("p (c d) -> p c d", c=4)
        W["moe_w2"] = W["moe_w2"].rearrange("p (c d) -> p c d", c=4)
        W["slots"] = W["slots"].rearrange("p (c d) -> p c d", c=4)
        W["gains"] = prepared[:, 0:3]
        W["minus_half"] = prepared[:, 8:24]
        load(nc, X, pack, prepared, W, x, weights, (rms_w, w1, w2), (erms, ew1, ew2), experts_in)
        chain = (lambda: stage_conv_gru(nc, X, W), lambda: stage_attention(nc, X, W, 0, ctx_in),
                 lambda: stage_soft_mixture(nc, X, W), lambda: stage_attention(nc, X, W, 1, ctx_in),
                 lambda: stage_cross(nc, X, W, ctx_in, mask), lambda: stage_experts(nc, X, W, erms, ew1, ew2, experts_in))
        for k, stage in enumerate(chain):
            if k < stages or k == -stages - 1:
                with nc.cleanup_on_exit():
                    stage()
        store(nc, X, out)


def load(nc, X, pack, prepared, W, x, weights, expert_weights, expert_tiles, experts_in):
    with ExitStack() as ctx:
        x_in = ctx.enter_context(nc.semaphore("x_in"))
        w_in = ctx.enter_context(nc.semaphore("w_in"))
        block = ctx.enter_context(nc.Block())

        @block.sync
        def _(sp):
            sp.dma_start(X[:, :, :], x.rearrange("(t p) d -> p t d", p=P)).then_inc(x_in, 16)
            sp.wait_ge(x_in, 16)
            (rms_w, w1, w2), (erms, ew1, ew2) = expert_weights, expert_tiles
            sp.dma_start(erms[:, :], rms_w).then_inc(experts_in, 16)
            sp.dma_start(ew1[:, :, :], w1.rearrange("e d h -> d e h")).then_inc(experts_in, 16)
            sp.dma_start(ew2[:, :, :, :], w2.rearrange("e (c p) d -> p e c d", p=P)).then_inc(experts_in, 16)

        @block.scalar
        def _(act):
            act.dma_start(pack[:, :], weights).then_inc(w_in, 16)

        @block.vector
        def _(dve):
            nc.vector.memset(W["minus_half"], -0.5)
            dve.wait_ge(w_in, 16)
            nc.vector.tensor_scalar(W["gains"], W["gains_raw"], 1.0, float(D) ** 0.5, ALU.add, ALU.mult)


def store(nc, X, out):
    with ExitStack() as ctx:
        stored = ctx.enter_context(nc.semaphore("stored"))
        block = ctx.enter_context(nc.Block())

        @block.sync
        def _(sp):
            sp.dma_start(out.rearrange("(t p) d -> p t d", p=P), X[:, :, :]).then_inc(stored, 16)
            sp.wait_ge(stored, 16)


def pack_weights(v):
    def rows(a):
        return np.broadcast_to(np.asarray(a).reshape(1, -1), (P, np.asarray(a).size))

    def chunks(a):
        a = np.asarray(a)
        return a.reshape(4, P, a.shape[1]).transpose(1, 0, 2).reshape(P, -1)

    def col(a):
        return np.asarray(a).reshape(-1, 1)

    f, q = np.arange(P), np.arange(P)[:, None] % SEQ
    k = np.arange(SEQ)[None, :]
    allowed = (q - k >= 0) & (q - k < WINDOW)
    parts = {
        "ident": np.eye(P, dtype=np.float32),
        "pwT": v["L0_attn_conv_pw_w"].T, "gruT": v["L0_attn_gru_w"].T, "ff1T": v["L0_attn_ff_w1"].T,
        "ff2T": chunks(v["L0_attn_ff_w2"].T), "dw": v["L0_attn_conv_dw_w"].reshape(D, 3),
        "dw_b": col(v["L0_attn_conv_dw_b"]),
        "gains_raw": np.stack([v["L0_attn_conv_norm_g"], v["L0_attn_gru_norm_g"], v["L0_attn_ff_norm_g"]], 1),
        "ff_b1": v["L0_attn_ff_b1"].reshape(4, P).T, "pw_b": rows(v["L0_attn_conv_pw_b"]), "ff_b2": rows(v["L0_attn_ff_b2"]),
        "WqT": v["L0_xattn_Wq"].T, "WkT": v["L0_xattn_Wk"].T, "WvT": v["L0_xattn_Wv"].T, "WoT": v["L0_xattn_Wo"].T,
        "gamma_x": col(v["L0_ffn_gamma_x"]), "gamma_slot": col(v["L0_ffn_gamma_slot"]),
        "slots": chunks(v["L0_ffn_slot_embeds"].reshape(SLOTS, D)), "moe_w1": v["L0_ffn_w1"], "moe_w2": chunks(v["L0_ffn_w2"]),
        "Wqkv": v["L1_attn_W_qkv"], "qk_b": v["L1_attn_b_qkv"][:2 * D].reshape(2, D).T, "v_b": col(v["L1_attn_b_qkv"][2 * D:]),
        "Wout": v["L1_attn_W_out"], "out_b": rows(v["L1_attn_b_out"]),
        "lnx_g": col(v["L1_xattn_ln_x_g"]), "lnx_b": col(v["L1_xattn_ln_x_b"]),
        "lnl_g": col(v["L1_xattn_ln_l_g"]), "lnl_b": col(v["L1_xattn_ln_l_b"]),
        "q_gamma": col(np.concatenate([v["L1_xattn_q_gamma"]] * 2)), "k_gamma": col(np.concatenate([v["L1_xattn_k_gamma"]] * 2)),
        "XWq": v["L1_xattn_W_q"], "XWkv": v["L1_xattn_W_kv"], "XWout": v["L1_xattn_W_out"], "xout_b": rows(v["L1_xattn_b_out"]),
        "router": v["L1_ffn_router_w"],
        "head_mask": (f[:, None] % 32 // HD == np.arange(4)[None, :]).astype(np.float32),
        "window": np.where(allowed, np.float32(0), np.float32(-1e30)),
        "first_rank": rows(np.arange(ROUTED, 0, -1).astype(np.float32)),
    }
    layout, columns = weight_layout()
    packed = np.zeros((P, columns), np.float32)
    for name, (a, n) in layout.items():
        packed[:, a:a + n] = parts[name]
    return packed


_OUT = ((BATCH, SEQ, D), "float32")


def kernel(**inputs):
    import concourse.bacc as _bacc
    from concourse.bass_utils import run_bass_kernel_spmd as _run

    v = {n: np.asarray(a) for n, a in inputs.items()}
    arrays = {
        "x": v["x"].reshape(BATCH * SEQ, D), "ctx": v["ctx_1024"].reshape(BATCH * SEQ, D),
        "mask": v["mask_BxS2_bk0"], "weights": pack_weights(v),
        "rms_w": np.ascontiguousarray(np.concatenate([v["L1_ffn_rms_w"], v["L1_ffn_rms_w_s"]]).T),
        "w1": np.concatenate([v["L1_ffn_w1"], v["L1_ffn_w1_s"]]), "w2": np.concatenate([v["L1_ffn_w2"], v["L1_ffn_w2_s"]]),
    }
    arrays = {n: np.ascontiguousarray(a) for n, a in arrays.items()}
    nc = _bacc.Bacc("TRN2", target_bir_lowering=False, num_devices=1)
    aps = [nc.dram_tensor(n, a.shape, mybir.dt.from_np(a.dtype), kind="ExternalInput").ap() for n, a in arrays.items()]
    out = nc.dram_tensor("out", [BATCH * SEQ, D], F32, kind="ExternalOutput").ap()
    build(nc, *aps, out)
    r = _run(nc, [arrays], core_ids=[0])
    return r.results[0]["out"].reshape(_OUT[0])
```

```python
from contextlib import ExitStack

import numpy as np

import concourse.bass as bass
from concourse import mybir

ALU = mybir.AluOpType
ACT = mybir.ActivationFunctionType
F32 = mybir.dt.float32
F32R = mybir.dt.float32r
BF16 = mybir.dt.bfloat16
U8 = mybir.dt.uint8
AX_X = mybir.AxisListType.X

P = 128
D = 128
BATCH, SEQ = 64, 64
SPT = P // SEQ
TILES = BATCH // SPT
FIRST_TILES = 12
HIDDEN = 4 * D
SLOTS = 512
HEADS, HD = 16, 8
ROUTED, SHARED, EH = 14, 2, 256
EXPERTS = ROUTED + SHARED
WINDOW = 32
LN_EPS = 1e-5
NORM_FLOOR = 1e-24


class Signal:

    def __init__(self, ctx, nc, name, per):
        self.sem, self.per = nc.alloc_semaphore(name), per

    def now(self, turn, n):
        return (turn + 1) * self.per + n

    def before(self, turn, n):
        return turn * self.per + n


def credit(engine, *signals):
    for s in signals:
        engine.nop().then_inc(s.sem, s.per)
class NormTail:

    def __init__(self, ctx, nc, name, n):
        def sb(part, shape):
            return ctx.enter_context(nc.sbuf_tensor(f"{name}_{part}", shape, F32))

        def sig(part):
            return Signal(ctx, nc, f"{name}_{part}", 1)

        self.nc, self.n = nc, n
        self.total = sb("total", [P, n, D])
        self.stats = sb("stats", [P, n, 6])
        self.moments = sb("moments", [P, n, 2])
        self.var_eps = sb("var_eps", [P, n])
        self.rstd = sb("rstd", [P, n])
        self.scrap = sb("scrap", [P, 1])
        self.added, self.counted, self.aggregated, self.floored = sig("added"), sig("counted"), sig("aggregated"), sig("floored")
        self.rooted, self.done = sig("rooted"), sig("done")

    def credit_vector(self, dve):
        credit(dve, self.added, self.counted, self.aggregated, self.floored, self.done)

    def credit_pool(self, pool):
        credit(pool, self.rooted)

    def moments_vector(self, dve, t, branch, residual):
        nc = self.nc
        dve.wait_ge(self.done.sem, self.done.before(t, 1))
        nc.vector.tensor_tensor(self.total[:, :, :], branch, residual, ALU.add).then_inc(self.added.sem, 1)
        dve.wait_ge(self.added.sem, self.added.now(t, 1))
        for j in range(self.n):
            last = nc.vector.bn_stats(self.stats[:, j, :], self.total[:, j, :])
        last.then_inc(self.counted.sem, 1)
        dve.wait_ge(self.counted.sem, self.counted.now(t, 1))
        nc.vector.memset(self.scrap[:, :], 0.0)
        for j in range(self.n):
            last = nc.vector.bn_aggr(self.moments[:, j, :], self.stats[:, j, :])
        last.then_inc(self.aggregated.sem, 1)
        dve.wait_ge(self.aggregated.sem, self.aggregated.now(t, 1))
        dve.wait_ge(self.rooted.sem, self.rooted.before(t, 1))
        nc.vector.tensor_scalar(self.var_eps[:, :], self.moments[:, :, 1], LN_EPS, None, ALU.add)\
            .then_inc(self.floored.sem, 1)

    def root_pool(self, pool, t, minus_half):
        pool.wait_ge(self.done.sem, self.done.before(t, 1))
        pool.wait_ge(self.floored.sem, self.floored.now(t, 1))
        self.nc.gpsimd.tensor_tensor(self.rstd[:, :], self.var_eps[:, :], minus_half[:, 0:self.n], ALU.pow)\
            .then_inc(self.rooted.sem, 1)

    def write_vector(self, dve, t, out_tile):
        dve.wait_ge(self.rooted.sem, self.rooted.now(t, 1))
        for j in range(self.n):
            last = self.nc.vector.tensor_scalar(out_tile(j), self.total[:, j, :].unsqueeze(1), self.moments[:, j, 0:1],
                                                self.rstd[:, j:j + 1], ALU.subtract, ALU.mult)
        last.then_inc(self.done.sem, 1)
def stage_conv_gru(nc, X, W, landed):
    GT = 4
    GN = GT * P
    TURNS = TILES // GT
    CONV, GRU, FF = 0, 1, 2
    with ExitStack() as ctx:
        def sb(name, shape, dt=F32):
            return ctx.enter_context(nc.sbuf_tensor("cg_" + name, shape, dt))

        def ps(name, shape):
            return ctx.enter_context(nc.psum_tensor("cg_" + name, shape, F32))

        def sig(name, per=1):
            return Signal(ctx, nc, "cg_" + name, per)

        def sig3(name):
            return [sig(f"{name}{k}") for k in range(3)]

        squares = sb("squares", [P, 3, GT, D])
        ssq = sb("ssq", [P, 3, GT])
        floored_ssq = sb("floored_ssq", [P, 3, GT])
        rnorm = sb("rnorm", [P, 3, GT])
        x_bias = sb("x_bias", [P, GT, D])
        x_conv = sb("x_conv", [P, GT, D])
        x_gru = sb("x_gru", [P, GT, D])
        x_twice = sb("x_twice", [P, GT, D])
        x_scaled = sb("x_scaled", [P, 3, GT, D])
        padded = sb("padded", [P, GN // SEQ, SEQ + 2])
        conv = sb("conv", [P, GN])
        xn_gru = sb("xn_gru", [P, GN])
        xn_ff = sb("xn_ff", [P, GN])
        sig_hidden = sb("sig_hidden", [P, GN])
        update = sb("update", [P, GN])
        keep = sb("keep", [P, GN])
        hgru = sb("hgru", [P, GN])
        hff = sb("hff", [P, 4, GN])
        p_a = ps("p_a", [P, GN])
        p_b = ps("p_b", [P, GN])
        p_hg = ps("p_hg", [P, 2, GN])
        p_f1 = ps("p_f1", [P, 3, GN])
        p_f2 = ps("p_f2", [P, GN])
        gain = [W["gains"][:, k:k + 1] for k in range(3)]

        tail = NormTail(ctx, nc, "cg_tail", GT)
        zeroed = nc.alloc_semaphore("cg_zeroed")
        squared, floored, rooted, scaled = sig3("squared"), sig3("floored"), sig3("rooted"), sig3("scaled")
        turned, feats_ready = sig3("turned"), sig3("feats_ready")
        biased = sig("biased")
        convolved = sig("convolved", 3)
        pointwise = sig("pointwise")
        conv_added = sig("conv_added")
        hg_done = sig("hg_done")
        sigmoids = sig("sigmoids", 2)
        gated = sig("gated", 2)
        scanned = sig("scanned")
        h_turned = sig("h_turned")
        gru_added = sig("gru_added")
        doubled = sig("doubled", 2)
        ff1_done = sig("ff1_done", 4)
        gelu_done = sig("gelu_done", 4)
        ff2_done = sig("ff2_done")

        block = ctx.enter_context(nc.Block())

        def group(g):
            return X[:, bass.ds(g * GT, GT), :]

        def tile_of(g, j):
            return X[:, bass.ds(g * GT + j, 1), :]

        def source(k, g, j):
            if k == CONV:
                return tile_of(g, j)
            return (x_conv if k == GRU else x_gru)[:, j, :].unsqueeze(1)

        def by_seq(a):
            return a.rearrange("p (b s) -> p b s", s=SEQ)

        def by_tile(a):
            return a.rearrange("p (j d) -> p j d", d=D)

        def all_turns(engine, turn):
            engine.wait_ge(landed["x"], 16)
            with engine.Fori(0, TURNS - 3) as g:
                turn(g, True, True, True)
            turn(TURNS - 3, True, True, False)
            turn(TURNS - 2, True, False, False)
            turn(TURNS - 1, False, False, False)

        @block.sync
        def _(sp):
            sp.wait_ge(landed["weights"], 16)

        @block.scalar
        def _(act):
            credit(act, *squared, *feats_ready, sigmoids, gelu_done)
            act.wait_ge(zeroed, 2)

            def sum_squares(k, g):
                if k == GRU:
                    act.wait_ge(conv_added.sem, conv_added.now(g, 1))
                if k == FF:
                    act.wait_ge(gru_added.sem, gru_added.now(g, 1))
                act.wait_ge(floored[k].sem, floored[k].before(g, 1))
                for j in range(GT):
                    last = nc.scalar.activation(squares[:, k, j, :].unsqueeze(1), source(k, g, j), ACT.Square,
                                                accum_out=ssq[:, k, j:j + 1])
                last.then_inc(squared[k].sem, 1)

            def to_features(k, g):
                act.wait_ge(turned[k].sem, turned[k].now(g, 1))
                if k == CONV:
                    act.wait_ge(convolved.sem, convolved.before(g, 3))
                    out, src = padded[:, :, 2:], by_seq(p_a[:, :])
                elif k == GRU:
                    act.wait_ge(hg_done.sem, hg_done.before(g, 1))
                    out, src = xn_gru[:, :], p_b[:, :]
                else:
                    act.wait_ge(ff1_done.sem, ff1_done.before(g, 4))
                    out, src = xn_ff[:, :], p_f2[:, :]
                nc.scalar.activation(out, src, ACT.Copy, scale=gain[k]).then_inc(feats_ready[k].sem, 1)

            def gate_sigmoids(g):
                act.wait_ge(hg_done.sem, hg_done.now(g, 1))
                act.wait_ge(gated.sem, gated.before(g, 2))
                nc.scalar.activation(sig_hidden[:, :], p_hg[:, 0, :], ACT.Sigmoid).then_inc(sigmoids.sem, 1)
                act.wait_ge(scanned.sem, scanned.before(g, 1))
                nc.scalar.activation(update[:, :], p_hg[:, 1, :], ACT.Sigmoid)
                nc.scalar.activation(by_seq(keep[:, :])[:, :, 1:], by_seq(p_hg[:, 1, :])[:, :, 1:], ACT.Sigmoid, scale=-1.0)\
                    .then_inc(sigmoids.sem, 1)

            def gelus(g):
                act.wait_ge(ff2_done.sem, ff2_done.before(g, 1))
                for c in range(4):
                    act.wait_ge(ff1_done.sem, ff1_done.now(g, c + 1))
                    nc.scalar.activation(hff[:, c, :], p_f1[:, c % 3, :], ACT.Gelu, bias=W["ff_b1"][:, c:c + 1])\
                        .then_inc(gelu_done.sem, 1)

            def turn(g, one, two, three):
                if one:
                    to_features(GRU, g + 1)
                to_features(FF, g)
                if two:
                    to_features(CONV, g + 2)
                if one:
                    gate_sigmoids(g + 1)
                gelus(g)
                if one:
                    sum_squares(FF, g + 1)
                if two:
                    sum_squares(GRU, g + 2)
                if three:
                    sum_squares(CONV, g + 3)

            sum_squares(CONV, 0)
            sum_squares(CONV, 1)
            to_features(CONV, 0)
            sum_squares(GRU, 0)
            to_features(CONV, 1)
            to_features(GRU, 0)
            gate_sigmoids(0)
            sum_squares(FF, 0)
            sum_squares(GRU, 1)
            sum_squares(CONV, 2)
            all_turns(act, turn)

        @block.gpsimd
        def _(pool):
            nc.gpsimd.memset(padded[:, :, 0:2], 0.0).then_inc(zeroed, 1)
            nc.gpsimd.memset(by_seq(keep[:, :])[:, :, 0:1], 0.0).then_inc(zeroed, 1)
            credit(pool, *rooted, biased, doubled)
            tail.credit_pool(pool)

            def root(k, g):
                pool.wait_ge(scaled[k].sem, scaled[k].before(g, 1))
                pool.wait_ge(floored[k].sem, floored[k].now(g, 1))
                nc.gpsimd.tensor_tensor(rnorm[:, k, :], floored_ssq[:, k, :], W["minus_half"][:, 0:GT], ALU.pow)\
                    .then_inc(rooted[k].sem, 1)

            def add_conv_bias(g):
                pool.wait_ge(conv_added.sem, conv_added.before(g, 1))
                pool.wait_ge(rooted[CONV].sem, rooted[CONV].now(g, 1))
                nc.gpsimd.tensor_tensor(x_bias[:, :, :], group(g), W["pw_b"].unsqueeze(1).broadcast_to((P, GT, D)), ALU.add)\
                    .then_inc(biased.sem, 1)

            def add_residuals(g):
                pool.wait_ge(tail.added.sem, tail.added.before(g, 1))
                pool.wait_ge(gru_added.sem, gru_added.now(g, 1))
                nc.gpsimd.tensor_tensor(x_twice[:, :, :], group(g), W["ff_b2"].unsqueeze(1).broadcast_to((P, GT, D)), ALU.add)\
                    .then_inc(doubled.sem, 1)
                pool.wait_ge(doubled.sem, doubled.now(g, 1))
                nc.gpsimd.tensor_tensor(x_twice[:, :, :], x_twice[:, :, :], x_gru[:, :, :], ALU.add).then_inc(doubled.sem, 1)

            def turn(g, one, two, three):
                add_residuals(g)
                if two:
                    add_conv_bias(g + 2)
                if one:
                    root(FF, g + 1)
                if two:
                    root(GRU, g + 2)
                if three:
                    root(CONV, g + 3)
                tail.root_pool(pool, g, W["minus_half"])

            root(CONV, 0)
            add_conv_bias(0)
            root(CONV, 1)
            root(GRU, 0)
            add_conv_bias(1)
            root(FF, 0)
            root(GRU, 1)
            root(CONV, 2)
            all_turns(pool, turn)

        @block.tensor
        def _(pe):
            credit(pe, *turned, pointwise, hg_done, h_turned, ff1_done, ff2_done)

            def transposes(k, g):
                pe.wait_ge(scaled[k].sem, scaled[k].now(g, 1))
                out, reader = ((p_a, conv_added), (p_b, gru_added), (p_f2, tail.added))[k]
                pe.wait_ge(reader.sem, reader.before(g, 1))
                for j in range(GT):
                    last = pe.transpose(out[:, j * P:(j + 1) * P], x_scaled[:, k, j, :], W["ident"])
                last.then_inc(turned[k].sem, 1)

            def pointwise_conv(g):
                pe.wait_ge(convolved.sem, convolved.now(g, 3))
                for j in range(GT):
                    last = pe.matmul(p_a[:, j * P:(j + 1) * P], conv[:, j * P:(j + 1) * P], W["pwT"], start=True, stop=True)
                last.then_inc(pointwise.sem, 1)

            def hidden_gate(g):
                pe.wait_ge(feats_ready[GRU].sem, feats_ready[GRU].now(g, 1))
                pe.wait_ge(sigmoids.sem, sigmoids.before(g, 2))
                pe.wait_ge(gated.sem, gated.before(g, 1))
                pe.matmul(p_hg[:, 0, :], W["gruT"][:, 0:D], xn_gru[:, :], start=True, stop=True)
                pe.matmul(p_hg[:, 1, :], W["gruT"][:, D:2 * D], xn_gru[:, :], start=True, stop=True).then_inc(hg_done.sem, 1)

            def turn_back(g):
                pe.wait_ge(scanned.sem, scanned.now(g, 1))
                for j in range(GT):
                    last = pe.transpose(p_b[:, j * P:(j + 1) * P], hgru[:, j * P:(j + 1) * P], W["ident"])
                last.then_inc(h_turned.sem, 1)

            def ff1(g, c):
                if c == 0:
                    pe.wait_ge(feats_ready[FF].sem, feats_ready[FF].now(g, 1))
                    pe.wait_ge(gelu_done.sem, gelu_done.before(g, 4))
                if c == 3:
                    pe.wait_ge(gelu_done.sem, gelu_done.now(g, 1))
                pe.matmul(p_f1[:, c % 3, :], W["ff1T"][:, c * P:(c + 1) * P], xn_ff[:, :], start=True, stop=True)\
                    .then_inc(ff1_done.sem, 1)

            def ff2(g):
                pe.wait_ge(gelu_done.sem, gelu_done.now(g, 4))
                for j in range(GT):
                    for c in range(4):
                        last = pe.matmul(p_f2[:, j * P:(j + 1) * P], hff[:, c, j * P:(j + 1) * P], W["ff2T"][:, c, :],
                                         start=(c == 0), stop=(c == 3))
                last.then_inc(ff2_done.sem, 1)

            def turn(g, one, two, three):
                if one:
                    transposes(GRU, g + 1)
                transposes(FF, g)
                if two:
                    transposes(CONV, g + 2)
                if one:
                    hidden_gate(g + 1)
                for c in range(3):
                    ff1(g, c)
                if two:
                    pointwise_conv(g + 2)
                ff1(g, 3)
                if one:
                    turn_back(g + 1)
                ff2(g)

            transposes(CONV, 0)
            pointwise_conv(0)
            transposes(CONV, 1)
            transposes(GRU, 0)
            hidden_gate(0)
            pointwise_conv(1)
            turn_back(0)
            all_turns(pe, turn)

        @block.vector
        def _(dve):
            credit(dve, *scaled, *floored, convolved, conv_added, gated, scanned, gru_added)
            tail.credit_vector(dve)
            dve.wait_ge(zeroed, 2)

            def floor(k, g):
                dve.wait_ge(squared[k].sem, squared[k].now(g, 1))
                dve.wait_ge(rooted[k].sem, rooted[k].before(g, 1))
                nc.vector.tensor_scalar(floored_ssq[:, k, :], ssq[:, k, :], NORM_FLOOR, None, ALU.max)\
                    .then_inc(floored[k].sem, 1)

            def scale(k, g):
                dve.wait_ge(turned[k].sem, turned[k].before(g, 1))
                dve.wait_ge(rooted[k].sem, rooted[k].now(g, 1))
                for j in range(GT):
                    last = nc.vector.tensor_scalar(x_scaled[:, k, j, :].unsqueeze(1), source(k, g, j), rnorm[:, k, j:j + 1],
                                                   None, ALU.mult)
                last.then_inc(scaled[k].sem, 1)

            def depthwise(g):
                dve.wait_ge(pointwise.sem, pointwise.before(g, 1))
                dve.wait_ge(feats_ready[CONV].sem, feats_ready[CONV].now(g, 1))
                y = by_seq(conv[:, :])
                nc.vector.tensor_scalar(y, padded[:, :, 0:SEQ], W["dw"][:, 0:1], W["dw_b"], ALU.mult, ALU.add)\
                    .then_inc(convolved.sem, 1)
                for k in (1, 2):
                    dve.wait_ge(convolved.sem, convolved.now(g, k))
                    nc.vector.scalar_tensor_tensor(out=y, in0=padded[:, :, k:k + SEQ], scalar=W["dw"][:, k:k + 1], in1=y,
                                                   op0=ALU.mult, op1=ALU.add).then_inc(convolved.sem, 1)

            def add_conv(g):
                dve.wait_ge(gru_added.sem, gru_added.before(g, 1))
                dve.wait_ge(scaled[GRU].sem, scaled[GRU].before(g, 1))
                dve.wait_ge(biased.sem, biased.now(g, 1))
                dve.wait_ge(pointwise.sem, pointwise.now(g, 1))
                nc.vector.tensor_tensor(x_conv[:, :, :], by_tile(p_a[:, :]), x_bias[:, :, :], ALU.add).then_inc(conv_added.sem, 1)

            def gates(g):
                dve.wait_ge(sigmoids.sem, sigmoids.now(g, 1))
                nc.vector.scalar_tensor_tensor(out=sig_hidden[:, :], in0=p_hg[:, 0, :], scalar=0.5, in1=sig_hidden[:, :],
                                               op0=ALU.add, op1=ALU.max).then_inc(gated.sem, 1)
                dve.wait_ge(gated.sem, gated.now(g, 1))
                dve.wait_ge(sigmoids.sem, sigmoids.now(g, 2))
                nc.vector.tensor_tensor(update[:, :], update[:, :], sig_hidden[:, :], ALU.mult).then_inc(gated.sem, 1)
                dve.wait_ge(gated.sem, gated.now(g, 2))
                dve.wait_ge(h_turned.sem, h_turned.before(g, 1))
                nc.vector.tensor_tensor_scan(hgru[:, :], keep[:, :], update[:, :], 0.0, ALU.mult, ALU.add)\
                    .then_inc(scanned.sem, 1)

            def add_gru(g):
                dve.wait_ge(scaled[FF].sem, scaled[FF].before(g, 1))
                dve.wait_ge(doubled.sem, doubled.before(g, 2))
                dve.wait_ge(conv_added.sem, conv_added.now(g, 1))
                dve.wait_ge(h_turned.sem, h_turned.now(g, 1))
                nc.vector.tensor_tensor(x_gru[:, :, :], by_tile(p_b[:, :]), x_conv[:, :, :], ALU.add).then_inc(gru_added.sem, 1)

            def turn(g, one, two, three):
                if two:
                    depthwise(g + 2)
                if one:
                    gates(g + 1)
                    add_gru(g + 1)
                if two:
                    add_conv(g + 2)
                if one:
                    floor(FF, g + 1)
                if two:
                    floor(GRU, g + 2)
                if one:
                    scale(FF, g + 1)
                if three:
                    floor(CONV, g + 3)
                if two:
                    scale(GRU, g + 2)
                if three:
                    scale(CONV, g + 3)
                dve.wait_ge(doubled.sem, doubled.now(g, 2))
                dve.wait_ge(ff2_done.sem, ff2_done.now(g, 1))
                tail.moments_vector(dve, g, by_tile(p_f2[:, :]), x_twice[:, :, :])
                tail.write_vector(dve, g, lambda j: tile_of(g, j))

            floor(CONV, 0)
            scale(CONV, 0)
            floor(CONV, 1)
            depthwise(0)
            add_conv(0)
            floor(GRU, 0)
            scale(CONV, 1)
            scale(GRU, 0)
            depthwise(1)
            gates(0)
            add_gru(0)
            add_conv(1)
            floor(FF, 0)
            floor(GRU, 1)
            scale(FF, 0)
            floor(CONV, 2)
            scale(GRU, 1)
            scale(CONV, 2)
            all_turns(dve, turn)
def stage_attention(nc, X, W, layer, ctx_in):
    NT = 2
    NB = NT * SPT
    TN = NT * P
    TURNS = TILES // NT
    cross = layer == 0
    if cross:
        w_q, w_k, w_v, w_o = W["WqT"], W["WkT"], W["WvT"], W["WoT"]
    else:
        w_q, w_k, w_v, w_o = W["Wqkv"][:, 0:D], W["Wqkv"][:, D:2 * D], W["Wqkv"][:, 2 * D:], W["Wout"]
    name = f"at{layer}_"
    with ExitStack() as ctx:
        def sb(n, shape, dt=F32):
            return ctx.enter_context(nc.sbuf_tensor(name + n, shape, dt))

        def ps(n, shape):
            return ctx.enter_context(nc.psum_tensor(name + n, shape, F32))

        def sig(n, per=1):
            return Signal(ctx, nc, name + n, per)

        x_in = sb("x_in", [P, NT, D])
        c_in = sb("c_in", [P, NT, D]) if cross else None
        feats = sb("feats", [P, 2, TN])
        spread_q = sb("spread_q", [P, NB, 2, 2, SEQ])
        spread_k = sb("spread_k", [P, NB, 4, SEQ])
        spread_v = sb("spread_v", [P, NB, 2, 4, 4, HD])
        neg_max = sb("neg_max", [P, NB, 8])
        shifted = sb("shifted", [P, NB, 8, SEQ])
        probs = sb("probs", [P, NB, 8, SEQ])
        sums = sb("sums", [P, NB, 8])
        rsum = sb("rsum", [P, NB, 8])
        probs_n = sb("probs_n", [P, NB, 8, SEQ])
        probs_t = sb("probs_t", [P, NB, 2, 2 * P])
        mixed = sb("mixed", [P, NB, SEQ])
        residual = sb("residual", [P, NT, D])
        q_bias = sb("q_bias", [P, 1])
        k_bias = sb("k_bias", [P, 4])
        window = sb("window", [P, 8, SEQ], BF16) if not cross else None
        ident_b = sb("ident_b", [P, P], BF16) if not cross else None
        p_t = ps("p_t", [P, 2, TN])
        p_q = ps("p_q", [P, TN])
        p_v = ps("p_v", [P, NB, D])
        p_s = ps("p_s", [P, 2, 8, SEQ])
        p_pt = ps("p_pt", [P, 2, 2, 2 * P])
        p_o = ps("p_o", [P, 2, 4, SEQ])
        p_y = p_o[:, 0, :, :].rearrange("p g s -> p (g s)").rearrange("p (j d) -> p j d", j=NT)

        tail = NormTail(ctx, nc, name + "tail", NT)
        constants = nc.alloc_semaphore(name + "constants")
        x_copied = sig("x_copied")
        c_landed = sig("c_landed", 16)
        turned = sig("turned")
        feats_done = sig("feats_done")
        qk_done = sig("qk_done")
        q_spread = sig("q_spread")
        k_spread = sig("k_spread")
        v_done = sig("v_done")
        v_spread = sig("v_spread")
        scored = sig("scored", NB)
        maxed = sig("maxed", NB)
        shift_done = sig("shift_done", NB)
        exped = sig("exped", NB)
        summed = sig("summed", NB)
        inverted = sig("inverted", NB)
        normed = sig("normed", NB)
        probs_turned = sig("probs_turned", NB)
        probs_copied = sig("probs_copied", NB)
        weighted = sig("weighted", NB)
        mixed_ready = sig("mixed_ready", 2)
        projected = sig("projected")
        residual_done = sig("residual_done")

        block = ctx.enter_context(nc.Block())
        CONSTANTS = 4 if cross else 8

        def tiles(t):
            return X[:, bass.ds(t * NT, NT), :]

        def all_turns(engine, turn):
            with engine.Fori(0, TURNS - 2) as t:
                turn(t, True, True)
            turn(TURNS - 2, True, False)
            turn(TURNS - 1, False, False)

        @block.sync
        def _(sp):
            if cross:
                def load(t):
                    sp.wait_ge(turned.sem, turned.before(t, 1))
                    sp.dma_start(c_in[:, :, :], ctx_in[bass.ds(t * TN, TN), :].rearrange("(j p) d -> p j d", p=P))\
                        .then_inc(c_landed.sem, 16)
                with sp.Fori(0, TURNS) as t:
                    load(t)
                sp.wait_ge(c_landed.sem, 16 * TURNS)

        @block.gpsimd
        def _(pool):
            nc.gpsimd.memset(spread_q[:, :, :, :, :], 0.0).then_inc(constants, 1)
            nc.gpsimd.memset(spread_v[:, :, :, :, :, :], 0.0).then_inc(constants, 1)
            if not cross:
                nc.gpsimd.tensor_copy(ident_b[:, :], W["ident"]).then_inc(constants, 1)
                nc.gpsimd.tensor_copy(window[:, :, :], W["window"].unsqueeze(1).broadcast_to((P, 8, SEQ)))\
                    .then_inc(constants, 1)
            credit(pool, x_copied, normed, residual_done)
            tail.credit_pool(pool)

            def copy_x(t):
                pool.wait_ge(turned.sem, turned.before(t, 1))
                nc.gpsimd.tensor_copy(x_in[:, :, :], tiles(t)).then_inc(x_copied.sem, 1)

            def normalise(t, b):
                pool.wait_ge(probs_turned.sem, probs_turned.before(t, b + 1))
                pool.wait_ge(inverted.sem, inverted.now(t, b + 1))
                nc.gpsimd.tensor_tensor(probs_n[:, b, :, :], probs[:, b, :, :],
                                        rsum[:, b, :].unsqueeze(2).broadcast_to((P, 8, SEQ)), ALU.mult)\
                    .then_inc(normed.sem, 1)

            def keep_residual(t):
                if cross:
                    nc.gpsimd.tensor_copy(residual[:, :, :], tiles(t)).then_inc(residual_done.sem, 1)
                else:
                    nc.gpsimd.tensor_tensor(residual[:, :, :], tiles(t), W["out_b"].unsqueeze(1).broadcast_to((P, NT, D)),
                                            ALU.add).then_inc(residual_done.sem, 1)

            def turn(t, one, two, three):
                if one:
                    for b in range(NB - 1):
                        normalise(t + 1, b)
                keep_residual(t)
                if three:
                    copy_x(t + 3)
                tail.root_pool(pool, t, W["minus_half"])
                if one:
                    normalise(t + 1, NB - 1)

            copy_x(0)
            copy_x(1)
            for b in range(NB):
                normalise(0, b)
            copy_x(2)
            with pool.Fori(0, TURNS - 3) as t:
                turn(t, True, True, True)
            turn(TURNS - 3, True, True, False)
            turn(TURNS - 2, True, False, False)
            turn(TURNS - 1, False, False, False)

        @block.tensor
        def _(pe):
            credit(pe, turned, qk_done, v_done, scored, probs_turned, weighted, projected)
            pe.wait_ge(constants, CONSTANTS)

            def transposes(t):
                pe.wait_ge(x_copied.sem, x_copied.now(t, 1))
                pe.wait_ge(feats_done.sem, feats_done.before(t, 1))
                pe.wait_ge(k_spread.sem, k_spread.before(t, 1))
                for j in range(NT):
                    last = pe.transpose(p_t[:, 0, j * P:(j + 1) * P], x_in[:, j, :], W["ident"])
                if cross:
                    pe.wait_ge(c_landed.sem, (t + 1) * 16)
                    for j in range(NT):
                        last = pe.transpose(p_t[:, 1, j * P:(j + 1) * P], c_in[:, j, :], W["ident"])
                last.then_inc(turned.sem, 1)

            def queries_keys(t):
                pe.wait_ge(feats_done.sem, feats_done.now(t, 1))
                pe.wait_ge(q_spread.sem, q_spread.before(t, 1))
                pe.wait_ge(k_spread.sem, k_spread.before(t, 1))
                pe.matmul(p_q[:, :], w_q, feats[:, 0, :], start=True, stop=True)
                pe.matmul(p_t[:, 0, :], w_k, feats[:, 1 if cross else 0, :], start=True, stop=True)\
                    .then_inc(qk_done.sem, 1)

            def values(t):
                pe.wait_ge(v_spread.sem, v_spread.before(t, 1))
                for b in range(NB):
                    kv = feats[:, 1 if cross else 0, b * SEQ:(b + 1) * SEQ]
                    for half in range(2):
                        last = pe.matmul(p_v[SEQ * half:SEQ * half + SEQ, b, :], kv, w_v, start=True, stop=True)
                last.then_inc(v_done.sem, 1)

            def scores(t, b):
                if b == 0:
                    pe.wait_ge(q_spread.sem, q_spread.now(t, 1))
                    pe.wait_ge(k_spread.sem, k_spread.now(t, 1))
                pe.wait_ge(shift_done.sem, shift_done.now(t, b - 1) if b >= 2 else shift_done.before(t, b + 3))
                if not cross:
                    pe.matmul(p_s[:, b % 2, :, :], ident_b[:, :], window[:, :, :], start=True, stop=False,
                              skip_group_check=True)
                for half in range(2):
                    last = pe.matmul(p_s[:, b % 2, 4 * half:4 * half + 4, :], spread_q[:, b, half, :, :],
                                     spread_k[:, b, :, :], start=cross, stop=True, skip_group_check=True)
                last.then_inc(scored.sem, 1)

            def turn_probs(t, b):
                pe.wait_ge(normed.sem, normed.now(t, b + 1))
                pe.wait_ge(probs_copied.sem, probs_copied.now(t, b - 1) if b >= 2 else probs_copied.before(t, b + 3))
                for g2 in range(2):
                    for j2 in range(2):
                        last = pe.transpose(p_pt[:, b % 2, j2, g2 * P:(g2 + 1) * P],
                                            probs_n[:, b, 4 * g2 + 2 * j2:4 * g2 + 2 * j2 + 2, :], W["ident"])
                last.then_inc(probs_turned.sem, 1)

            def weigh(t, b):
                pe.wait_ge(probs_copied.sem, probs_copied.now(t, b + 1))
                if b == 0:
                    pe.wait_ge(v_spread.sem, v_spread.now(t, 1))
                    pe.wait_ge(tail.added.sem, tail.added.before(t, 1))
                if b % 2 == 0:
                    pe.wait_ge(mixed_ready.sem, mixed_ready.now(t, 1) if b else mixed_ready.before(t, 2))
                for j2 in range(2):
                    last = pe.matmul(p_o[:, b % 2, :, :], spread_v[:, b, j2, :, :, :], probs_t[:, b, j2, :],
                                     start=(j2 == 0), stop=(j2 == 1))
                last.then_inc(weighted.sem, 1)

            def project(t):
                pe.wait_ge(mixed_ready.sem, mixed_ready.now(t, 2))
                for j in range(NT):
                    last = pe.matmul(p_y[:, j, :], mixed[:, SPT * j:SPT * j + SPT, :], w_o, start=True, stop=True)
                last.then_inc(projected.sem, 1)

            def turn(t, one, two):
                turn_probs(t, 0)
                if one:
                    scores(t + 1, 1)
                turn_probs(t, 1)
                weigh(t, 0)
                if one:
                    scores(t + 1, 2)
                    values(t + 1)
                if two:
                    transposes(t + 2)
                turn_probs(t, 2)
                weigh(t, 1)
                if one:
                    scores(t + 1, 3)
                turn_probs(t, 3)
                if two:
                    queries_keys(t + 2)
                weigh(t, 2)
                weigh(t, 3)
                if two:
                    scores(t + 2, 0)
                project(t)

            transposes(0)
            queries_keys(0)
            for b in range(NB):
                scores(0, b)
            values(0)
            transposes(1)
            queries_keys(1)
            scores(1, 0)
            all_turns(pe, turn)

        @block.scalar
        def _(act):
            credit(act, feats_done, q_spread, v_spread, exped, probs_copied, mixed_ready)
            act.wait_ge(constants, CONSTANTS)

            def copy_feats(t):
                n = 2 if cross else 1
                act.wait_ge(turned.sem, turned.now(t, 1))
                act.wait_ge(v_done.sem, v_done.before(t, 1))
                nc.scalar.activation(feats[:, 0:n, :], p_t[:, 0:n, :], ACT.Copy).then_inc(feats_done.sem, 1)

            def spread(t):
                act.wait_ge(scored.sem, scored.before(t, NB))
                act.wait_ge(qk_done.sem, qk_done.now(t, 1))
                for g in range(4):
                    r = slice(32 * g, 32 * g + 32)
                    last = nc.scalar.activation(spread_q[r, :, g // 2, g % 2, :],
                                                p_q[r, :].rearrange("p (b s) -> p b s", s=SEQ), ACT.Identity,
                                                bias=q_bias[r, :], scale=HD ** -0.5)
                last.then_inc(q_spread.sem, 1)

            def spread_values(t):
                act.wait_ge(v_done.sem, v_done.now(t, 1))
                act.wait_ge(weighted.sem, weighted.before(t, NB))
                for half in range(2):
                    r = slice(SEQ * half, SEQ * half + SEQ)
                    values = p_v[r, :, :].rearrange("p b (g j d) -> p b g j d", g=4, j=4)
                    for j2 in range(2):
                        last = nc.scalar.activation(spread_v[r, :, j2, :, 2 * j2 + half, :], values[:, :, :, 2 * j2 + half, :],
                                                    ACT.Copy)
                last.then_inc(v_spread.sem, 1)

            def exp(t, b):
                act.wait_ge(normed.sem, normed.before(t, b + 1))
                act.wait_ge(shift_done.sem, shift_done.now(t, b + 1))
                nc.scalar.activation(probs[:, b, :, :], shifted[:, b, :, :], ACT.Exp).then_inc(exped.sem, 1)

            def copy_probs(t, b):
                act.wait_ge(weighted.sem, weighted.before(t, b + 1))
                act.wait_ge(probs_turned.sem, probs_turned.now(t, b + 1))
                nc.scalar.activation(probs_t[:, b, :, :], p_pt[:, b % 2, :, :], ACT.Copy).then_inc(probs_copied.sem, 1)

            def copy_mixed(t, pair):
                act.wait_ge(projected.sem, projected.before(t, 1))
                act.wait_ge(weighted.sem, weighted.now(t, 2 * pair + 2))
                for g in range(4):
                    r = slice(32 * g, 32 * g + 32)
                    last = nc.scalar.activation(mixed[r, 2 * pair:2 * pair + 2, :], p_o[r, :, g, :], ACT.Identity,
                                                bias=(0.0 if cross else W["v_b"][r, :]))
                last.then_inc(mixed_ready.sem, 1)

            def turn(t, one, two):
                copy_probs(t, 0)
                spread_values(t)
                if one:
                    exp(t + 1, 0)
                copy_probs(t, 1)
                if one:
                    exp(t + 1, 1)
                if two:
                    copy_feats(t + 2)
                copy_probs(t, 2)
                copy_mixed(t, 0)
                if one:
                    exp(t + 1, 2)
                copy_probs(t, 3)
                if two:
                    spread(t + 2)
                if one:
                    exp(t + 1, 3)
                copy_mixed(t, 1)

            copy_feats(0)
            spread(0)
            for b in range(NB):
                exp(0, b)
            copy_feats(1)
            spread(1)
            all_turns(act, turn)

        @block.vector
        def _(dve):
            if cross:
                nc.vector.memset(q_bias[:, :], 0.0).then_inc(constants, 1)
                nc.vector.memset(k_bias[:, :], 0.0).then_inc(constants, 1)
            else:
                nc.vector.tensor_scalar(q_bias[:, :], W["qk_b"][:, 0:1], HD ** -0.5, None, ALU.mult).then_inc(constants, 2)
                nc.vector.tensor_scalar(k_bias[:, :], W["head_mask"], W["qk_b"][:, 1:2], None, ALU.mult).then_inc(constants, 2)
            credit(dve, k_spread, maxed, shift_done, summed, inverted)
            tail.credit_vector(dve)
            dve.wait_ge(constants, CONSTANTS)

            def spread_keys(t):
                dve.wait_ge(scored.sem, scored.before(t, NB))
                dve.wait_ge(qk_done.sem, qk_done.now(t, 1))
                for j in range(4):
                    last = nc.vector.tensor_scalar(spread_k[:, :, j, :], p_t[:, 0, :].rearrange("p (b s) -> p b s", s=SEQ),
                                                   W["head_mask"][:, j:j + 1], k_bias[:, j:j + 1], ALU.mult, ALU.add)
                last.then_inc(k_spread.sem, 1)

            def take_max(t, b):
                dve.wait_ge(scored.sem, scored.now(t, b + 1))
                nc.vector.tensor_reduce(neg_max[:, b, :], p_s[:, b % 2, :, :], AX_X, ALU.max, negate=True)\
                    .then_inc(maxed.sem, 1)

            def subtract_max(t, b):
                dve.wait_ge(maxed.sem, maxed.now(t, b + 1))
                dve.wait_ge(exped.sem, exped.before(t, b + 1))
                nc.vector.tensor_tensor(shifted[:, b, :, :], p_s[:, b % 2, :, :],
                                        neg_max[:, b, :].unsqueeze(2).broadcast_to((P, 8, SEQ)), ALU.add)\
                    .then_inc(shift_done.sem, 1)

            def sum_up(t, b):
                dve.wait_ge(exped.sem, exped.now(t, b + 1))
                nc.vector.tensor_reduce(sums[:, b, :], probs[:, b, :, :], AX_X, ALU.add).then_inc(summed.sem, 1)

            def invert(t, b):
                dve.wait_ge(summed.sem, summed.now(t, b + 1))
                dve.wait_ge(normed.sem, normed.before(t, b + 1))
                nc.vector.reciprocal(rsum[:, b, :], sums[:, b, :]).then_inc(inverted.sem, 1)

            def shift(t, b):
                take_max(t, b)
                subtract_max(t, b)

            def sum_and_invert(t, b):
                sum_up(t, b)
                invert(t, b)

            def shift_beside_sum(t, b):
                take_max(t, b)
                sum_up(t, b - 1)
                subtract_max(t, b)
                invert(t, b - 1)

            def turn(t, one, two):
                if one:
                    shift_beside_sum(t + 1, 1)
                    shift_beside_sum(t + 1, 2)
                if one:
                    shift(t + 1, 3)
                if two:
                    spread_keys(t + 2)
                if one:
                    sum_and_invert(t + 1, 2)
                if two:
                    shift(t + 2, 0)
                dve.wait_ge(residual_done.sem, residual_done.now(t, 1))
                dve.wait_ge(projected.sem, projected.now(t, 1))
                tail.moments_vector(dve, t, p_y[:, :, :], residual[:, :, :])
                if one:
                    sum_and_invert(t + 1, 3)
                tail.write_vector(dve, t, lambda j: X[:, bass.ds(t * NT + j, 1), :])

            spread_keys(0)
            shift(0, 0)
            for b in range(1, NB):
                shift_beside_sum(0, b)
            sum_and_invert(0, NB - 1)
            spread_keys(1)
            shift(1, 0)
            all_turns(dve, turn)
def stage_soft_mixture(nc, X, W):
    C = SLOTS // P
    NH = C * SPT
    RING = 4
    TURNS = TILES
    ROOT = float(D) ** 0.5
    HI, LO = 0, 1
    with ExitStack() as ctx:
        def sb(n, shape, dt=F32):
            return ctx.enter_context(nc.sbuf_tensor("sm_" + n, shape, dt))

        def ps(n, shape):
            return ctx.enter_context(nc.psum_tensor("sm_" + n, shape, F32))

        def sig(n, per=1):
            return Signal(ctx, nc, "sm_" + n, per)

        slots_t = sb("slots_t", [P, SLOTS])
        slots_p = sb("slots_p", [P, 2, SLOTS], F32R)
        w1_p = sb("w1_p", [P, 2, HIDDEN], F32R)
        slot_sq = sb("slot_sq", [P, 2, C])
        slot_rn = sb("slot_rn", [P, C])
        slots_n = sb("slots_n", [P, C, D])
        gain_x = sb("gain_x", [P, 1])
        gain_s = sb("gain_s", [P, 1])
        squares = sb("squares", [P, D])
        ssq = sb("ssq", [P, 1])
        floor_ssq = sb("floor_ssq", [P, 1])
        rnorm = sb("rnorm", [P, 1])
        x_scaled = sb("x_scaled", [P, D])
        x_t = sb("x_t", [P, P])
        x_p = sb("x_p", [P, 2, 2, 2 * P], F32R)
        xw = sb("xw", [P, 2, SPT, 2, HIDDEN], F32R)
        neg_max = sb("neg_max", [P, 1 + NH])
        shifted = sb("shifted", [P, 2, SLOTS])
        exps = sb("exps", [P, 2, SLOTS])
        sums = sb("sums", [P, 1 + NH])
        rsums = sb("rsums", [P, 2, 1 + NH])
        combine_t = sb("combine_t", [P, 2, C, P])
        dispatch = sb("dispatch", [P, 2, SPT, SLOTS], F32R)
        hidden = sb("hidden", [P, RING, HIDDEN])
        gathered = sb("gathered", [P, HIDDEN])
        gathered_t = sb("gathered_t", [P, C, P])
        residual = sb("residual", [P, 1, D])
        p_x = ps("p_x", [P, 4, P])
        p_l = ps("p_l", [P, SLOTS])
        p_lt = ps("p_lt", [P, C, P])
        p_tr = ps("p_tr", [P, C, P])
        p_xw = ps("p_xw", [P, HIDDEN])
        p_h = ps("p_h", [P, 2, HIDDEN])
        p_g = ps("p_g", [P, HIDDEN])

        tail = NormTail(ctx, nc, "sm_tail", 1)
        prep = nc.alloc_semaphore("sm_prep")
        prep_v = nc.alloc_semaphore("sm_prep_v")
        parts_hi = nc.alloc_semaphore("sm_parts_hi")
        parts_lo = nc.alloc_semaphore("sm_parts_lo")
        squared = sig("squared")
        floored = sig("floored")
        rooted = sig("rooted")
        scaled = sig("scaled")
        x_turned = sig("x_turned")
        x_ready = sig("x_ready")
        x_low_ready = sig("x_low_ready")
        xw_done = sig("xw_done", SPT)
        xw_high = sig("xw_high", SPT)
        xw_low = sig("xw_low", SPT)
        logits_done = sig("logits_done")
        logits_t_done = sig("logits_t_done")
        maxed = sig("maxed", 2)
        shift_done = sig("shift_done", 2)
        exped = sig("exped")
        summed = sig("summed")
        inverted = sig("inverted")
        exps_turned = sig("exps_turned", 2)
        combine_ready = sig("combine_ready")
        dispatch_high = sig("dispatch_high", SPT)
        dispatch_low = sig("dispatch_low", SPT)
        h_done = sig("h_done", NH)
        gelu_done = sig("gelu_done", NH)
        mixed = sig("mixed", NH)
        gathered_ready = sig("gathered_ready")
        gathered_turned = sig("gathered_turned")
        gathered_t_ready = sig("gathered_t_ready")
        y_done = sig("y_done")
        residual_done = sig("residual_done")

        block = ctx.enter_context(nc.Block())

        def tile(t):
            return X[:, bass.ds(t, 1), :]

        def rows(b):
            return slice(SEQ * b, SEQ * b + SEQ)

        def all_turns(engine, turn):
            with engine.Fori(0, TURNS // 2 - 2) as k:
                turn(2 * k, 0, True, True, True)
                turn(2 * k + 1, 1, True, True, True)
            turn(TURNS - 4, 0, True, True, True)
            turn(TURNS - 3, 1, True, True, False)
            turn(TURNS - 2, 0, True, False, False)
            turn(TURNS - 1, 1, False, False, False)

        @block.gpsimd
        def _(pool):
            credit(pool, rooted, residual_done)
            tail.credit_pool(pool)
            pool.wait_ge(prep_v, 1)
            nc.gpsimd.tensor_tensor(slot_rn[:, :], slot_sq[:, 1, :], W["minus_half"][:, 0:C], ALU.pow).then_inc(prep, 1)

            def root(t):
                pool.wait_ge(scaled.sem, scaled.before(t, 1))
                pool.wait_ge(floored.sem, floored.now(t, 1))
                nc.gpsimd.tensor_tensor(rnorm[:, :], floor_ssq[:, :], W["minus_half"][:, 0:1], ALU.pow)\
                    .then_inc(rooted.sem, 1)

            def turn(t, par, one, two, three):
                pool.wait_ge(tail.added.sem, tail.added.before(t, 1))
                nc.gpsimd.tensor_copy(residual[:, :, :], tile(t)).then_inc(residual_done.sem, 1)
                if three:
                    root(t + 3)
                tail.root_pool(pool, t, W["minus_half"])

            root(0)
            root(1)
            root(2)
            all_turns(pool, turn)

        @block.scalar
        def _(act):
            credit(act, squared, x_ready, exped, xw_high, dispatch_high, gelu_done)
            nc.scalar.activation(w1_p[:, HI, :], W["moe_w1"], ACT.Copy).then_inc(parts_hi, 1)
            for c in range(C):
                last = nc.scalar.activation(slots_n[:, c, :], W["slots"][:, c, :], ACT.Square,
                                            accum_out=slot_sq[:, 0, c:c + 1])
            last.then_inc(prep, 1)
            act.wait_ge(prep, 3)
            act.wait_ge(prep_v, 4)
            nc.scalar.activation(slots_t[:, :], p_l[:, :], ACT.Copy, scale=gain_s[:, :]).then_inc(prep, 1)
            act.wait_ge(prep, 4)
            nc.scalar.activation(slots_p[:, HI, :], slots_t[:, :], ACT.Copy).then_inc(parts_hi, 1)

            def square(t):
                act.wait_ge(floored.sem, floored.before(t, 1))
                nc.scalar.activation(squares[:, :].unsqueeze(1), tile(t), ACT.Square, accum_out=ssq[:, :])\
                    .then_inc(squared.sem, 1)

            def x_copy(t, par, first=False, fenced=True):
                act.wait_ge(x_turned.sem, x_turned.now(t, 1))
                act.wait_ge(logits_t_done.sem, logits_t_done.before(t, 1))
                if not first:
                    act.wait_ge(xw_done.sem, xw_done.before(t - 1, SPT))
                if fenced:
                    act.wait_ge(tail.added.sem, tail.added.before(t - 2, 1))
                twice = p_x[:, 0, :].rearrange("p (b s) -> p b s", s=SEQ).unsqueeze(2).broadcast_to((P, SPT, 2, SEQ))
                nc.scalar.activation(x_t[:, :], p_x[:, 0, :], ACT.Copy, scale=gain_x[:, :])
                nc.scalar.activation(x_p[:, par, HI, :].rearrange("p (b k s) -> p b k s", b=SPT, k=2), twice, ACT.Copy,
                                     scale=gain_x[:, :]).then_inc(x_ready.sem, 1)

            def exp(t):
                act.wait_ge(exps_turned.sem, exps_turned.before(t, 2))
                act.wait_ge(summed.sem, summed.before(t, 1))
                act.wait_ge(inverted.sem, inverted.before(t, 1))
                act.wait_ge(shift_done.sem, shift_done.now(t, 2))
                nc.scalar.activation(exps[:, 0, :], shifted[:, 0, :], ACT.Exp, accum_out=sums[:, 0:1])
                nc.scalar.activation(exps[:, 1, :], shifted[:, 1, :], ACT.Exp).then_inc(exped.sem, 1)

            def xw_copy(t, par, b, first=False):
                if not first:
                    act.wait_ge(h_done.sem, h_done.before(t - 1, NH))
                act.wait_ge(xw_done.sem, xw_done.now(t, b + 1))
                nc.scalar.activation(xw[:, par, b, HI, :], p_xw[:, :], ACT.Copy).then_inc(xw_high.sem, 1)

            def dispatch_copy(t, par, b, first=False):
                if not first:
                    act.wait_ge(h_done.sem, h_done.before(t - 1, NH))
                act.wait_ge(exps_turned.sem, exps_turned.now(t, 2))
                nc.scalar.activation(dispatch[rows(b), par, b, :], p_lt[rows(b), :, :].rearrange("p c s -> p (c s)"), ACT.Copy)\
                    .then_inc(dispatch_high.sem, 1)

            def gelu(t, par, i):
                if i == 0:
                    act.wait_ge(inverted.sem, inverted.now(t, 1))
                act.wait_ge(mixed.sem, mixed.now(t, i - RING + 1) if i >= RING else mixed.before(t, NH - RING + i + 1))
                act.wait_ge(h_done.sem, h_done.now(t, i + 1))
                nc.scalar.activation(hidden[:, i % RING, :], p_h[:, i % 2, :], ACT.Gelu, scale=rsums[:, par, 1 + i:2 + i])\
                    .then_inc(gelu_done.sem, 1)

            def turn(t, par, one, two, three):
                for i in range(NH):
                    gelu(t, par, i)
                    if i == 0 and one:
                        dispatch_copy(t + 1, 1 - par, 0)
                    if i == 1 and one:
                        dispatch_copy(t + 1, 1 - par, 1)
                    if i == 2 and two:
                        x_copy(t + 2, par)
                    if i == 4 and one:
                        xw_copy(t + 1, 1 - par, 0)
                    if i == 3 and three:
                        square(t + 3)
                    if i == 7 and one:
                        xw_copy(t + 1, 1 - par, 1)
                if two:
                    exp(t + 2)

            square(0)
            x_copy(0, 0, True, False)
            square(1)
            xw_copy(0, 0, 0, True)
            xw_copy(0, 0, 1, True)
            exp(0)
            dispatch_copy(0, 0, 0, True)
            dispatch_copy(0, 0, 1, True)
            x_copy(1, 1, fenced=False)
            square(2)
            exp(1)
            all_turns(act, turn)

        @block.tensor
        def _(pe):
            credit(pe, x_turned, xw_done, logits_done, logits_t_done, exps_turned, h_done, mixed, gathered_turned, y_done)
            pe.wait_ge(prep_v, 3)
            for c in range(C):
                last = pe.transpose(p_l[:, c * P:(c + 1) * P], slots_n[:, c, :], W["ident"])
            last.then_inc(prep, 1)
            pe.wait_ge(parts_lo, 2)

            def three_passes(out, left_hi, left_lo, right):
                pe.matmul(out, left_hi, right[:, HI, :], start=True, stop=False)
                pe.matmul(out, left_lo, right[:, HI, :], start=False, stop=False)
                return pe.matmul(out, left_hi, right[:, LO, :], start=False, stop=True)

            def x_transpose(t, first=False):
                pe.wait_ge(scaled.sem, scaled.now(t, 1))
                pe.wait_ge(x_low_ready.sem, x_low_ready.before(t, 1))
                if not first:
                    pe.wait_ge(tail.added.sem, tail.added.before(t - 3, 1))
                pe.transpose(p_x[:, 0, :], x_scaled[:, :], W["ident"]).then_inc(x_turned.sem, 1)

            def times_w1(t, par, b):
                pe.wait_ge(x_low_ready.sem, x_low_ready.now(t, 1))
                pe.wait_ge(xw_low.sem, xw_low.now(t, 1) if b else xw_low.before(t, SPT))
                cols = slice(P * b, P * b + P)
                three_passes(p_xw[:, :], x_p[:, par, HI, cols], x_p[:, par, LO, cols], w1_p).then_inc(xw_done.sem, 1)

            def logits(t, par, first=False):
                pe.wait_ge(x_low_ready.sem, x_low_ready.now(t, 1))
                if not first:
                    pe.wait_ge(combine_ready.sem, combine_ready.before(t, 1))
                    pe.wait_ge(dispatch_low.sem, dispatch_low.before(t, SPT))
                cols = slice(SEQ, SEQ + P)
                three_passes(p_l[:, :], x_p[:, par, HI, cols], x_p[:, par, LO, cols], slots_p).then_inc(logits_done.sem, 1)
                for c in range(C):
                    last = pe.matmul(p_lt[:, c, :], slots_t[:, c * P:(c + 1) * P], x_t[:, :], start=True, stop=True)
                last.then_inc(logits_t_done.sem, 1)

            def exps_transpose(t):
                pe.wait_ge(exped.sem, exped.now(t, 1))
                for k in range(2):
                    for c in range(C):
                        out = p_lt[:, c, :] if k else p_l[:, c * P:(c + 1) * P]
                        last = pe.transpose(out, exps[:, k, c * P:(c + 1) * P], W["ident"])
                    last.then_inc(exps_turned.sem, 1)

            def hidden_block(t, par, i):
                c, b = i // SPT, i % SPT
                if i < SPT:
                    pe.wait_ge(xw_low.sem, xw_low.now(t, b + 1))
                    pe.wait_ge(dispatch_low.sem, dispatch_low.now(t, b + 1))
                pe.wait_ge(gelu_done.sem, gelu_done.now(t, i - 1) if i >= 2 else gelu_done.before(t, NH - 1 + i))
                for part in (HI, LO):
                    last = pe.matmul(p_h[:, i % 2, :], dispatch[:, par, b, c * P:(c + 1) * P], xw[:, par, b, part, :],
                                     start=(part == HI), stop=(part == LO))
                last.then_inc(h_done.sem, 1)

            def gather_block(t, par, i):
                c, b = i // SPT, i % SPT
                if i == 0:
                    pe.wait_ge(combine_ready.sem, combine_ready.now(t, 1))
                    pe.wait_ge(gathered_ready.sem, gathered_ready.before(t, 1))
                pe.wait_ge(gelu_done.sem, gelu_done.now(t, i + 1))
                pe.matmul(p_g[rows(b), :], combine_t[:, par, c, rows(b)], hidden[:, i % RING, :], start=(c == 0),
                          stop=(c == C - 1)).then_inc(mixed.sem, 1)

            def turn(t, par, one, two, three):
                hidden_block(t, par, 2)
                gather_block(t, par, 0)
                hidden_block(t, par, 3)
                gather_block(t, par, 1)
                hidden_block(t, par, 4)
                gather_block(t, par, 2)
                hidden_block(t, par, 5)
                if two:
                    logits(t + 2, par)
                gather_block(t, par, 3)
                hidden_block(t, par, 6)
                gather_block(t, par, 4)
                hidden_block(t, par, 7)
                if one:
                    times_w1(t + 1, 1 - par, 1)
                gather_block(t, par, 5)
                gather_block(t, par, 6)
                gather_block(t, par, 7)
                if one:
                    hidden_block(t + 1, 1 - par, 0)
                pe.wait_ge(gathered_t_ready.sem, gathered_t_ready.before(t, 1))
                pe.wait_ge(gathered_ready.sem, gathered_ready.now(t, 1))
                for c in range(C):
                    last = pe.transpose(p_tr[:, c, :], gathered[:, c * P:(c + 1) * P], W["ident"])
                last.then_inc(gathered_turned.sem, 1)
                if one:
                    hidden_block(t + 1, 1 - par, 1)
                if two:
                    times_w1(t + 2, par, 0)
                if three:
                    x_transpose(t + 3)
                if two:
                    exps_transpose(t + 2)
                pe.wait_ge(gathered_t_ready.sem, gathered_t_ready.now(t, 1))
                for c in range(C):
                    last = pe.matmul(p_x[:, 1, :], gathered_t[:, c, :], W["moe_w2"][:, c, :], start=(c == 0),
                                     stop=(c == C - 1))
                last.then_inc(y_done.sem, 1)

            x_transpose(0, True)
            times_w1(0, 0, 0)
            logits(0, 0, True)
            x_transpose(1, True)
            times_w1(0, 0, 1)
            exps_transpose(0)
            logits(1, 1)
            times_w1(1, 1, 0)
            x_transpose(2, True)
            hidden_block(0, 0, 0)
            hidden_block(0, 0, 1)
            exps_transpose(1)
            all_turns(pe, turn)

        @block.vector
        def _(dve):
            credit(dve, floored, scaled, x_low_ready, xw_low, maxed, shift_done, summed, inverted, combine_ready,
                   dispatch_low, gathered_ready, gathered_t_ready)
            tail.credit_vector(dve)
            dve.wait_ge(prep, 1)
            nc.vector.tensor_scalar(slot_sq[:, 1, :], slot_sq[:, 0, :], NORM_FLOOR, None, ALU.max).then_inc(prep_v, 1)
            dve.wait_ge(prep, 2)
            for c in range(C):
                last = nc.vector.tensor_scalar(slots_n[:, c, :], W["slots"][:, c, :], slot_rn[:, c:c + 1], None, ALU.mult)
            last.then_inc(prep_v, 2)
            nc.vector.tensor_scalar(gain_x[:, :], W["gamma_x"], ROOT, None, ALU.mult)
            nc.vector.tensor_scalar(gain_s[:, :], W["gamma_slot"], ROOT, None, ALU.mult).then_inc(prep_v, 1)
            dve.wait_ge(parts_hi, 1)
            nc.vector.tensor_tensor(w1_p[:, LO, :], W["moe_w1"], w1_p[:, HI, :].bitcast(F32), ALU.subtract).then_inc(parts_lo, 1)
            dve.wait_ge(parts_hi, 2)
            nc.vector.tensor_tensor(slots_p[:, LO, :], slots_t[:, :], slots_p[:, HI, :].bitcast(F32), ALU.subtract)\
                .then_inc(parts_lo, 1)

            def floor_row(t):
                dve.wait_ge(squared.sem, squared.now(t, 1))
                dve.wait_ge(rooted.sem, rooted.before(t, 1))
                nc.vector.tensor_scalar(floor_ssq[:, :], ssq[:, :], NORM_FLOOR, None, ALU.max).then_inc(floored.sem, 1)

            def scale_row(t):
                dve.wait_ge(x_turned.sem, x_turned.before(t, 1))
                dve.wait_ge(rooted.sem, rooted.now(t, 1))
                nc.vector.tensor_scalar(x_scaled[:, :].unsqueeze(1), tile(t), rnorm[:, :], None, ALU.mult)\
                    .then_inc(scaled.sem, 1)

            def x_low(t, par):
                dve.wait_ge(x_ready.sem, x_ready.now(t, 1))
                hi, lo = (x_p[:, par, k, :].rearrange("p (b k s) -> p b k s", b=SPT, k=2) for k in (HI, LO))
                for b in range(SPT):
                    twice = p_x[:, 0, SEQ * b:SEQ * b + SEQ].unsqueeze(1).broadcast_to((P, 2, SEQ))
                    last = nc.vector.scalar_tensor_tensor(out=lo[:, b, :, :], in0=twice, scalar=gain_x[:, :],
                                                          in1=hi[:, b, :, :].bitcast(F32), op0=ALU.mult, op1=ALU.subtract)
                last.then_inc(x_low_ready.sem, 1)

            def xw_rest(t, par, b):
                dve.wait_ge(xw_high.sem, xw_high.now(t, b + 1))
                nc.vector.tensor_tensor(xw[:, par, b, LO, :], p_xw[:, :], xw[:, par, b, HI, :].bitcast(F32), ALU.subtract)\
                    .then_inc(xw_low.sem, 1)

            def dispatch_rest(t, par, b):
                dve.wait_ge(dispatch_high.sem, dispatch_high.now(t, b + 1))
                nc.vector.tensor_tensor(dispatch[rows(1 - b), par, b, :], p_lt[rows(b), :, :].rearrange("p c s -> p (c s)"),
                                        dispatch[rows(b), par, b, :].bitcast(F32), ALU.subtract).then_inc(dispatch_low.sem, 1)

            def shift(t):
                dve.wait_ge(exped.sem, exped.before(t, 1))
                dve.wait_ge(logits_done.sem, logits_done.now(t, 1))
                nc.vector.tensor_reduce(neg_max[:, 0:1], p_l[:, :], AX_X, ALU.max, negate=True).then_inc(maxed.sem, 1)
                dve.wait_ge(maxed.sem, maxed.now(t, 1))
                nc.vector.tensor_scalar(shifted[:, 0, :], p_l[:, :], neg_max[:, 0:1], None, ALU.add)\
                    .then_inc(shift_done.sem, 1)
                logits_t = p_lt[:, :, :].rearrange("p c (b s) -> p (c b) s", s=SEQ)
                dve.wait_ge(logits_t_done.sem, logits_t_done.now(t, 1))
                nc.vector.tensor_reduce(neg_max[:, 1:], logits_t, AX_X, ALU.max, negate=True).then_inc(maxed.sem, 1)
                dve.wait_ge(maxed.sem, maxed.now(t, 2))
                nc.vector.tensor_tensor(shifted[:, 1, :].rearrange("p (c s) -> p c s", s=SEQ), logits_t,
                                        neg_max[:, 1:].unsqueeze(2).broadcast_to((P, NH, SEQ)), ALU.add)\
                    .then_inc(shift_done.sem, 1)

            def sum_up(t, par, first=False):
                dve.wait_ge(inverted.sem, inverted.before(t, 1))
                dve.wait_ge(exped.sem, exped.now(t, 1))
                nc.vector.tensor_reduce(sums[:, 1:], exps[:, 1, :].rearrange("p (c s) -> p c s", s=SEQ), AX_X, ALU.add)\
                    .then_inc(summed.sem, 1)
                if not first:
                    dve.wait_ge(gelu_done.sem, gelu_done.before(t - 1, NH))
                    dve.wait_ge(gathered_ready.sem, gathered_ready.before(t - 1, 1))
                dve.wait_ge(summed.sem, summed.now(t, 1))
                nc.vector.reciprocal(rsums[:, par, :], sums[:, :]).then_inc(inverted.sem, 1)

            def combine_copy(t, par, first=False):
                if not first:
                    dve.wait_ge(mixed.sem, mixed.before(t - 1, NH))
                dve.wait_ge(exps_turned.sem, exps_turned.now(t, 1))
                nc.vector.tensor_copy(combine_t[:, par, :, :], p_l[:, :].rearrange("p (c s) -> p c s", s=P))\
                    .then_inc(combine_ready.sem, 1)

            def turn(t, par, one, two, three):
                if two:
                    x_low(t + 2, par)
                if one:
                    xw_rest(t + 1, 1 - par, 0)
                if three:
                    floor_row(t + 3)
                if two:
                    shift(t + 2)
                if three:
                    scale_row(t + 3)
                if one:
                    xw_rest(t + 1, 1 - par, 1)
                dve.wait_ge(gathered_turned.sem, gathered_turned.before(t, 1))
                dve.wait_ge(mixed.sem, mixed.now(t, NH))
                nc.vector.tensor_scalar(gathered[:, :], p_g[:, :], rsums[:, par, 0:1], None, ALU.mult)                    .then_inc(gathered_ready.sem, 1)
                dve.wait_ge(y_done.sem, y_done.before(t, 1))
                dve.wait_ge(gathered_turned.sem, gathered_turned.now(t, 1))
                nc.vector.tensor_copy(gathered_t[:, :, :], p_tr[:, :, :]).then_inc(gathered_t_ready.sem, 1)
                if two:
                    sum_up(t + 2, par)
                    combine_copy(t + 2, par)
                    dispatch_rest(t + 2, par, 0)
                dve.wait_ge(residual_done.sem, residual_done.now(t, 1))
                dve.wait_ge(y_done.sem, y_done.now(t, 1))
                tail.moments_vector(dve, t, p_x[:, 1:2, :], residual[:, :, :])
                if two:
                    dispatch_rest(t + 2, par, 1)
                tail.write_vector(dve, t, lambda j: tile(t))

            floor_row(0)
            scale_row(0)
            x_low(0, 0)
            floor_row(1)
            scale_row(1)
            xw_rest(0, 0, 0)
            shift(0)
            xw_rest(0, 0, 1)
            sum_up(0, 0, True)
            combine_copy(0, 0, True)
            dispatch_rest(0, 0, 0)
            dispatch_rest(0, 0, 1)
            x_low(1, 1)
            shift(1)
            floor_row(2)
            scale_row(2)
            sum_up(1, 1)
            combine_copy(1, 1)
            dispatch_rest(1, 1, 0)
            dispatch_rest(1, 1, 1)
            all_turns(dve, turn)
def stage_cross(nc, X, W, ctx_in, mask):
    NT = 2
    NB = NT * SPT
    TURNS = TILES // NT
    XHEADS, XHD = 2, 64
    SOURCES = 2
    MASKED = -float(np.finfo(np.float32).max)
    with ExitStack() as ctx:
        def sb(n, shape, dt=F32):
            return ctx.enter_context(nc.sbuf_tensor("cr_" + n, shape, dt))

        def ps(n, shape):
            return ctx.enter_context(nc.psum_tensor("cr_" + n, shape, F32))

        def sig(n, per=1):
            return Signal(ctx, nc, "cr_" + n, per)

        c_in = sb("c_in", [P, NT, D])
        masks = sb("masks", [P, BATCH, SEQ], U8)
        q_gain = sb("q_gain", [P, 1])
        stats = sb("stats", [P, NT, SOURCES, 6])
        moments = sb("moments", [P, NT, SOURCES, 2])
        var_eps = sb("var_eps", [P, NT, SOURCES])
        rstd = sb("rstd", [P, NT, SOURCES])
        scrap = sb("scrap", [P, 1])
        normed = sb("normed", [P, NT, SOURCES, D])
        feats = sb("feats", [P, SOURCES, NT, P])
        squares = sb("squares", [P, NT, 3, D])
        ssq = sb("ssq", [P, NT * 3 * XHEADS])
        floor_ssq = sb("floor_ssq", [P, NT * 3 * XHEADS])
        rnorm = sb("rnorm", [P, NT * 3 * XHEADS])
        scaled = sb("scaled", [P, NT, 3, D])
        spread_q = sb("spread_q", [P, NB, XHEADS, SEQ])
        keys = sb("keys", [P, NB, 2, SEQ])
        values = sb("values", [P, NB, D])
        neg_max = sb("neg_max", [P, NB])
        probs = sb("probs", [P, NB, P])
        sums = sb("sums", [P, NB])
        rsum = sb("rsum", [P, NB])
        probs_n = sb("probs_n", [P, NB, P])
        probs_t = sb("probs_t", [P, NB, P])
        mixed = sb("mixed", [P, NB, SEQ])
        residual = sb("residual", [P, NT, D])
        p_t = ps("p_t", [P, SOURCES * NT, P])
        p_q = ps("p_q", [P, NT, D])
        p_key = ps("p_key", [P, NT, SOURCES, D])
        p_v = ps("p_v", [P, NT, SOURCES, D])
        p_k = ps("p_k", [P, SOURCES, NT, P])
        p_s = ps("p_s", [P, NB, P])
        p_pt = ps("p_pt", [P, NB, P])
        p_o = ps("p_o", [P, NB, XHEADS, SEQ])
        p_y = p_o[:, 0:NT, :, :].rearrange("p j h s -> p j (h s)")

        tail = NormTail(ctx, nc, "cr_tail", NT)
        constants = nc.alloc_semaphore("cr_constants")
        mask_in = nc.alloc_semaphore("cr_mask_in")
        mask_ready = nc.alloc_semaphore("cr_mask_ready")
        c_landed = sig("c_landed", 16)
        counted, aggregated, floored, rooted = sig("counted"), sig("aggregated"), sig("floored"), sig("rooted")
        normed_done = sig("normed_done")
        turned = sig("turned")
        feats_done = sig("feats_done")
        qk_done = sig("qk_done")
        v_done = sig("v_done")
        squared = sig("squared")
        summed_sq = sig("summed_sq")
        floored_sq = sig("floored_sq")
        rooted_sq = sig("rooted_sq")
        scale_done = sig("scale_done")
        qk_turned = sig("qk_turned")
        qk_ready = sig("qk_ready")
        values_ready = sig("values_ready")
        scored = sig("scored")
        masked = sig("masked")
        maxed = sig("maxed")
        exped = sig("exped")
        inverted = sig("inverted")
        probs_normed = sig("probs_normed")
        probs_turned = sig("probs_turned")
        probs_ready = sig("probs_ready")
        weighted = sig("weighted")
        mixed_ready = sig("mixed_ready")
        projected = sig("projected")
        residual_done = sig("residual_done")

        block = ctx.enter_context(nc.Block())

        def tiles(t):
            return X[:, bass.ds(t * NT, NT), :]

        def all_turns(engine, turn):
            with engine.Fori(0, TURNS - 3) as t:
                turn(t, True, True, True)
            turn(TURNS - 3, True, True, False)
            turn(TURNS - 2, True, False, False)
            turn(TURNS - 1, False, False, False)

        @block.sync
        def _(sp):
            sp.dma_start(masks[:, :, :], mask.rearrange("b s -> (b s)").partition_broadcast(P)).then_inc(mask_in, 16)
            sp.dma_start(c_in[:, :, :], ctx_in[0:NT * P, :].rearrange("(j p) d -> p j d", p=P)).then_inc(c_landed.sem, 16)
            with sp.Fori(1, TURNS) as t:
                sp.wait_ge(normed_done.sem, normed_done.before(t, 1))
                sp.dma_start(c_in[:, :, :], ctx_in[bass.ds(t * (NT * P), NT * P), :].rearrange("(j p) d -> p j d", p=P))\
                    .then_inc(c_landed.sem, 16)
            sp.wait_ge(c_landed.sem, 16 * TURNS)
            sp.wait_ge(mask_in, 16)

        @block.gpsimd
        def _(pool):
            nc.gpsimd.memset(spread_q[:, :, :, :], 0.0).then_inc(constants, 1)
            credit(pool, rooted, rooted_sq, probs_normed, residual_done)
            tail.credit_pool(pool)

            pool.wait_ge(mask_in, 16)
            nc.gpsimd.tensor_scalar(masks[:, :, :], masks[:, :, :], -1.0, 1.0, ALU.mult, ALU.add).then_inc(mask_ready, 1)

            def root(t):
                pool.wait_ge(normed_done.sem, normed_done.before(t, 1))
                pool.wait_ge(floored.sem, floored.now(t, 1))
                nc.gpsimd.tensor_tensor(rstd[:, :, :], var_eps[:, :, :],
                                        W["minus_half"][:, 0:4].rearrange("p (a b) -> p a b", a=NT), ALU.pow)\
                    .then_inc(rooted.sem, 1)

            def root_sq(t):
                pool.wait_ge(scale_done.sem, scale_done.before(t, 1))
                pool.wait_ge(floored_sq.sem, floored_sq.now(t, 1))
                nc.gpsimd.tensor_tensor(rnorm[:, :], floor_ssq[:, :], W["minus_half"][:, 0:12], ALU.pow)\
                    .then_inc(rooted_sq.sem, 1)

            def normalise(t):
                pool.wait_ge(probs_turned.sem, probs_turned.before(t, 1))
                pool.wait_ge(inverted.sem, inverted.now(t, 1))
                nc.gpsimd.tensor_tensor(probs_n[:, :, :], probs[:, :, :],
                                        rsum[:, :].unsqueeze(2).broadcast_to((P, NB, P)), ALU.mult)\
                    .then_inc(probs_normed.sem, 1)

            def turn(t, one, two, three):
                nc.gpsimd.tensor_tensor(residual[:, :, :], tiles(t), W["xout_b"].unsqueeze(1).broadcast_to((P, NT, D)),
                                        ALU.add).then_inc(residual_done.sem, 1)
                if three:
                    root(t + 3)
                if two:
                    root_sq(t + 2)
                if one:
                    normalise(t + 1)
                tail.root_pool(pool, t, W["minus_half"])

            root(0)
            root(1)
            root_sq(0)
            root(2)
            root_sq(1)
            normalise(0)
            all_turns(pool, turn)

        @block.tensor
        def _(pe):
            credit(pe, turned, qk_done, v_done, qk_turned, scored, probs_turned, weighted, projected)
            pe.wait_ge(constants, 2)

            def transposes(t, queries=None):
                pe.wait_ge(normed_done.sem, normed_done.now(t, 1))
                if queries is not None:
                    pe.wait_ge(qk_ready.sem, qk_ready.now(queries, 1))
                pe.wait_ge(feats_done.sem, feats_done.before(t, 1))
                for j in range(NT):
                    for s in range(SOURCES):
                        last = pe.transpose(p_t[:, s * NT + j, :], normed[:, j, s, :], W["ident"])
                last.then_inc(turned.sem, 1)

            def project_heads(t):
                pe.wait_ge(feats_done.sem, feats_done.now(t, 1))
                pe.wait_ge(scale_done.sem, scale_done.before(t, 1))
                for j in range(NT):
                    pe.matmul(p_q[:, j, :], feats[:, 1, j, :], W["XWq"], start=True, stop=True)
                    for s in range(SOURCES):
                        last = pe.matmul(p_key[:, j, s, :], feats[:, s, j, :], W["XWkv"][:, 0:D], start=True, stop=True)
                last.then_inc(qk_done.sem, 1)

            def project_values(t):
                pe.wait_ge(values_ready.sem, values_ready.before(t, 1))
                for j in range(NT):
                    for s in range(SOURCES):
                        last = pe.matmul(p_v[:, j, s, :], feats[:, s, j, :], W["XWkv"][:, D:], start=True, stop=True)
                last.then_inc(v_done.sem, 1)

            def qk_transposes(t, sources):
                pe.wait_ge(scale_done.sem, scale_done.now(t, 1))
                pe.wait_ge(qk_ready.sem, qk_ready.before(t, 1))
                pe.wait_ge(feats_done.sem, feats_done.now(sources, 1))
                for j in range(NT):
                    pe.transpose(p_t[:, j, :], scaled[:, j, 0, :], W["ident"])
                    for s in range(SOURCES):
                        last = pe.transpose(p_k[:, s, j, :], scaled[:, j, 1 + s, :], W["ident"])
                last.then_inc(qk_turned.sem, 1)

            def scores(t):
                pe.wait_ge(qk_ready.sem, qk_ready.now(t, 1))
                pe.wait_ge(exped.sem, exped.before(t, 1))
                for b in range(NB):
                    last = pe.matmul(p_s[:, b, :], spread_q[:, b, :, :], keys[:, b, :, :], start=True, stop=True)
                last.then_inc(scored.sem, 1)

            def weigh(t):
                pe.wait_ge(probs_ready.sem, probs_ready.before(t, 1))
                pe.wait_ge(probs_normed.sem, probs_normed.now(t, 1))
                for b in range(NB):
                    last = pe.transpose(p_pt[:, b, :], probs_n[:, b, :], W["ident"])
                last.then_inc(probs_turned.sem, 1)

            def mix(t):
                pe.wait_ge(values_ready.sem, values_ready.now(t, 1))
                pe.wait_ge(mixed_ready.sem, mixed_ready.before(t, 1))
                pe.wait_ge(tail.added.sem, tail.added.before(t, 1))
                pe.wait_ge(probs_ready.sem, probs_ready.now(t, 1))
                for b in range(NB):
                    last = pe.matmul(p_o[:, b, :, :], values[:, b, :], probs_t[:, b, :], start=True, stop=True)
                last.then_inc(weighted.sem, 1)

            def project(t):
                pe.wait_ge(mixed_ready.sem, mixed_ready.now(t, 1))
                for j in range(NT):
                    last = pe.matmul(p_y[:, j, :], mixed[:, SPT * j:SPT * j + SPT, :], W["XWout"], start=True, stop=True)
                last.then_inc(projected.sem, 1)

            def turn(t, one, two, three):
                if one:
                    qk_transposes(t + 1, t + 2 if two else t + 1)
                if two:
                    project_heads(t + 2)
                weigh(t)
                mix(t)
                if one:
                    scores(t + 1)
                project(t)
                if two:
                    project_values(t + 2)
                if three:
                    transposes(t + 3, queries=t + 1)

            transposes(0)
            project_heads(0)
            project_values(0)
            transposes(1)
            qk_transposes(0, 1)
            project_heads(1)
            scores(0)
            project_values(1)
            transposes(2, queries=0)
            all_turns(pe, turn)

        @block.scalar
        def _(act):
            credit(act, feats_done, squared, qk_ready, exped, values_ready, mixed_ready)
            act.wait_ge(constants, 2)

            def to_features(t):
                act.wait_ge(turned.sem, turned.now(t, 1))
                act.wait_ge(v_done.sem, v_done.before(t, 1))
                for s, n in ((0, "lnx"), (1, "lnl")):
                    last = nc.scalar.activation(feats[:, s, :, :], p_t[:, s * NT:s * NT + NT, :], ACT.Identity,
                                                bias=W[n + "_b"], scale=W[n + "_g"])
                last.then_inc(feats_done.sem, 1)

            def square(t):
                act.wait_ge(summed_sq.sem, summed_sq.before(t, 1))
                act.wait_ge(qk_done.sem, qk_done.now(t, 1))
                nc.scalar.activation(squares[:, :, 0, :], p_q[:, :, :], ACT.Square)
                nc.scalar.activation(squares[:, :, 1:3, :], p_key[:, :, :, :], ACT.Square).then_inc(squared.sem, 1)

            def spread(t):
                act.wait_ge(scored.sem, scored.before(t, 1))
                act.wait_ge(qk_turned.sem, qk_turned.now(t, 1))
                for h in range(XHEADS):
                    r = slice(XHD * h, XHD * h + XHD)
                    nc.scalar.activation(spread_q[r, :, h, :], p_t[r, 0:NT, :].rearrange("p j (b s) -> p (j b) s", s=SEQ),
                                         ACT.Copy, scale=q_gain[r, :])
                for b in range(SPT):
                    for s in range(SOURCES):
                        out = keys[:, :, s ^ b, :].rearrange("p (j b) s -> p j b s", b=SPT)[:, :, b, :]
                        last = nc.scalar.activation(out, p_k[:, s, :, SEQ * b:SEQ * b + SEQ], ACT.Copy, scale=W["k_gamma"])
                last.then_inc(qk_ready.sem, 1)

            def place_values(t):
                act.wait_ge(v_done.sem, v_done.now(t, 1))
                act.wait_ge(weighted.sem, weighted.before(t, 1))
                for b in range(SPT):
                    for s in range(SOURCES):
                        src = p_v[SEQ * b:SEQ * b + SEQ, :, s, :]
                        to = SEQ * (s ^ b)
                        last = nc.scalar.activation(
                            values[to:to + SEQ, :, :].rearrange("p (j b) d -> p j b d", b=SPT)[:, :, b, :], src, ACT.Copy)
                last.then_inc(values_ready.sem, 1)

            def copy_mixed(t):
                act.wait_ge(projected.sem, projected.before(t, 1))
                act.wait_ge(weighted.sem, weighted.now(t, 1))
                for h in range(XHEADS):
                    r = slice(XHD * h, XHD * h + XHD)
                    last = nc.scalar.activation(mixed[r, :, :], p_o[r, :, h, :], ACT.Copy)
                last.then_inc(mixed_ready.sem, 1)

            def exp(t):
                act.wait_ge(probs_normed.sem, probs_normed.before(t, 1))
                act.wait_ge(inverted.sem, inverted.before(t, 1))
                act.wait_ge(maxed.sem, maxed.now(t, 1))
                for b in range(NB):
                    last = nc.scalar.activation(probs[:, b, :], p_s[:, b, :], ACT.Exp, bias=neg_max[:, b:b + 1],
                                                accum_out=sums[:, b:b + 1])
                last.then_inc(exped.sem, 1)

            def turn(t, one, two, three):
                if one:
                    spread(t + 1)
                if two:
                    square(t + 2)
                copy_mixed(t)
                if one:
                    place_values(t + 1)
                    exp(t + 1)
                if three:
                    to_features(t + 3)

            to_features(0)
            square(0)
            to_features(1)
            spread(0)
            square(1)
            place_values(0)
            exp(0)
            to_features(2)
            all_turns(act, turn)

        @block.vector
        def _(dve):
            nc.vector.tensor_scalar(q_gain[:, :], W["q_gamma"], XHD ** -0.5, None, ALU.mult).then_inc(constants, 1)
            credit(dve, counted, aggregated, floored, normed_done, summed_sq, floored_sq, scale_done, masked,
                   maxed, inverted, probs_ready)
            tail.credit_vector(dve)

            def norm_inputs(t):
                dve.wait_ge(aggregated.sem, aggregated.before(t, 1))
                dve.wait_ge(c_landed.sem, (t + 1) * 16)
                for j in range(NT):
                    nc.vector.bn_stats(stats[:, j, 0, :], c_in[:, j, :])
                    last = nc.vector.bn_stats(stats[:, j, 1, :], X[:, bass.ds(t * NT + j, 1), :])
                last.then_inc(counted.sem, 1)
                dve.wait_ge(counted.sem, counted.now(t, 1))
                nc.vector.memset(scrap[:, :], 0.0)
                for j in range(NT):
                    for s in range(SOURCES):
                        last = nc.vector.bn_aggr(moments[:, j, s, :], stats[:, j, s, :])
                last.then_inc(aggregated.sem, 1)
                dve.wait_ge(aggregated.sem, aggregated.now(t, 1))
                nc.vector.tensor_scalar(var_eps[:, :, :], moments[:, :, :, 1], LN_EPS, None, ALU.add).then_inc(floored.sem, 1)

            def write_inputs(t):
                dve.wait_ge(turned.sem, turned.before(t, 1))
                dve.wait_ge(rooted.sem, rooted.now(t, 1))
                for j in range(NT):
                    for s, src in ((0, c_in[:, j, :].unsqueeze(1)), (1, X[:, bass.ds(t * NT + j, 1), :])):
                        last = nc.vector.tensor_scalar(normed[:, j, s, :].unsqueeze(1), src, moments[:, j, s, 0:1],
                                                       rstd[:, j, s:s + 1], ALU.subtract, ALU.mult)
                last.then_inc(normed_done.sem, 1)

            def head_norms(t):
                dve.wait_ge(squared.sem, squared.now(t, 1))
                dve.wait_ge(floored_sq.sem, floored_sq.before(t, 1))
                nc.vector.tensor_reduce(ssq[:, :], squares[:, :, :, :].rearrange("p j k (h d) -> p (j k h) d", d=XHD),
                                        AX_X, ALU.add).then_inc(summed_sq.sem, 1)
                dve.wait_ge(summed_sq.sem, summed_sq.now(t, 1))
                dve.wait_ge(rooted_sq.sem, rooted_sq.before(t, 1))
                nc.vector.tensor_scalar(floor_ssq[:, :], ssq[:, :], 1.0 / XHD, 1e-16, ALU.mult, ALU.max)\
                    .then_inc(floored_sq.sem, 1)

            def scale_heads(t):
                dve.wait_ge(qk_turned.sem, qk_turned.before(t, 1))
                dve.wait_ge(rooted_sq.sem, rooted_sq.now(t, 1))
                for j in range(NT):
                    a = j * 3 * XHEADS
                    nc.vector.tensor_tensor(scaled[:, j, 0, :].rearrange("p (h d) -> p h d", d=XHD),
                                            p_q[:, j, :].rearrange("p (h d) -> p h d", d=XHD),
                                            rnorm[:, a:a + 2].unsqueeze(2).broadcast_to((P, 2, XHD)), ALU.mult)
                    last = nc.vector.tensor_tensor(scaled[:, j, 1:3, :].rearrange("p k (h d) -> p k h d", d=XHD),
                                                   p_key[:, j, :, :].rearrange("p k (h d) -> p k h d", d=XHD),
                                                   rnorm[:, a + 2:a + 6].rearrange("p (k h) -> p k h", h=2).unsqueeze(3)
                                                   .broadcast_to((P, 2, 2, XHD)), ALU.mult)
                last.then_inc(scale_done.sem, 1)

            def mask_scores(t):
                dve.wait_ge(scored.sem, scored.now(t, 1))
                for b in range(NB):
                    cols = slice(0, SEQ) if b % 2 == 0 else slice(SEQ, P)
                    last = nc.vector.scalar_tensor_tensor(out=p_s[:, b:b + 1, cols], in0=masks[:, bass.ds(t * NB + b, 1), :],
                                                          scalar=MASKED, in1=p_s[:, b:b + 1, cols], op0=ALU.mult, op1=ALU.add)
                last.then_inc(masked.sem, 1)
                dve.wait_ge(masked.sem, masked.now(t, 1))
                nc.vector.tensor_reduce(neg_max[:, :], p_s[:, :, :], AX_X, ALU.max, negate=True).then_inc(maxed.sem, 1)

            def invert(t):
                dve.wait_ge(probs_normed.sem, probs_normed.before(t, 1))
                dve.wait_ge(exped.sem, exped.now(t, 1))
                nc.vector.reciprocal(rsum[:, :], sums[:, :]).then_inc(inverted.sem, 1)

            def copy_probs(t):
                dve.wait_ge(weighted.sem, weighted.before(t, 1))
                dve.wait_ge(probs_turned.sem, probs_turned.now(t, 1))
                nc.vector.tensor_copy(probs_t[:, :, :], p_pt[:, :, :]).then_inc(probs_ready.sem, 1)

            def turn(t, one, two, three):
                copy_probs(t)
                if three:
                    norm_inputs(t + 3)
                if two:
                    head_norms(t + 2)
                if one:
                    mask_scores(t + 1)
                if three:
                    write_inputs(t + 3)
                if two:
                    scale_heads(t + 2)
                if one:
                    invert(t + 1)
                dve.wait_ge(residual_done.sem, residual_done.now(t, 1))
                dve.wait_ge(projected.sem, projected.now(t, 1))
                tail.moments_vector(dve, t, p_y, residual[:, :, :])
                tail.write_vector(dve, t, lambda j: X[:, bass.ds(t * NT + j, 1), :])

            norm_inputs(0)
            write_inputs(0)
            norm_inputs(1)
            write_inputs(1)
            dve.wait_ge(mask_ready, 1)
            head_norms(0)
            scale_heads(0)
            norm_inputs(2)
            write_inputs(2)
            head_norms(1)
            mask_scores(0)
            scale_heads(1)
            invert(0)
            all_turns(dve, turn)
def stage_experts(nc, X, W, rms_w, w1, w2, landed, out):
    GT = 4
    GN = GT * P
    TURNS = TILES // GT
    HC = EH // P
    ORDER = [ROUTED] + list(range(ROUTED)) + [ROUTED + 1]
    RMS_EPS = 1.1920929e-07
    with ExitStack() as ctx:
        def sb(n, shape, dt=F32):
            return ctx.enter_context(nc.sbuf_tensor("ex_" + n, shape, dt))

        def ps(n, shape):
            return ctx.enter_context(nc.psum_tensor("ex_" + n, shape, F32))

        def sig(n, per=1):
            return Signal(ctx, nc, "ex_" + n, per)

        squares = sb("squares", [P, GT, D])
        ssq = sb("ssq", [P, GT])
        mean_sq = sb("mean_sq", [P, GT])
        rnorm = sb("rnorm", [P, GT])
        x_raw = sb("x_raw", [P, GT, D])
        x_scaled = sb("x_scaled", [P, GT, D])
        x_raw_t = sb("x_raw_t", [P, GN])
        x_hi = sb("x_hi", [P, GN], F32R)
        x_lo = sb("x_lo", [P, GN], F32R)
        w1_hi = sb("w1_hi", [P, EXPERTS, EH], F32R)
        w1_lo = sb("w1_lo", [P, EXPERTS, EH], F32R)
        hidden = sb("hidden", [P, 4, GN])
        acc = sb("acc", [P, GT, D])
        R = [P, GT, ROUTED]
        top = sb("top", [P, GT, 5])
        logits, exps, gates, hits, picks, rest, picks2 = (sb(n, R) for n in
                                                          ("logits", "exps", "gates", "hits", "picks", "rest", "picks2"))
        gate_next = sb("gate_next", R)
        gate = sb("gate", R)
        p_h = ps("p_h", [P, 3, GN])
        p_o = ps("p_o", [P, 2, GT, D])
        p_t = ps("p_t", [P, GN])
        p_x = ps("p_x", [P, GN])
        p_r = ps("p_r", [P, GT, P])

        tail = NormTail(ctx, nc, "ex_tail", GT)
        w1_scaled = nc.alloc_semaphore("ex_w1_scaled")
        stored = nc.alloc_semaphore("ex_stored")
        w1_hi_ready = nc.alloc_semaphore("ex_w1_hi_ready")
        w1_lo_ready = nc.alloc_semaphore("ex_w1_lo_ready")
        squared, mean_done, rooted, scaled = sig("squared"), sig("mean_done"), sig("rooted"), sig("scaled")
        raw_copied = sig("raw_copied")
        turned = sig("turned")
        raw_turned = sig("raw_turned")
        raw_t_ready = sig("raw_t_ready")
        x_hi_ready = sig("x_hi_ready")
        x_lo_ready = sig("x_lo_ready")
        routed = sig("routed")
        shifted = sig("shifted")
        exped = sig("exped")
        STEPS = 20
        step = sig("step", STEPS)
        gate_copied = sig("gate_copied")
        h_done = sig("h_done", EXPERTS * HC)
        silu_done = sig("silu_done", EXPERTS * HC)
        out_done = sig("out_done", EXPERTS)
        acc_done = sig("acc_done", EXPERTS - 1)

        block = ctx.enter_context(nc.Block())

        def group(t):
            return X[:, bass.ds(t * GT, GT), :]

        def w1_low_part(engine, ops, e):
            engine.wait_ge(w1_hi_ready, e + 1)
            ops.tensor_tensor(w1_lo[:, e, :], w1[:, e, :], w1_hi[:, e, :].bitcast(F32), ALU.subtract).then_inc(w1_lo_ready, 1)

        def all_turns(engine, turn):
            with engine.Fori(0, TURNS - 1) as t:
                turn(t, True)
            turn(TURNS - 1, False)

        @block.sync
        def _(sp):
            rows = out.rearrange("(t p) d -> p t d", p=P)
            with sp.Fori(0, TURNS) as t:
                sp.wait_ge(tail.done.sem, tail.done.now(t, 1))
                sp.dma_start(rows[:, bass.ds(t * GT, GT), :], group(t)).then_inc(stored, 16)
            sp.wait_ge(stored, 16 * TURNS)

        @block.gpsimd
        def _(pool):
            credit(pool, rooted, raw_copied)
            tail.credit_pool(pool)

            def front(t, first=False):
                pool.wait_ge(raw_turned.sem, raw_turned.before(t, 1))
                if not first:
                    pool.wait_ge(acc_done.sem, acc_done.before(t, 1))
                pool.wait_ge(scaled.sem, scaled.before(t, 1))
                pool.wait_ge(mean_done.sem, mean_done.now(t, 1))
                nc.gpsimd.tensor_tensor(rnorm[:, :], mean_sq[:, :], W["minus_half"][:, 0:GT], ALU.pow)\
                    .then_inc(rooted.sem, 1)
                nc.gpsimd.tensor_copy(x_raw[:, :, :], group(t)).then_inc(raw_copied.sem, 1)

            def turn(t, one):
                if one:
                    front(t + 1)
                tail.root_pool(pool, t, W["minus_half"])

            front(0, True)
            for e in range(1, EXPERTS, 2):
                w1_low_part(pool, nc.gpsimd, e)
            all_turns(pool, turn)

        @block.tensor
        def _(pe):
            credit(pe, turned, raw_turned, routed, h_done, out_done)

            def transpose_raw(t):
                pe.wait_ge(raw_copied.sem, raw_copied.now(t, 1))
                pe.wait_ge(raw_t_ready.sem, raw_t_ready.before(t, 1))
                for j in range(GT):
                    last = pe.transpose(p_x[:, j * P:(j + 1) * P], x_raw[:, j, :], W["ident"])
                last.then_inc(raw_turned.sem, 1)

            def transpose_scaled(t):
                pe.wait_ge(scaled.sem, scaled.now(t, 1))
                pe.wait_ge(x_lo_ready.sem, x_lo_ready.before(t, 1))
                for j in range(GT):
                    last = pe.transpose(p_t[:, j * P:(j + 1) * P], x_scaled[:, j, :], W["ident"])
                last.then_inc(turned.sem, 1)

            def route(t):
                pe.wait_ge(raw_t_ready.sem, raw_t_ready.now(t, 1))
                pe.wait_ge(shifted.sem, shifted.before(t, 1))
                for j in range(GT):
                    last = pe.matmul(p_r[:, j, 0:ROUTED], x_raw_t[:, j * P:(j + 1) * P], W["router"], start=True, stop=True)
                last.then_inc(routed.sem, 1)

            def up(t, n):
                if n == 0:
                    pe.wait_ge(x_hi_ready.sem, x_hi_ready.now(t, 1))
                    pe.wait_ge(x_lo_ready.sem, x_lo_ready.now(t, 1))
                for c in range(HC):
                    i = HC * n + c
                    pe.wait_ge(silu_done.sem, silu_done.now(t, i - 2) if i >= 3 else silu_done.before(t, EXPERTS * HC + i - 2))
                    w_hi, w_lo = (w[:, ORDER[n], c * P:(c + 1) * P] for w in (w1_hi, w1_lo))
                    pe.matmul(p_h[:, i % 3, :], w_hi, x_hi[:, :], start=True, stop=False)
                    pe.matmul(p_h[:, i % 3, :], w_hi, x_lo[:, :], start=False, stop=False)
                    pe.matmul(p_h[:, i % 3, :], w_lo, x_hi[:, :], start=False, stop=True).then_inc(h_done.sem, 1)

            def down(t, n):
                pe.wait_ge(silu_done.sem, silu_done.now(t, HC * n + HC))
                if n >= 2:
                    pe.wait_ge(acc_done.sem, acc_done.now(t, n - 1))
                elif n == 0:
                    pe.wait_ge(acc_done.sem, acc_done.before(t, EXPERTS - 1))
                else:
                    pe.wait_ge(tail.added.sem, tail.added.before(t, 1))
                for j in range(GT):
                    for c in range(HC):
                        last = pe.matmul(p_o[:, n % 2, j, :], hidden[:, (HC * n + c) % 4, j * P:(j + 1) * P],
                                         w2[:, ORDER[n], c, :], start=(c == 0), stop=(c == HC - 1))
                last.then_inc(out_done.sem, 1)

            def turn(t, one):
                for n in range(EXPERTS + 1):
                    if n < EXPERTS:
                        up(t, n)
                    if n >= 1:
                        down(t, n - 1)
                    if one and n == 6:
                        transpose_raw(t + 1)
                        transpose_scaled(t + 1)
                    if one and n == 7:
                        route(t + 1)

            transpose_raw(0)
            transpose_scaled(0)
            route(0)
            pe.wait_ge(w1_lo_ready, EXPERTS)
            all_turns(pe, turn)

        @block.scalar
        def _(act):
            credit(act, squared, raw_t_ready, x_hi_ready, exped, silu_done)

            def square(t):
                act.wait_ge(mean_done.sem, mean_done.before(t, 1))
                for j in range(GT):
                    last = nc.scalar.activation(squares[:, j, :].unsqueeze(1), X[:, bass.ds(t * GT + j, 1), :], ACT.Square,
                                                accum_out=ssq[:, j:j + 1])
                last.then_inc(squared.sem, 1)

            def raw_copy(t):
                act.wait_ge(raw_turned.sem, raw_turned.now(t, 1))
                act.wait_ge(routed.sem, routed.before(t, 1))
                nc.scalar.activation(x_raw_t[:, :], p_x[:, :], ACT.Copy).then_inc(raw_t_ready.sem, 1)

            def x_copy(t):
                act.wait_ge(turned.sem, turned.now(t, 1))
                act.wait_ge(h_done.sem, h_done.before(t, EXPERTS * HC))
                nc.scalar.activation(x_hi[:, :], p_t[:, :], ACT.Copy).then_inc(x_hi_ready.sem, 1)

            def exp(t):
                act.wait_ge(step.sem, step.before(t, STEPS))
                act.wait_ge(shifted.sem, shifted.now(t, 1))
                nc.scalar.activation(exps[:, :, :], logits[:, :, :], ACT.Exp).then_inc(exped.sem, 1)

            def turn(t, one):
                for i in range(EXPERTS * HC):
                    n = i // HC
                    if n >= 2:
                        act.wait_ge(out_done.sem, out_done.now(t, n - 1))
                    else:
                        act.wait_ge(out_done.sem, out_done.before(t, EXPERTS - 1 + n))
                    act.wait_ge(h_done.sem, h_done.now(t, i + 1))
                    nc.scalar.activation(hidden[:, i % 4, :], p_h[:, i % 3, :], ACT.Silu).then_inc(silu_done.sem, 1)
                    if one and i == 2:
                        square(t + 1)
                    if one and i == 14:
                        raw_copy(t + 1)
                    if one and i == 21:
                        exp(t + 1)
                    if one and i == 30:
                        x_copy(t + 1)

            square(0)
            raw_copy(0)
            x_copy(0)
            for e in range(EXPERTS):
                act.wait_ge(w1_scaled, e + 1)
                nc.scalar.activation(w1_hi[:, e, :], w1[:, e, :], ACT.Copy).then_inc(w1_hi_ready, 1)
            exp(0)
            all_turns(act, turn)

        @block.vector
        def _(dve):
            credit(dve, x_lo_ready, mean_done, scaled, shifted, step, gate_copied, acc_done)
            tail.credit_vector(dve)

            def mean_rows(t):
                dve.wait_ge(squared.sem, squared.now(t, 1))
                dve.wait_ge(rooted.sem, rooted.before(t, 1))
                nc.vector.tensor_scalar(mean_sq[:, :], ssq[:, :], 1.0 / D, RMS_EPS, ALU.mult, ALU.add)\
                    .then_inc(mean_done.sem, 1)

            def scale_rows(t):
                dve.wait_ge(turned.sem, turned.before(t, 1))
                dve.wait_ge(rooted.sem, rooted.now(t, 1))
                for j in range(GT):
                    last = nc.vector.tensor_scalar(x_scaled[:, j, :].unsqueeze(1), X[:, bass.ds(t * GT + j, 1), :],
                                                   rnorm[:, j:j + 1], None, ALU.mult)
                last.then_inc(scaled.sem, 1)

            rank = W["first_rank"].unsqueeze(1).broadcast_to((P, GT, ROUTED))
            tt, reduce = nc.vector.tensor_tensor, nc.vector.tensor_reduce

            def wide(k):
                return top[:, :, k:k + 1].broadcast_to((P, GT, ROUTED))

            def small(t, n, ins):
                ins.then_inc(step.sem, 1)
                dve.wait_ge(step.sem, step.now(t, n))

            def best_of(t, n, values, picked):
                small(t, n, reduce(top[:, :, 2:3], values[:, :, :], AX_X, ALU.max))
                small(t, n + 1, tt(hits[:, :, :], values[:, :, :], wide(2), ALU.is_equal))
                small(t, n + 2, tt(hits[:, :, :], hits[:, :, :], rank, ALU.mult))
                small(t, n + 3, reduce(top[:, :, 3:4], hits[:, :, :], AX_X, ALU.max))
                small(t, n + 4, tt(picked[:, :, :], hits[:, :, :], wide(3), ALU.is_equal))

            def shift_logits(t):
                dve.wait_ge(exped.sem, exped.before(t, 1))
                dve.wait_ge(routed.sem, routed.now(t, 1))
                small(t, 1, reduce(top[:, :, 0:1], p_r[:, :, 0:ROUTED], AX_X, ALU.max, negate=True))
                tt(logits[:, :, :], p_r[:, :, 0:ROUTED], wide(0), ALU.add).then_inc(shifted.sem, 1)

            def softmax(t):
                dve.wait_ge(exped.sem, exped.now(t, 1))
                small(t, 2, reduce(top[:, :, 1:2], exps[:, :, :], AX_X, ALU.add))
                small(t, 3, nc.vector.reciprocal(top[:, :, 1:2], top[:, :, 1:2]))
                small(t, 4, tt(gates[:, :, :], exps[:, :, :], wide(1), ALU.mult))

            def first_best(t):
                best_of(t, 5, gates, picks)

            def second_best(t):
                small(t, 10, nc.vector.scalar_tensor_tensor(out=rest[:, :, :], in0=picks[:, :, :], scalar=-2.0,
                                                            in1=gates[:, :, :], op0=ALU.mult, op1=ALU.add))
                best_of(t, 11, rest, picks2)

            def keep_two(t):
                small(t, 16, tt(picks[:, :, :], picks[:, :, :], picks2[:, :, :], ALU.add))
                small(t, 17, tt(gates[:, :, :], gates[:, :, :], picks[:, :, :], ALU.mult))
                small(t, 18, reduce(top[:, :, 4:5], gates[:, :, :], AX_X, ALU.add))
                small(t, 19, nc.vector.tensor_scalar(top[:, :, 4:5], top[:, :, 4:5], 1e-9, None, ALU.add))
                small(t, 20, nc.vector.reciprocal(top[:, :, 4:5], top[:, :, 4:5]))

            ROUTER = {8: shift_logits, 10: softmax, 11: first_best, 12: second_best, 13: keep_two}

            def gate_ready(t):
                dve.wait_ge(acc_done.sem, acc_done.before(t, EXPERTS - 1))
                nc.vector.tensor_tensor(gate[:, :, :], gates[:, :, :], top[:, :, 4:5].broadcast_to((P, GT, ROUTED)), ALU.mult)\
                    .then_inc(gate_copied.sem, 1)
                dve.wait_ge(gate_copied.sem, gate_copied.now(t, 1))

            def accumulate(t, n):
                dve.wait_ge(out_done.sem, out_done.now(t, n + 1))
                out = p_o[:, n % 2, :, :]
                if n == 0:
                    dve.wait_ge(tail.added.sem, tail.added.before(t, 1))
                    nc.vector.tensor_tensor(acc[:, :, :], out, x_raw[:, :, :], ALU.add).then_inc(acc_done.sem, 1)
                else:
                    dve.wait_ge(acc_done.sem, acc_done.now(t, n))
                    for j in range(GT):
                        last = nc.vector.scalar_tensor_tensor(out=acc[:, j, :], in0=out[:, j, :],
                                                              scalar=gate[:, j, ORDER[n]:ORDER[n] + 1], in1=acc[:, j, :],
                                                              op0=ALU.mult, op1=ALU.add)
                    last.then_inc(acc_done.sem, 1)

            def low_part(t):
                dve.wait_ge(h_done.sem, h_done.before(t, EXPERTS * HC))
                dve.wait_ge(x_hi_ready.sem, x_hi_ready.now(t, 1))
                nc.vector.tensor_tensor(x_lo[:, :], p_t[:, :], x_hi[:, :].bitcast(F32), ALU.subtract)\
                    .then_inc(x_lo_ready.sem, 1)

            def turn(t, one):
                gate_ready(t)
                for n in range(EXPERTS - 1):
                    accumulate(t, n)
                    if one and n == 2:
                        mean_rows(t + 1)
                    if one and n == 4:
                        scale_rows(t + 1)
                    if one and n in ROUTER:
                        ROUTER[n](t + 1)
                    if one and n == EXPERTS - 3:
                        low_part(t + 1)
                dve.wait_ge(acc_done.sem, acc_done.now(t, EXPERTS - 1))
                dve.wait_ge(out_done.sem, out_done.now(t, EXPERTS))
                tail.moments_vector(dve, t, p_o[:, (EXPERTS - 1) % 2, :, :], acc[:, :, :])
                tail.write_vector(dve, t, lambda j: X[:, bass.ds(t * GT + j, 1), :])

            mean_rows(0)
            scale_rows(0)
            dve.wait_ge(landed["experts"], 48)
            for e in range(EXPERTS):
                nc.vector.tensor_scalar(w1[:, e, :], w1[:, e, :], rms_w[:, e:e + 1], None, ALU.mult).then_inc(w1_scaled, 1)
            low_part(0)
            for e in range(0, EXPERTS, 2):
                w1_low_part(dve, nc.vector, e)
            for part in ROUTER.values():
                part(0)
            all_turns(dve, turn)
def weight_layout():
    sizes = [("ident", P), ("pwT", D), ("gruT", 2 * D), ("ff1T", HIDDEN), ("ff2T", HIDDEN),
             ("dw", 3), ("dw_b", 1), ("gains_raw", 3), ("ff_b1", 4), ("pw_b", D), ("ff_b2", D),
             ("WqT", D), ("WkT", D), ("WvT", D), ("WoT", D),
             ("gamma_x", 1), ("gamma_slot", 1), ("slots", SLOTS), ("moe_w1", HIDDEN), ("moe_w2", HIDDEN),
             ("Wqkv", 3 * D), ("qk_b", 2), ("v_b", 1), ("Wout", D), ("out_b", D),
             ("lnx_g", 1), ("lnx_b", 1), ("lnl_g", 1), ("lnl_b", 1), ("q_gamma", 1), ("k_gamma", 1),
             ("XWq", D), ("XWkv", 2 * D), ("XWout", D), ("xout_b", D),
             ("router", ROUTED), ("head_mask", 4), ("window", SEQ), ("first_rank", ROUTED)]
    at, out = 0, {}
    for name, n in sizes:
        out[name] = (at, n)
        at += n
    return out, at


def build(nc, x, ctx_in, mask, weights, rms_w, w1, w2, out):
    layout, columns = weight_layout()
    with ExitStack() as ctx:
        X = ctx.enter_context(nc.sbuf_tensor("X", [P, TILES, D], F32))
        pack = ctx.enter_context(nc.sbuf_tensor("pack", [P, columns], F32))
        gains = ctx.enter_context(nc.sbuf_tensor("gains", [P, 3], F32))
        minus_half = ctx.enter_context(nc.sbuf_tensor("minus_half", [P, 16], F32))
        ew1 = ctx.enter_context(nc.sbuf_tensor("ew1", [P, EXPERTS, EH], F32))
        ew2 = ctx.enter_context(nc.sbuf_tensor("ew2", [P, EXPERTS, EH // P, D], F32))
        erms = ctx.enter_context(nc.sbuf_tensor("erms", [P, EXPERTS], F32))
        landed = {n: ctx.enter_context(nc.semaphore(n + "_landed")) for n in ("x", "weights", "experts")}
        W = {n: pack[:, a:a + k] for n, (a, k) in layout.items()}
        W["ff2T"] = W["ff2T"].rearrange("p (c d) -> p c d", c=4)
        W["moe_w2"] = W["moe_w2"].rearrange("p (c d) -> p c d", c=4)
        W["slots"] = W["slots"].rearrange("p (c d) -> p c d", c=4)
        W["gains"], W["minus_half"] = gains[:, :], minus_half[:, :]
        load(nc, X, pack, layout["WqT"][0], W, x, weights, (rms_w, w1, w2), (erms, ew1, ew2), landed)
        chain = (lambda: stage_conv_gru(nc, X, W, landed), lambda: stage_attention(nc, X, W, 0, ctx_in),
                 lambda: stage_soft_mixture(nc, X, W), lambda: stage_attention(nc, X, W, 1, ctx_in),
                 lambda: stage_cross(nc, X, W, ctx_in, mask), lambda: stage_experts(nc, X, W, erms, ew1, ew2, landed, out))
        for stage in chain:
            with nc.cleanup_on_exit():
                stage()


def load(nc, X, pack, first_columns, W, x, weights, expert_weights, expert_tiles, landed):
    x_tiles = x.rearrange("(t p) d -> p t d", p=P)
    with ExitStack() as ctx:
        w_first = ctx.enter_context(nc.semaphore("w_first"))
        x_first = ctx.enter_context(nc.semaphore("x_first"))
        block = ctx.enter_context(nc.Block())

        @block.sync
        def _(sp):
            sp.dma_start(pack[:, 0:first_columns], weights[:, 0:first_columns]).then_inc(w_first, 16)
            sp.dma_start(pack[:, first_columns:], weights[:, first_columns:]).then_inc(landed["weights"], 16)
            (rms_w, w1, w2), (erms, ew1, ew2) = expert_weights, expert_tiles
            sp.dma_start(erms[:, :], rms_w).then_inc(landed["experts"], 16)
            sp.dma_start(ew1[:, :, :], w1.rearrange("e d h -> d e h")).then_inc(landed["experts"], 16)
            sp.dma_start(ew2[:, :, :, :], w2.rearrange("e (c p) d -> p e c d", p=P)).then_inc(landed["experts"], 16)

        @block.scalar
        def _(act):
            act.dma_start(X[:, 0:FIRST_TILES, :], x_tiles[:, 0:FIRST_TILES, :]).then_inc(x_first, 16)
            act.dma_start(X[:, FIRST_TILES:, :], x_tiles[:, FIRST_TILES:, :]).then_inc(landed["x"], 16)
            act.wait_ge(x_first, 16)

        @block.vector
        def _(dve):
            nc.vector.memset(W["minus_half"], -0.5)
            dve.wait_ge(w_first, 16)
            nc.vector.tensor_scalar(W["gains"], W["gains_raw"], 1.0, float(D) ** 0.5, ALU.add, ALU.mult)


def pack_weights(v):
    def rows(a):
        return np.broadcast_to(np.asarray(a).reshape(1, -1), (P, np.asarray(a).size))

    def chunks(a):
        a = np.asarray(a)
        return a.reshape(4, P, a.shape[1]).transpose(1, 0, 2).reshape(P, -1)

    def col(a):
        return np.asarray(a).reshape(-1, 1)

    f, q = np.arange(P), np.arange(P)[:, None] % SEQ
    k = np.arange(SEQ)[None, :]
    allowed = (q - k >= 0) & (q - k < WINDOW)
    parts = {
        "ident": np.eye(P, dtype=np.float32),
        "pwT": v["L0_attn_conv_pw_w"].T, "gruT": v["L0_attn_gru_w"].T, "ff1T": v["L0_attn_ff_w1"].T,
        "ff2T": chunks(v["L0_attn_ff_w2"].T), "dw": v["L0_attn_conv_dw_w"].reshape(D, 3),
        "dw_b": col(v["L0_attn_conv_dw_b"]),
        "gains_raw": np.stack([v["L0_attn_conv_norm_g"], v["L0_attn_gru_norm_g"], v["L0_attn_ff_norm_g"]], 1),
        "ff_b1": v["L0_attn_ff_b1"].reshape(4, P).T, "pw_b": rows(v["L0_attn_conv_pw_b"]), "ff_b2": rows(v["L0_attn_ff_b2"]),
        "WqT": v["L0_xattn_Wq"].T, "WkT": v["L0_xattn_Wk"].T, "WvT": v["L0_xattn_Wv"].T, "WoT": v["L0_xattn_Wo"].T,
        "gamma_x": col(v["L0_ffn_gamma_x"]), "gamma_slot": col(v["L0_ffn_gamma_slot"]),
        "slots": chunks(v["L0_ffn_slot_embeds"].reshape(SLOTS, D)), "moe_w1": v["L0_ffn_w1"], "moe_w2": chunks(v["L0_ffn_w2"]),
        "Wqkv": v["L1_attn_W_qkv"], "qk_b": v["L1_attn_b_qkv"][:2 * D].reshape(2, D).T, "v_b": col(v["L1_attn_b_qkv"][2 * D:]),
        "Wout": v["L1_attn_W_out"], "out_b": rows(v["L1_attn_b_out"]),
        "lnx_g": col(v["L1_xattn_ln_x_g"]), "lnx_b": col(v["L1_xattn_ln_x_b"]),
        "lnl_g": col(v["L1_xattn_ln_l_g"]), "lnl_b": col(v["L1_xattn_ln_l_b"]),
        "q_gamma": col(np.concatenate([v["L1_xattn_q_gamma"]] * 2)), "k_gamma": col(np.concatenate([v["L1_xattn_k_gamma"]] * 2)),
        "XWq": v["L1_xattn_W_q"], "XWkv": v["L1_xattn_W_kv"], "XWout": v["L1_xattn_W_out"], "xout_b": rows(v["L1_xattn_b_out"]),
        "router": v["L1_ffn_router_w"],
        "head_mask": (f[:, None] % 32 // HD == np.arange(4)[None, :]).astype(np.float32),
        "window": np.where(allowed, np.float32(0), np.float32(-1e30)),
        "first_rank": rows(np.arange(ROUTED, 0, -1).astype(np.float32)),
    }
    layout, columns = weight_layout()
    packed = np.zeros((P, columns), np.float32)
    for name, (a, n) in layout.items():
        packed[:, a:a + n] = parts[name]
    return packed


_OUT = ((BATCH, SEQ, D), "float32")


def kernel(**inputs):
    import concourse.bacc as _bacc
    from concourse.bass_utils import run_bass_kernel_spmd as _run

    v = {n: np.asarray(a) for n, a in inputs.items()}
    arrays = {
        "x": v["x"].reshape(BATCH * SEQ, D), "ctx": v["ctx_1024"].reshape(BATCH * SEQ, D),
        "mask": v["mask_BxS2_bk0"], "weights": pack_weights(v),
        "rms_w": np.ascontiguousarray(np.concatenate([v["L1_ffn_rms_w"], v["L1_ffn_rms_w_s"]]).T),
        "w1": np.concatenate([v["L1_ffn_w1"], v["L1_ffn_w1_s"]]), "w2": np.concatenate([v["L1_ffn_w2"], v["L1_ffn_w2_s"]]),
    }
    arrays = {n: np.ascontiguousarray(a) for n, a in arrays.items()}
    nc = _bacc.Bacc("TRN2", target_bir_lowering=False, num_devices=1)
    aps = [nc.dram_tensor(n, a.shape, mybir.dt.from_np(a.dtype), kind="ExternalInput").ap() for n, a in arrays.items()]
    out = nc.dram_tensor("out", [BATCH * SEQ, D], F32, kind="ExternalOutput").ap()
    build(nc, *aps, out)
    r = _run(nc, [arrays], core_ids=[0])
    return r.results[0]["out"].reshape(_OUT[0])
```
